# Optimizing a Trainium2 kernel written in Bass

```python
import numpy as np
import jax
import jax.numpy as jnp

def _softmax(x, axis=-1):
    return jax.nn.softmax(x, axis=axis)

def _gelu(x):
    return jax.nn.gelu(x, approximate=True)

def _silu(x):
    return jax.nn.silu(x)

def _sigmoid(x):
    return jax.nn.sigmoid(x)

def _layernorm(x, axis=-1, eps=1e-05):
    m = jnp.mean(x, axis=axis, keepdims=True)
    v = jnp.var(x, axis=axis, keepdims=True)
    return (x - m) / jnp.sqrt(v + eps)

def _scatter_add(tgt, idx, src, axis=0):
    return tgt.at[idx].add(src)

def _segment_sum(src, seg, n):
    return jax.ops.segment_sum(src, seg, n)
kernel_name = 'mk_gnn_preln_d4_gnn_r32_866929'

def setup_inputs(seed: int=0):
    np.random.seed(seed)
    _w = jnp.asarray

    def _rec_inputs():
        import jax
        import jax.numpy as jnp
        _gk = jax.random.key(seed)
        x = -0.000202 + 1 * jax.random.normal(jax.random.fold_in(_gk, 1), (3125, 128), jnp.float32)
        src = jax.random.randint(jax.random.fold_in(_gk, 2), (50000,), 0, 3125, jnp.int32)
        dst = jax.random.randint(jax.random.fold_in(_gk, 3), (50000,), 0, 3125, jnp.int32)
        _o = jnp.argsort(dst, stable=True)
        src = src[_o]
        dst = dst[_o]
        edge_type_200 = jax.random.randint(jax.random.fold_in(_gk, 13), (50000,), 0, 200, jnp.int32)
        edge_type_8 = jax.random.randint(jax.random.fold_in(_gk, 14), (50000,), 0, 8, jnp.int32)
        edge_weight = jax.random.uniform(jax.random.fold_in(_gk, 15), (50000,), jnp.float32, 0.0, 0.999999)
        node_type_8 = jax.random.randint(jax.random.fold_in(_gk, 16), (3125,), 0, 8, jnp.int32)
        return (x, src, dst, edge_type_200, edge_type_8, edge_weight, node_type_8)
    x, src, dst, edge_type_200, edge_type_8, edge_weight, node_type_8 = _rec_inputs()

    def _L0_gnn_setup():
        import jax, jax.numpy as jnp
        import numpy as np
        from jax.ops import segment_sum, segment_max
        N_ENT = 50000
        N_REL = 200
        E = 25000
        D = 128
        R = 128
        H = 8
        HD = D // H
        SLOPE = 0.2

        def leaky(x):
            return jnp.where(x >= 0, x, SLOPE * x)
        key = jax.random.key(seed)
        ks = jax.random.split(key, 8)
        h = jax.random.normal(ks[0], (N_ENT, D), dtype=jnp.float32)
        z = jax.random.normal(ks[1], (N_REL, R), dtype=jnp.float32)
        Wc_w = jax.random.normal(ks[2], (D + R, D), dtype=jnp.float32) / np.sqrt(D + R)
        P_w = jax.random.normal(ks[3], (2 * D + R, D), dtype=jnp.float32) / np.sqrt(2 * D + R)
        y_w = jax.random.normal(ks[4], (D, H), dtype=jnp.float32) / np.sqrt(D)
        residual_weight = jnp.ones((1,), dtype=jnp.float32)
        edge_index = jax.random.randint(ks[5], (2, E), 0, N_ENT, dtype=jnp.int32)
        edge_type = jax.random.randint(ks[6], (E,), 0, N_REL, dtype=jnp.int32)
        return {'h': h, 'z': z, 'Wc_w': Wc_w, 'P_w': P_w, 'y_w': y_w, 'residual_weight': residual_weight, 'edge_index': edge_index, 'edge_type': edge_type}
    _L0_gnn_all = _L0_gnn_setup()
    _L0_gnn_in = {k: v for k, v in _L0_gnn_all.items() if k in ('z', 'Wc_w', 'P_w', 'y_w', 'residual_weight')}
    del _L0_gnn_all

    def _L1_gnn_setup():
        import jax, jax.numpy as jnp
        import numpy as np
        N, IN_C, H, C = (50000, 128, 4, 32)
        E = 25000
        NEG_SLOPE = 0.2
        BN_EPS = 1e-05
        key = jax.random.key(seed)
        ks = jax.random.split(key, 8)
        x = jax.random.normal(ks[0], (N, IN_C), dtype=jnp.float32)
        edge_index = jax.random.randint(ks[1], (2, E), 0, N, dtype=jnp.int64)
        W = jax.random.normal(ks[2], (IN_C, H * C), dtype=jnp.float32) * 0.1
        att_src = jax.random.normal(ks[3], (H, C), dtype=jnp.float32) * 0.1
        att_dst = jax.random.normal(ks[4], (H, C), dtype=jnp.float32) * 0.1
        bias = jnp.zeros((H * C,), dtype=jnp.float32)
        gamma = jnp.ones((H * C,), dtype=jnp.float32)
        beta = jnp.zeros((H * C,), dtype=jnp.float32)
        return {'x': x, 'edge_index': edge_index, 'W': W, 'att_src': att_src, 'att_dst': att_dst, 'bias': bias, 'gamma': gamma, 'beta': beta}
    _L1_gnn_all = _L1_gnn_setup()
    _L1_gnn_in = {k: v for k, v in _L1_gnn_all.items() if k in ('W', 'att_src', 'att_dst', 'bias', 'gamma', 'beta')}
    del _L1_gnn_all

    def _L2_gnn_setup():
        import jax, jax.numpy as jnp
        import numpy as np
        N_NODES = 3125
        N_EDGES = 50000
        IN_CH = 128
        HEADS = 4
        OUT_CH = 32
        key = jax.random.key(seed)
        k = jax.random.split(key, 6)
        x = jax.random.normal(k[0], (N_NODES, IN_CH), dtype=jnp.float32)
        edge_index = jax.random.randint(k[1], (2, N_EDGES), 0, N_NODES, dtype=jnp.int64)
        edge_weight = jax.random.uniform(k[2], (N_EDGES,), dtype=jnp.float32)
        W = jax.random.normal(k[3], (HEADS * OUT_CH, IN_CH), dtype=jnp.float32) * (1.0 / np.sqrt(IN_CH))
        a_src = jax.random.normal(k[4], (1, HEADS, OUT_CH), dtype=jnp.float32) * 0.1
        a_dst = jax.random.normal(k[5], (1, HEADS, OUT_CH), dtype=jnp.float32) * 0.1
        return {'x': x, 'edge_index': edge_index, 'edge_weight': edge_weight, 'W': W, 'a_src': a_src, 'a_dst': a_dst}
    _L2_gnn_all = _L2_gnn_setup()
    _L2_gnn_in = {k: v for k, v in _L2_gnn_all.items() if k in ('W', 'a_src', 'a_dst')}
    del _L2_gnn_all

    def _L3_gnn_setup():
        import jax, jax.numpy as jnp
        import numpy as np
        N = 50000
        E = 25000
        DIN = 128
        DH = 128
        H = 8
        DK = DH // H
        TN = 8
        TE = 8
        NB = 4

        def _decomp(x, nt, w_comp, w_basis):
            T = w_comp.shape[0]
            W = (w_comp @ w_basis).reshape(T, x.shape[-1], -1)
            h_all = jnp.einsum('ni,tio->tno', x, W)
            return h_all[nt, jnp.arange(x.shape[0])]
        key = jax.random.key(seed)
        ks = jax.random.split(key, 20)
        inp = {}
        inp['node_feat'] = jax.random.normal(ks[0], (N, DIN), jnp.float32)
        inp['node_type'] = jax.random.randint(ks[1], (N,), 0, TN)
        inp['src'] = jax.random.randint(ks[2], (E,), 0, N)
        inp['dst'] = jax.random.randint(ks[3], (E,), 0, N)
        inp['edge_type'] = jax.random.randint(ks[4], (E,), 0, TE)
        s = 0.05
        for i, nm in enumerate(['k', 'q', 'v', 'a']):
            inp['w_comp_' + nm] = jax.random.normal(ks[5 + 2 * i], (TN, NB), jnp.float32) * s
            inp['w_basis_' + nm] = jax.random.normal(ks[6 + 2 * i], (NB, DIN * DH), jnp.float32) * s
        inp['relation_pri'] = jnp.ones((TE, H), jnp.float32)
        inp['relation_att'] = jax.random.uniform(ks[13], (TE, H, DK, DK), jnp.float32, -0.25, 0.25)
        inp['relation_msg'] = jax.random.uniform(ks[14], (TE, H, DK, DK), jnp.float32, -0.25, 0.25)
        inp['loop_weight'] = jax.random.uniform(ks[15], (DIN, DH), jnp.float32, -0.08, 0.08)
        inp['bias'] = jnp.zeros((DH,), jnp.float32)
        return inp
    _L3_gnn_all = _L3_gnn_setup()
    _L3_gnn_in = {k: v for k, v in _L3_gnn_all.items() if k in ('w_comp_k', 'w_basis_k', 'w_comp_q', 'w_basis_q', 'w_comp_v', 'w_basis_v', 'w_comp_a', 'w_basis_a', 'relation_pri', 'relation_att', 'relation_msg', 'loop_weight', 'bias')}
    del _L3_gnn_all
    return {'x': x, 'src': src, 'dst': dst, 'edge_type_200': edge_type_200, 'edge_type_8': edge_type_8, 'edge_weight': edge_weight, 'node_type_8': node_type_8, 'L0_gnn_z': _L0_gnn_in['z'], 'L0_gnn_Wc_w': _L0_gnn_in['Wc_w'], 'L0_gnn_P_w': _L0_gnn_in['P_w'], 'L0_gnn_y_w': _L0_gnn_in['y_w'], 'L0_gnn_residual_weight': _L0_gnn_in['residual_weight'], 'L1_gnn_W': _L1_gnn_in['W'], 'L1_gnn_att_src': _L1_gnn_in['att_src'], 'L1_gnn_att_dst': _L1_gnn_in['att_dst'], 'L1_gnn_bias': _L1_gnn_in['bias'], 'L1_gnn_gamma': _L1_gnn_in['gamma'], 'L1_gnn_beta': _L1_gnn_in['beta'], 'L2_gnn_W': _L2_gnn_in['W'], 'L2_gnn_a_src': _L2_gnn_in['a_src'], 'L2_gnn_a_dst': _L2_gnn_in['a_dst'], 'L3_gnn_w_comp_k': _L3_gnn_in['w_comp_k'], 'L3_gnn_w_basis_k': _L3_gnn_in['w_basis_k'], 'L3_gnn_w_comp_q': _L3_gnn_in['w_comp_q'], 'L3_gnn_w_basis_q': _L3_gnn_in['w_basis_q'], 'L3_gnn_w_comp_v': _L3_gnn_in['w_comp_v'], 'L3_gnn_w_basis_v': _L3_gnn_in['w_basis_v'], 'L3_gnn_w_comp_a': _L3_gnn_in['w_comp_a'], 'L3_gnn_w_basis_a': _L3_gnn_in['w_basis_a'], 'L3_gnn_relation_pri': _L3_gnn_in['relation_pri'], 'L3_gnn_relation_att': _L3_gnn_in['relation_att'], 'L3_gnn_relation_msg': _L3_gnn_in['relation_msg'], 'L3_gnn_loop_weight': _L3_gnn_in['loop_weight'], 'L3_gnn_bias': _L3_gnn_in['bias']}

def reference(x, src, dst, edge_type_200, edge_type_8, edge_weight, node_type_8, L0_gnn_z, L0_gnn_Wc_w, L0_gnn_P_w, L0_gnn_y_w, L0_gnn_residual_weight, L1_gnn_W, L1_gnn_att_src, L1_gnn_att_dst, L1_gnn_bias, L1_gnn_gamma, L1_gnn_beta, L2_gnn_W, L2_gnn_a_src, L2_gnn_a_dst, L3_gnn_w_comp_k, L3_gnn_w_basis_k, L3_gnn_w_comp_q, L3_gnn_w_basis_q, L3_gnn_w_comp_v, L3_gnn_w_basis_v, L3_gnn_w_comp_a, L3_gnn_w_basis_a, L3_gnn_relation_pri, L3_gnn_relation_att, L3_gnn_relation_msg, L3_gnn_loop_weight, L3_gnn_bias):
    import jax
    import jax.numpy as jnp

    def _L0_gnn_ref(h, z, Wc_w, P_w, y_w, residual_weight, edge_index, edge_type):
        import jax, jax.numpy as jnp
        import numpy as np
        from jax.ops import segment_sum, segment_max
        N_ENT = 50000
        N_REL = 200
        E = 25000
        D = 128
        R = 128
        H = 8
        HD = D // H
        SLOPE = 0.2

        def leaky(x):
            return jnp.where(x >= 0, x, SLOPE * x)
        src, dst = (edge_index[0], edge_index[1])
        n = h.shape[0]
        deg = segment_sum(jnp.ones_like(dst, dtype=h.dtype), dst, num_segments=n)
        z_edge = z[edge_type]
        z_bar = segment_sum(z_edge, dst, num_segments=n) / jnp.maximum(deg, 1.0)[:, None]
        P1, P2, P3 = (P_w[:D], P_w[D:2 * D], P_w[2 * D:])
        hP1 = h @ P1
        hP2 = h @ P2
        zP3 = z @ P3
        pre_edge = hP1[dst] + hP2[src] + zP3[edge_type]
        attn_e = leaky(pre_edge) @ y_w
        pre_self = hP1 + hP2 + z_bar @ P3
        attn_s = leaky(pre_self) @ y_w
        m_e = segment_max(attn_e, dst, num_segments=n)
        m = jnp.maximum(attn_s, m_e)
        e_e = jnp.exp(attn_e - m[dst])
        e_s = jnp.exp(attn_s - m)
        denom = segment_sum(e_e, dst, num_segments=n) + e_s
        w_e = e_e / denom[dst]
        w_s = e_s / denom
        Wc_h, Wc_z = (Wc_w[:D], Wc_w[D:])
        hWc = h @ Wc_h
        zWc = z @ Wc_z
        t_e = hWc[src] + zWc[edge_type]
        t_s = hWc + z_bar @ Wc_z
        agg_e = segment_sum(w_e[:, :, None] * t_e.reshape(-1, H, HD), dst, num_segments=n)
        agg = agg_e + w_s[:, :, None] * t_s.reshape(-1, H, HD)
        h_new = leaky(agg.reshape(-1, D) + residual_weight * h)
        return jnp.where(deg[:, None] > 0, h_new, h)

    def _L1_gnn_ref(x, edge_index, W, att_src, att_dst, bias, gamma, beta):
        import jax, jax.numpy as jnp
        import numpy as np
        N, IN_C, H, C = (50000, 128, 4, 32)
        E = 25000
        NEG_SLOPE = 0.2
        BN_EPS = 1e-05
        n = x.shape[0]
        loops = jnp.arange(n, dtype=edge_index.dtype)
        src = jnp.concatenate([edge_index[0], loops])
        dst = jnp.concatenate([edge_index[1], loops])
        h = (x @ W).reshape(n, H, C)
        a_src = jnp.einsum('nhc,hc->nh', h, att_src)
        a_dst = jnp.einsum('nhc,hc->nh', h, att_dst)
        e = jax.nn.leaky_relu(a_src[src] + a_dst[dst], NEG_SLOPE)
        m = jax.ops.segment_max(e, dst, num_segments=n)
        ex = jnp.exp(e - m[dst])
        denom = jax.ops.segment_sum(ex, dst, num_segments=n)
        alpha = ex / (denom[dst] + 1e-16)
        msg = alpha[:, :, None] * h[src]
        out = jax.ops.segment_sum(msg, dst, num_segments=n)
        out = out.reshape(n, H * C) + bias
        mean = out.mean(axis=0)
        var = out.var(axis=0)
        out = (out - mean) / jnp.sqrt(var + BN_EPS) * gamma + beta
        return jax.nn.elu(out)

    def _L2_gnn_ref(x, edge_index, edge_weight, W, a_src, a_dst):
        import jax, jax.numpy as jnp
        import numpy as np
        N_NODES = 3125
        N_EDGES = 50000
        IN_CH = 128
        HEADS = 4
        OUT_CH = 32
        N = x.shape[0]
        H, C = (a_src.shape[1], a_src.shape[2])
        h = (x @ W.T).reshape(N, H, C)
        src, dst = (edge_index[0], edge_index[1])
        s_src = jnp.sum(h * a_src, axis=-1)
        s_dst = jnp.sum(h * a_dst, axis=-1)
        alpha = jax.nn.leaky_relu(s_src[src] + s_dst[dst], negative_slope=0.2)
        alpha = alpha * edge_weight[:, None]
        amax = jnp.zeros((N, H), dtype=alpha.dtype).at[dst].max(alpha)
        alpha = jnp.exp(alpha - amax[dst])
        asum = jnp.zeros((N, H), dtype=alpha.dtype).at[dst].add(alpha)
        alpha = alpha / (asum[dst] + 1e-08)
        out = jnp.zeros((N, H, C), dtype=h.dtype).at[dst].add(h[src] * alpha[:, :, None])
        return out.reshape(N, H * C)

    def _L3_gnn_ref(node_feat, node_type, src, dst, edge_type, w_comp_k, w_basis_k, w_comp_q, w_basis_q, w_comp_v, w_basis_v, w_comp_a, w_basis_a, relation_pri, relation_att, relation_msg, loop_weight, bias):
        import jax, jax.numpy as jnp
        import numpy as np
        N = 50000
        E = 25000
        DIN = 128
        DH = 128
        H = 8
        DK = DH // H
        TN = 8
        TE = 8
        NB = 4

        def _decomp(x, nt, w_comp, w_basis):
            T = w_comp.shape[0]
            W = (w_comp @ w_basis).reshape(T, x.shape[-1], -1)
            h_all = jnp.einsum('ni,tio->tno', x, W)
            return h_all[nt, jnp.arange(x.shape[0])]
        n = node_feat.shape[0]
        scale = (DH / H) ** (-0.5)
        k = _decomp(node_feat, node_type, w_comp_k, w_basis_k).reshape(n, H, DK)
        q = _decomp(node_feat, node_type, w_comp_q, w_basis_q).reshape(n, H, DK)
        v = _decomp(node_feat, node_type, w_comp_v, w_basis_v).reshape(n, H, DK)
        kt = jnp.einsum('nhi,thij->tnhj', k, relation_att)[edge_type, src]
        e = (q[dst] * kt).sum(-1) * relation_pri[edge_type] * scale
        m = jax.ops.segment_max(e, dst, num_segments=n)
        ex = jnp.exp(e - m[dst])
        denom = jax.ops.segment_sum(ex, dst, num_segments=n)
        a = ex / denom[dst]
        vt = jnp.einsum('nhi,thij->tnhj', v, relation_msg)[edge_type, src]
        agg = jax.ops.segment_sum(a[..., None] * vt, dst, num_segments=n)
        agg = agg.reshape(n, DH)
        out = _decomp(agg, node_type, w_comp_a, w_basis_a)
        out = out + node_feat @ loop_weight + bias
        return jax.nn.relu(out)
    edge_index = jnp.stack([src, dst])
    h = jnp.maximum(_layernorm(x, axis=-1), 0.0)
    x = x + _L0_gnn_ref(h, L0_gnn_z, L0_gnn_Wc_w, L0_gnn_P_w, L0_gnn_y_w, L0_gnn_residual_weight, edge_index, edge_type_200)
    h = jnp.maximum(_layernorm(x, axis=-1), 0.0)
    x = x + _L1_gnn_ref(h, edge_index, L1_gnn_W, L1_gnn_att_src, L1_gnn_att_dst, L1_gnn_bias, L1_gnn_gamma, L1_gnn_beta)
    h = jnp.maximum(_layernorm(x, axis=-1), 0.0)
    x = x + _L2_gnn_ref(h, edge_index, edge_weight, L2_gnn_W, L2_gnn_a_src, L2_gnn_a_dst)
    h = jnp.maximum(_layernorm(x, axis=-1), 0.0)
    x = x + _L3_gnn_ref(h, node_type_8, src, dst, edge_type_8, L3_gnn_w_comp_k, L3_gnn_w_basis_k, L3_gnn_w_comp_q, L3_gnn_w_basis_q, L3_gnn_w_comp_v, L3_gnn_w_basis_v, L3_gnn_w_comp_a, L3_gnn_w_basis_a, L3_gnn_relation_pri, L3_gnn_relation_att, L3_gnn_relation_msg, L3_gnn_loop_weight, L3_gnn_bias)
    return x

_drawn_inputs = setup_inputs


def setup_inputs(seed=0):
    import zlib

    import numpy as np

    out = dict(_drawn_inputs(seed))
    spreads = {'L1_gnn_bias': (0.0, 2.0),
     'L1_gnn_gamma': (1.0, 0.2),
     'L1_gnn_beta': (0.0, 0.1),
     'L3_gnn_relation_pri': (1.0, 0.6),
     'L3_gnn_bias': (0.0, 2.0)}
    factors = {'edge_weight': 3.945,
     'L2_gnn_a_src': 3.329,
     'L2_gnn_a_dst': 5.095,
     'L3_gnn_w_comp_k': 8.0,
     'L3_gnn_w_basis_k': 8.0,
     'L3_gnn_w_comp_q': 8.0,
     'L3_gnn_w_basis_q': 8.0,
     'L3_gnn_w_comp_v': 8.0,
     'L3_gnn_w_basis_v': 8.0,
     'L3_gnn_w_comp_a': 8.0,
     'L3_gnn_w_basis_a': 8.0,
     'L3_gnn_relation_att': 8.0,
     'L3_gnn_relation_msg': 8.0,
     'L3_gnn_loop_weight': 7.089}
    for name, (base, spread) in spreads.items():
        noise = np.random.default_rng([zlib.crc32(name.encode()), seed]).standard_normal(out[name].shape)
        drawn = base * np.exp(spread * noise) if base else spread * noise
        out[name] = jnp.asarray(drawn.astype(out[name].dtype))
    for name, factor in factors.items():
        out[name] = (out[name] * factor).astype(out[name].dtype)
    return out
```

```python
import numpy as np
import concourse.bass as bass
import concourse.mybir as mybir
from contextlib import ExitStack, contextmanager

F32 = mybir.dt.float32
BF16 = mybir.dt.bfloat16
I32 = mybir.dt.int32
ALU = mybir.AluOpType
ACT = mybir.ActivationFunctionType
AX = mybir.AxisListType

P = 128
N_NODES = 3125
N_EDGES = 50000
D = 128
WINDOWS = -(-N_NODES // P)
LAST_NODES = N_NODES - (WINDOWS - 1) * P
N_PAD = WINDOWS * P
EDGE_TILES = -(-N_EDGES // P)
STEPS = EDGE_TILES + WINDOWS - 1
U = 5
TRIPS = STEPS // U
HALVES = ((0, 3), (3, U))
CH = 83
NCH = STEPS // CH
assert TRIPS * U == STEPS and NCH * CH == STEPS
IC = 4
IP = 98
FULL_TILES = N_EDGES // P
TAIL = N_EDGES - FULL_TILES * P
LAST_ROWS = FULL_TILES - (IC - 1) * IP
SENTINEL = 4000
BIG = 1e30
RELS = 200
TYPES = 8
BASES = 4
GROUP = 512
GROUPS = [(n, min(GROUP, N_PAD - n)) for n in range(0, N_PAD, GROUP)]
SLOPE = 0.2
Z_ROW = 2 * D + 1
GAT_ROW = D + 4
H8, H4 = 8, 4


class State:

    def __init__(self):
        self.serial = 0
        self.semaphores = []
        self.layer = ""


def unique(c, name):
    c.serial += 1
    return f"{name}_{c.serial}"


@contextmanager
def semaphore(nc, c, name):
    handle = nc.alloc_semaphore(unique(c, name))
    c.semaphores.append(handle)
    yield handle


def clear_semaphores(nc, c):
    nc.all_engine_barrier()
    nc.clear_and_free_semaphores(c.semaphores)
    nc.all_engine_barrier()
    c.semaphores = []


class Chain:

    def __init__(self, engine, sem):
        self.engine, self.sem, self.n = engine, sem, 0

    def __call__(self, instruction):
        self.n += 1
        instruction.then_inc(self.sem, 1)
        self.engine.wait_ge(self.sem, self.n)


def half_of(u):
    return 0 if u < HALVES[0][1] else 1


def region(c, first_bank, u):
    k = half_of(u)
    at = (u - HALVES[k][0]) * P
    return c.banks[first_bank + k][:, at:at + P]


def half_bank(c, first_bank, k):
    n = HALVES[k][1] - HALVES[k][0]
    return c.banks[first_bank + k][:, 0:n * P].rearrange("p (u e) -> p u e", e=P)



def load_constants(nc, c, a):
    with semaphore(nc, c, "const_done") as const_done, semaphore(nc, c, "x_loaded") as x_loaded, \
            semaphore(nc, c, "vec_done") as vec_done, nc.sbuf_tensor(unique(c, "iota_i"), [P, 512], I32) as iota_i, \
            nc.Block() as block:

        @block.gpsimd
        def _(pool):
            nc.gpsimd.memset(c.ident[:], 0.0).then_inc(const_done, 1)
            pool.wait_ge(const_done, 1)
            nc.gpsimd.affine_select(out=c.ident[:], in_=c.ident[:], compare_op=ALU.not_equal, fill=1.0, base=0,
                                    pattern=[[-1, P]], channel_multiplier=1).then_inc(const_done, 1)
            nc.gpsimd.iota(iota_i[:], pattern=[[1, 512]], base=0, channel_multiplier=0).then_inc(const_done, 1)

        @block.vector
        def _(dve):
            chain = Chain(dve, vec_done)
            chain(nc.vector.memset(c.x[:], 0.0))
            chain(nc.vector.memset(c.ones[:], 1.0))
            dve.wait_ge(const_done, 3)
            chain(nc.vector.tensor_copy(c.iota[:], iota_i[:]))

        @block.sync
        def _(sp):
            sp.wait_ge(vec_done, 1)
            whole = (WINDOWS - 1) * P
            sp.dma_start(c.x[:, 0:WINDOWS - 1, :], a["x"][0:whole, :].rearrange("(w n) d -> n w d", n=P)).then_inc(x_loaded, 16)
            sp.dma_start(c.x[0:LAST_NODES, WINDOWS - 1, :], a["x"][whole:N_NODES, :]).then_inc(x_loaded, 16)
            sp.wait_ge(x_loaded, 32)


def build_steps(nc, c, a):
    with ExitStack() as st:
        def sb(name, shape, dt=F32):
            return st.enter_context(nc.sbuf_tensor(unique(c, name), shape, dt))

        nat_i = sb("nat_i", [IP, 5, IC, P], I32)
        nat = sb("nat", [IP, 6, IC, P])
        tile_i = sb("tile_i", [IP, IC], I32)
        tile_no = sb("tile_no", [IP, IC])
        tile_row = sb("tile_row", [IP, IC, P])
        win_i = sb("win_i", [IP, 2, IC], I32)
        key = sb("key", [IP, 2, IC])
        after = sb("after", [IP, STEPS])
        pick = sb("pick", [IP, IC, STEPS])
        ends = sb("ends", [IP, 2, IC, H8])
        tmp = sb("tmp", [P, STEPS])
        window = sb("window", [P, STEPS])
        dst_t = sb("dst_t", [CH, NCH, P])
        fl = sb("fl", [H8, 2, STEPS])
        single = sb("single", [H8, STEPS])
        loaded = st.enter_context(semaphore(nc, c, "edges_loaded"))
        cleared = st.enter_context(semaphore(nc, c, "nat_cleared"))
        tiles_numbered = st.enter_context(semaphore(nc, c, "tiles_numbered"))
        vec_done = st.enter_context(semaphore(nc, c, "vec_done"))
        picked = st.enter_context(semaphore(nc, c, "picked"))
        by_step = st.enter_context(semaphore(nc, c, "by_step"))
        taken = st.enter_context(semaphore(nc, c, "by_step_taken"))
        by_chunk = st.enter_context(semaphore(nc, c, "by_chunk"))
        block = st.enter_context(nc.Block())
        sources = [(a["dst"], 0), (a["dst"], 1), (a["src"], 0), (a["edge_type_200"], 0), (a["edge_type_8"], 0)]

        @block.sync
        def _(sp):
            sp.wait_ge(cleared, 6)
            n = 0
            for k in range(6):
                source, off = (a["edge_weight"], 0) if k == 5 else sources[k]
                to = nat[:, 5] if k == 5 else nat_i[:, k]
                rows = (IC - 1) * IP
                sp.dma_start(to[:, 0:IC - 1, :],
                             source[off:off + rows * P].rearrange("(c p e) -> p c e", p=IP, e=P)).then_inc(loaded, 16)
                sp.dma_start(to[0:LAST_ROWS, IC - 1, :],
                             source[off + rows * P:off + FULL_TILES * P].rearrange("(p e) -> p e", e=P)).then_inc(loaded, 16)
                sp.dma_start(to[LAST_ROWS:LAST_ROWS + 1, IC - 1, 0:TAIL - off],
                             source[off + FULL_TILES * P:N_EDGES].rearrange("(p e) -> p e", p=1)).then_inc(loaded, 16)
                n += 3
            sp.wait_ge(loaded, 16 * n)

        @block.gpsimd
        def _(pool):
            nc.gpsimd.iota(tile_i[:], pattern=[[IP, IC]], base=0, channel_multiplier=1).then_inc(tiles_numbered, 1)

        @block.vector
        def _(dve):
            for k in range(5):
                nc.vector.memset(nat_i[:, k], SENTINEL if k < 2 else 0).then_inc(cleared, 1)
            nc.vector.memset(nat[:, 5], 0.0).then_inc(cleared, 1)
            chain = Chain(dve, vec_done)
            dve.wait_ge(tiles_numbered, 1)
            chain(nc.vector.tensor_copy(tile_no[:], tile_i[:]))
            chain(nc.vector.tensor_copy(tile_row[:], tile_no[:].unsqueeze(2).to_broadcast([IP, IC, P])))
            dve.wait_ge(loaded, 16 * 18)
            chain(nc.vector.tensor_copy(nat[:, 0:5], nat_i[:]))
            nc.vector.tensor_single_scalar(win_i[:, 0], nat_i[:, 0, :, 0], 7, ALU.arith_shift_right)
            chain(nc.vector.tensor_single_scalar(win_i[:, 1], nat_i[:, 1, :, P - 1], 7, ALU.arith_shift_right))
            chain(nc.vector.tensor_copy(key[:], win_i[:]))
            chain(nc.vector.tensor_tensor(key[:, 0], key[:, 0], tile_no[:], ALU.add))
            chain(nc.vector.scalar_tensor_tensor(key[:, 1], key[:, 1], 1.0, tile_no[:], ALU.add, ALU.add))
            chain(nc.vector.memset(key[0:1, 0, 0:1], 0.0))
            for k in range(IC):
                chain(nc.vector.tensor_scalar(after[:], c.iota[0:IP, 0:STEPS], key[:, 1, k:k + 1], None, ALU.is_ge))
                chain(nc.vector.scalar_tensor_tensor(pick[:, k, :], c.iota[0:IP, 0:STEPS], key[:, 0, k:k + 1], after[:],
                                                     ALU.is_ge, ALU.subtract))
            chain(nc.vector.tensor_copy(ends[:, 0], nat[:, 0, :, 0:1].to_broadcast([IP, IC, H8])))
            chain(nc.vector.tensor_copy(ends[:, 1], nat[:, 0, :, P - 1:P].to_broadcast([IP, IC, H8])))
            nc.vector.tensor_tensor(nat[:, 1], nat[:, 0], nat[:, 1], ALU.not_equal).then_inc(picked, 1)
            dve.wait_ge(by_step, 7)
            chain(nc.vector.tensor_tensor(window[:], c.iota[:, 0:STEPS], c.banks[6][:, 0:STEPS], ALU.subtract))
            chain(nc.vector.tensor_copy(c.window_i[:], window[0:1, :]))
            chain(nc.vector.scalar_tensor_tensor(c.dst_local[:], window[:], -float(P), c.banks[0][:, 0:STEPS],
                                                 ALU.mult, ALU.add))
            chain(nc.vector.tensor_single_scalar(tmp[:], c.dst_local[:], 0.0, ALU.is_ge))
            chain(nc.vector.scalar_tensor_tensor(tmp[:], c.dst_local[:], float(P), tmp[:], ALU.is_lt, ALU.mult))
            chain(nc.vector.tensor_scalar(c.outside[:], tmp[:], 1.0, BIG, ALU.subtract, ALU.mult))
            chain(nc.vector.tensor_copy(c.is_end[:], c.banks[1][:, 0:STEPS]))
            chain(nc.vector.tensor_copy(tmp[:], c.banks[2][:, 0:STEPS]))
            chain(nc.vector.tensor_copy(c.idx_src[:, 0:STEPS], tmp[:]))
            chain(nc.vector.scalar_tensor_tensor(tmp[:], tmp[:], float(TYPES), c.banks[4][:, 0:STEPS],
                                                 ALU.mult, ALU.add))
            chain(nc.vector.tensor_copy(c.idx_typed[:, 0:STEPS], tmp[:]))
            chain(nc.vector.tensor_copy(c.idx_rel[:, 0:STEPS], c.banks[3][:, 0:STEPS]))
            chain(nc.vector.tensor_copy(c.weight[:], c.banks[5][:, 0:STEPS]))
            for t in (c.idx_src, c.idx_typed, c.idx_rel):
                chain(nc.vector.memset(t[:, STEPS:STEPS + U], 0))
            dve.sem_inc(taken, 1)
            dve.wait_ge(by_chunk, 2)
            for k in range(NCH):
                chain(nc.vector.tensor_copy(dst_t[:, k], c.banks[k // 4][0:CH, (k % 4) * P:(k % 4 + 1) * P]))
            chain(nc.vector.memset(c.border[:], -BIG))
            chain(nc.vector.tensor_tensor(c.border[:, :, 1:P], dst_t[:, :, 1:P], dst_t[:, :, 0:P - 1], ALU.not_equal))
            chain(nc.vector.tensor_single_scalar(c.border[:, :, 1:P], c.border[:, :, 1:P], -BIG, ALU.mult))
            for k in range(NCH):
                chain(nc.vector.tensor_scalar(c.not_first[:, k], dst_t[:, k], dst_t[:, k, 0:1], -BIG,
                                              ALU.not_equal, ALU.mult))
                chain(nc.vector.tensor_scalar(c.not_last[:, k], dst_t[:, k], dst_t[:, k, P - 1:P], -BIG,
                                              ALU.not_equal, ALU.mult))
            for k in range(2):
                chain(nc.vector.tensor_copy(fl[:, k], c.banks[2 + k][0:H8, 0:STEPS]))
            chain(nc.vector.memset(c.new_dst[:], -BIG))
            chain(nc.vector.tensor_tensor(c.new_dst[:, 1:STEPS], fl[:, 0, 1:STEPS], fl[:, 1, 0:STEPS - 1], ALU.not_equal))
            chain(nc.vector.tensor_single_scalar(c.new_dst[:, 1:STEPS], c.new_dst[:, 1:STEPS], -BIG, ALU.mult))
            chain(nc.vector.tensor_tensor(single[:], fl[:, 0], fl[:, 1], ALU.not_equal))
            chain(nc.vector.scalar_tensor_tensor(c.stop_forward[:], single[:], -BIG, c.new_dst[:, 0:STEPS], ALU.mult, ALU.add))
            chain(nc.vector.scalar_tensor_tensor(c.stop_backward[:], single[:], -BIG, c.new_dst[:, 1:STEPS + 1], ALU.mult, ALU.add))

        @block.tensor
        def _(pe):
            pe.wait_ge(picked, 1)
            for k in range(7):
                for i in range(IC):
                    lhs = tile_row[:, i, :] if k == 6 else nat[:, k, i, :]
                    last = nc.tensor.matmul(c.banks[k][:, 0:STEPS], lhs, pick[:, i, :], start=i == 0, stop=i == IC - 1)
                last.then_inc(by_step, 1)
            pe.wait_ge(taken, 1)
            for k in range(NCH):
                for i in range(IC):
                    last = nc.tensor.matmul(c.banks[k // 4][0:CH, (k % 4) * P:(k % 4 + 1) * P],
                                            pick[:, i, k * CH:(k + 1) * CH], nat[:, 0, i, :],
                                            start=i == 0, stop=i == IC - 1)
            last.then_inc(by_chunk, 1)
            for k in range(2):
                for i in range(IC):
                    last = nc.tensor.matmul(c.banks[2 + k][0:H8, 0:STEPS], ends[:, k, i, :], pick[:, i, :],
                                            start=i == 0, stop=i == IC - 1)
            last.then_inc(by_chunk, 1)



def layernorm(nc, c, chain):
    wide = [P, WINDOWS, D]
    chain(nc.vector.tensor_reduce(c.mean[:], c.x[:], AX.X, ALU.add))
    chain(nc.vector.tensor_single_scalar(c.mean[:], c.mean[:], 1.0 / D, ALU.mult))
    chain(nc.vector.tensor_tensor(c.h[:], c.x[:], c.mean[:].unsqueeze(2).to_broadcast(wide), ALU.subtract))
    chain(nc.vector.tensor_tensor(c.wide_a[:], c.h[:], c.h[:], ALU.mult))
    chain(nc.vector.tensor_reduce(c.rstd[:], c.wide_a[:], AX.X, ALU.add))
    nc.vector.tensor_scalar(c.rstd[:], c.rstd[:], 1.0 / D, 1e-5, ALU.mult, ALU.add).then_inc(c.stats_ready, 1)
    chain.engine.wait_ge(c.root_ready, 1)
    chain(nc.vector.reciprocal(c.rstd[:], c.rstd[:]))
    chain(nc.vector.tensor_tensor(c.h[:], c.h[:], c.rstd[:].unsqueeze(2).to_broadcast(wide), ALU.mult))
    chain(nc.vector.tensor_single_scalar(c.h[:], c.h[:], 0.0, ALU.max))


def normalise(nc, c):
    with semaphore(nc, c, "stats_ready") as c.stats_ready, semaphore(nc, c, "root_ready") as c.root_ready, \
            semaphore(nc, c, "vec_done") as vec_done, nc.Block() as block:

        @block.vector
        def _(dve):
            layernorm(nc, c, Chain(dve, vec_done))

        @block.scalar
        def _(act):
            act.wait_ge(c.stats_ready, 1)
            nc.scalar.activation(c.rstd[:], c.rstd[:], ACT.Sqrt).then_inc(c.root_ready, 1)


def transpose_windows(nc, c, source, to):
    groups = -(-WINDOWS // 4)
    with semaphore(nc, c, "group_ready") as group_ready, semaphore(nc, c, "group_taken") as group_taken, nc.Block() as block:

        @block.tensor
        def _(pe):
            for g in range(groups):
                if g >= 4:
                    pe.wait_ge(group_taken, g - 3)
                for w in range(4 * g, min(4 * g + 4, WINDOWS)):
                    last = nc.tensor.transpose(c.banks[g % 4][:, (w % 4) * P:(w % 4 + 1) * P], source[:, w, :], c.ident[:])
                last.then_inc(group_ready, 1)

        @block.scalar
        def _(act):
            for g in range(groups):
                n = (min(4 * g + 4, WINDOWS) - 4 * g) * P
                act.wait_ge(group_ready, g + 1)
                nc.scalar.copy(to[:, 4 * g * P:4 * g * P + n], c.banks[g % 4][:, 0:n]).then_inc(group_taken, 1)


def project(nc, c, weights, width, to):
    with semaphore(nc, c, "window_ready") as window_ready, semaphore(nc, c, "window_taken") as window_taken, nc.Block() as block:

        @block.tensor
        def _(pe):
            for w in range(WINDOWS):
                if w >= 4:
                    pe.wait_ge(window_taken, w - 3)
                nc.tensor.matmul(c.banks[w % 4][:, 0:width], c.h_t[:, w * P:(w + 1) * P], weights,
                                 start=True, stop=True).then_inc(window_ready, 1)

        @block.scalar
        def _(act):
            for w in range(WINDOWS):
                act.wait_ge(window_ready, w + 1)
                nc.scalar.copy(to[:, w, 0:width], c.banks[w % 4][:, 0:width]).then_inc(window_taken, 1)


def split_three(nc, chain, value, parts, rest):
    chain(nc.vector.tensor_copy(parts[0], value))
    chain(nc.vector.tensor_tensor(rest, value, parts[0], ALU.subtract))
    chain(nc.vector.tensor_copy(parts[1], rest))
    chain(nc.vector.tensor_tensor(rest, rest, parts[1], ALU.subtract))
    chain(nc.vector.tensor_copy(parts[2], rest))



def edge_softmax(nc, c, heads):
    hd = heads
    with ExitStack() as st:
        seg_max = st.enter_context(nc.sbuf_tensor(unique(c, "seg_max"), [CH, NCH, hd, P], F32))
        run = st.enter_context(nc.sbuf_tensor(unique(c, "run"), [CH, hd, P], F32))
        edge_vals = st.enter_context(nc.sbuf_tensor(unique(c, "edge_vals"), [CH, 2, NCH, hd], F32))
        chains = st.enter_context(nc.sbuf_tensor(unique(c, "chains"), [H8, 2, STEPS], F32))
        carry = st.enter_context(nc.sbuf_tensor(unique(c, "carry"), [H8, 2, STEPS], F32))
        carry_t = st.enter_context(nc.sbuf_tensor(unique(c, "carry_t"), [CH, NCH, 2, hd], F32))
        masked = st.enter_context(semaphore(nc, c, "logits_masked"))
        vec_done = st.enter_context(semaphore(nc, c, "vec_done"))
        turned = st.enter_context(semaphore(nc, c, "logits_turned"))
        scanned = st.enter_context(semaphore(nc, c, "chunk_scanned"))
        edges_out = st.enter_context(semaphore(nc, c, "edge_vals_ready"))
        edges_turned = st.enter_context(semaphore(nc, c, "edge_vals_turned"))
        carries = st.enter_context(semaphore(nc, c, "carries_ready"))
        carries_turned = st.enter_context(semaphore(nc, c, "carries_turned"))
        maxima = st.enter_context(semaphore(nc, c, "maxima_ready"))
        back = st.enter_context(semaphore(nc, c, "maxima_back"))
        args = st.enter_context(semaphore(nc, c, "exp_args_ready"))
        block = st.enter_context(nc.Block())

        def turned_logits(k, h):
            n = (k % 2) * 2 * 4 + h
            return c.banks[n // 4][0:CH, (n % 4) * P:(n % 4 + 1) * P]

        @block.tensor
        def _(pe):
            pe.wait_ge(masked, 1)
            for k in range(NCH):
                if k >= 2:
                    pe.wait_ge(scanned, k - 1)
                for h in range(hd):
                    last = nc.tensor.transpose(turned_logits(k, h), c.logits[:, h, k * CH:(k + 1) * CH], c.ident[:])
                last.then_inc(turned, 1)
            pe.wait_ge(edges_out, 1)
            for b in range(2):
                for k in range(NCH):
                    last = nc.tensor.transpose(c.banks[4 + b][0:hd, k * CH:(k + 1) * CH], edge_vals[:, b, k, :],
                                               c.ident[0:CH, 0:CH])
            last.then_inc(edges_turned, 1)
            pe.wait_ge(carries, 1)
            for k in range(NCH):
                for b in range(2):
                    n = (k * 2 + b) * hd
                    last = nc.tensor.transpose(c.banks[6][0:CH, n:n + hd], carry[0:hd, b, k * CH:(k + 1) * CH],
                                               c.ident[0:hd, 0:hd])
            last.then_inc(carries_turned, 1)
            pe.wait_ge(maxima, 1)
            for h in range(hd):
                for k in range(NCH):
                    last = nc.tensor.transpose(c.banks[h][:, k * CH:(k + 1) * CH], seg_max[:, k, h, :],
                                               c.ident[0:CH, 0:CH])
                last.then_inc(back, 1)

        @block.vector
        def _(dve):
            chain = Chain(dve, vec_done)
            nc.vector.tensor_tensor(c.logits[:, 0:hd, :], c.logits[:, 0:hd, :],
                                    c.outside[:].unsqueeze(1).to_broadcast([P, hd, STEPS]), ALU.add).then_inc(masked, 1)
            for k in range(NCH):
                dve.wait_ge(turned, k + 1)
                for h in range(hd):
                    last = nc.vector.tensor_tensor_scan(run[:, h, :], c.border[:, k, 0:P], turned_logits(k, h),
                                                        -BIG, ALU.add, ALU.max)
                chain(last)
                for h in range(hd):
                    last = nc.vector.tensor_tensor_scan(seg_max[:, k, h, ::-1], c.border[:, k, 1:P + 1][:, ::-1],
                                                        run[:, h, ::-1], -BIG, ALU.add, ALU.max)
                last.then_inc(scanned, 1)
                dve.wait_ge(scanned, k + 1)
            chain(nc.vector.tensor_copy(edge_vals[:, 0], seg_max[:, :, :, 0]))
            nc.vector.tensor_copy(edge_vals[:, 1], seg_max[:, :, :, P - 1]).then_inc(edges_out, 1)
            dve.wait_ge(edges_turned, 1)
            chain(nc.vector.tensor_tensor_scan(chains[0:hd, 0], c.stop_forward[0:hd, :], c.banks[5][0:hd, 0:STEPS],
                                               -BIG, ALU.add, ALU.max))
            chain(nc.vector.tensor_tensor_scan(chains[0:hd, 1, ::-1], c.stop_backward[0:hd, ::-1],
                                               c.banks[4][0:hd, 0:STEPS][:, ::-1], -BIG, ALU.add, ALU.max))
            chain(nc.vector.memset(carry[:], -BIG))
            chain(nc.vector.tensor_tensor(carry[0:hd, 0, 1:STEPS], chains[0:hd, 0, 0:STEPS - 1],
                                          c.new_dst[0:hd, 1:STEPS], ALU.add))
            nc.vector.tensor_tensor(carry[0:hd, 1, 0:STEPS - 1], chains[0:hd, 1, 1:STEPS],
                                    c.new_dst[0:hd, 1:STEPS], ALU.add).then_inc(carries, 1)
            dve.wait_ge(carries_turned, 1)
            chain(nc.vector.tensor_copy(carry_t[:].rearrange("p k b h -> p (k b h)"),
                                        c.banks[6][0:CH, 0:NCH * 2 * hd]))
            for b, off in ((0, c.not_first), (1, c.not_last)):
                for k in range(NCH):
                    for h in range(hd):
                        last = nc.vector.scalar_tensor_tensor(seg_max[:, k, h, :], off[:, k, :], carry_t[:, k, b, h:h + 1],
                                                              seg_max[:, k, h, :], ALU.add, ALU.max)
                chain(last)
            dve.sem_inc(maxima, 1)
            for h in range(hd):
                dve.wait_ge(back, h + 1)
                m = c.banks[h][:, 0:STEPS]
                nc.vector.tensor_tensor(c.shares[:, :, hd + h], m, c.is_end[:], ALU.mult)
                nc.vector.tensor_tensor(c.logits[:, h, :], c.logits[:, h, :], m, ALU.subtract).then_inc(args, 1)

        @block.scalar
        def _(act):
            for h in range(hd):
                act.wait_ge(args, h + 1)
                nc.scalar.activation(c.shares[:, :, h], c.logits[:, h, :], ACT.Exp)



def pass_b(nc, c, heads):
    with ExitStack() as st:
        def sb(name, shape, dt=F32):
            return st.enter_context(nc.sbuf_tensor(unique(c, name), shape, dt))

        values = sb("values", [P, U, D])
        weighted = sb("weighted", [P, U, D])
        onehot = sb("onehot", [P, U, P])
        values_in = [st.enter_context(semaphore(nc, c, f"values_in{u}")) for u in range(U)]
        weighted_ready = st.enter_context(semaphore(nc, c, "weighted_ready"))
        summed = st.enter_context(semaphore(nc, c, "summed"))
        added = st.enter_context(semaphore(nc, c, "added"))
        cleared = st.enter_context(semaphore(nc, c, "acc_cleared"))
        width = D + 2 * heads
        block = st.enter_context(nc.Block())

        @block.sync
        def _(sp):
            with sp.Fori(0, TRIPS) as t:
                for u in range(U):
                    s = t * U + u
                    sp.wait_ge(weighted_ready, s + 1)
                    sp.dma_start(values[:, u, :], c.stash[:, bass.ds(s * D, D)]).then_inc(values_in[u], 16)

        @block.vector
        def _(dve):
            nc.vector.memset(c.acc[:], 0.0).then_inc(cleared, 1)
            dve.sem_inc(weighted_ready, U)
            dve.sem_inc(added, U)
            dve.wait_ge(cleared, 1)
            with dve.Fori(0, TRIPS) as t:
                js = [dve.value_load(c.window_i[0:1, bass.ds(t * U + u, 1)], min_val=0, max_val=WINDOWS - 1)
                      for u in range(U)]
                for u in range(U):
                    s = t * U + u
                    dve.wait_ge(summed, s + 1)
                    nc.vector.tensor_scalar(onehot[:, u, :], c.iota[:, 0:P], c.dst_local[:, bass.ds(s, 1)], None, ALU.is_equal)
                    dve.wait_ge(values_in[u], t * 16 + 16)
                    nc.vector.tensor_tensor(
                        weighted[:, u, :].rearrange("p (h k) -> p h k", h=heads),
                        values[:, u, :].rearrange("p (h k) -> p h k", h=heads),
                        c.shares[:, bass.ds(s, 1), 0:heads].rearrange("p s h -> p (s h)").unsqueeze(2).to_broadcast([P, heads, D // heads]),
                        ALU.mult).then_inc(weighted_ready, 1)
                for u in range(U):
                    s = t * U + u
                    dve.wait_ge(summed, s + 1 + U)
                    dve.wait_ge(added, s + U)
                    nc.vector.tensor_tensor(c.acc[:, js[u], 0:width], c.acc[:, js[u], 0:width],
                                            c.banks[u][:, 0:width], ALU.add).then_inc(added, 1)

        @block.tensor
        def _(pe):
            pe.sem_inc(summed, U)
            with pe.Fori(0, TRIPS) as t:
                for u in range(U):
                    s = t * U + u
                    pe.wait_ge(weighted_ready, s + 1 + U)
                    pe.wait_ge(added, s + 1)
                    nc.tensor.matmul(c.banks[u][:, 0:D], onehot[:, u, :], weighted[:, u, :], start=True, stop=True)
                    nc.tensor.matmul(c.banks[u][:, D:width], onehot[:, u, :],
                                     c.shares[:, bass.ds(s, 1), 0:2 * heads].rearrange("p s h -> p (s h)"),
                                     start=True, stop=True).then_inc(summed, 1)


def attention(nc, c, heads, pass_a):
    with nc.sbuf_tensor(unique(c, c.layer + "_logits"), [P, heads, STEPS], F32) as c.logits:
        pass_a()
        with nc.sbuf_tensor(unique(c, c.layer + "_shares"), [P, STEPS, 2 * heads], F32) as c.shares:
            edge_softmax(nc, c, heads)
            pass_b(nc, c, heads)



def onehot_for_step(nc, c, onehot, u, s):
    return nc.vector.tensor_scalar(onehot[:, u, :], c.iota[:, 0:P], c.dst_local[:, bass.ds(s, 1)], None, ALU.is_equal)


def load_windows(engine, c, t):
    return [engine.value_load(c.window_i[0:1, bass.ds(t * U + u, 1)], min_val=0, max_val=WINDOWS - 1) for u in range(U)]


def pass_a_gat(nc, c, table, parts, weighted):
    with ExitStack() as st:
        def sb(name, shape, dt=F32):
            return st.enter_context(nc.sbuf_tensor(unique(c, name), shape, dt))

        rows = sb("rows", [P, U, GAT_ROW])
        idx = sb("idx", [P, U], I32)
        onehot = sb("onehot", [P, U, P])
        onehot_t = sb("onehot_t", [P, U, P], BF16)
        gathered = [st.enter_context(semaphore(nc, c, f"gathered{u}")) for u in range(U)]
        stored = [st.enter_context(semaphore(nc, c, f"stored{u}")) for u in range(U)]
        idx_ready = st.enter_context(semaphore(nc, c, "idx_ready"))
        issue = st.enter_context(semaphore(nc, c, "issue"))
        onehot_ready = st.enter_context(semaphore(nc, c, "onehot_ready"))
        turned = st.enter_context(semaphore(nc, c, "onehot_turned"))
        copied = st.enter_context(semaphore(nc, c, "onehot_t_copied"))
        fetched = st.enter_context(semaphore(nc, c, "dst_term_ready"))
        logits_out = st.enter_context(semaphore(nc, c, "logits_written"))
        block = st.enter_context(nc.Block())

        @block.gpsimd
        def _(pool):
            with pool.Fori(0, TRIPS) as t:
                for u in range(U):
                    s = t * U + u
                    pool.wait_ge(idx_ready, s + 1)
                    pool.wait_ge(logits_out, t + 1)
                    pool.wait_ge(stored[u], t * 16 + 16)
                    pool.sem_inc(issue, 1)
                    nc.gpsimd.indirect_dma_start(out=rows[:, u, :], out_offset=None, in_=table[:, :],
                                                 in_offset=bass.IndirectOffsetOnAxis(ap=idx[:, u:u + 1], axis=0)
                                                 ).then_inc(gathered[u], 16)

        @block.sync
        def _(sp):
            for u in range(U):
                sp.sem_inc(stored[u], 16)
            with sp.Fori(0, TRIPS) as t:
                for u in range(U):
                    s = t * U + u
                    sp.wait_ge(gathered[u], t * 16 + 16)
                    sp.dma_start(c.stash[:, bass.ds(s * D, D)], rows[:, u, 0:D]).then_inc(stored[u], 16)
            for u in range(U):
                sp.wait_ge(stored[u], 16 * (TRIPS + 1))

        @block.vector
        def _(dve):
            dve.sem_inc(logits_out, 1)
            nc.vector.tensor_copy(idx[:], c.idx_src[:, 0:U]).then_inc(idx_ready, U)
            with dve.Fori(0, TRIPS) as t:
                for u in range(U):
                    s = t * U + u
                    dve.wait_ge(turned, s + 1)
                    onehot_for_step(nc, c, onehot, u, s).then_inc(onehot_ready, 1)
                for u in range(U):
                    s = t * U + u
                    dve.wait_ge(gathered[u], t * 16 + 16)
                    nc.vector.tensor_scalar(idx[:, u:u + 1], c.idx_src[:, bass.ds(s + U, 1)], 0, None,
                                            ALU.add).then_inc(idx_ready, 1)
                dve.wait_ge(fetched, t * U + 2 * U)
                nc.vector.tensor_tensor(c.logits[:, 0:H4, bass.ds(t * U, U)], rows[:, :, D:D + H4].rearrange("p u h -> p h u"),
                                        c.banks[2][:, 0:U * H4].rearrange("p (u h) -> p h u", h=H4),
                                        ALU.add).then_inc(logits_out, 1)

        @block.tensor
        def _(pe):
            pe.sem_inc(turned, U)
            pe.sem_inc(fetched, U)
            with pe.Fori(0, TRIPS) as t:
                js = load_windows(pe, c, t)
                for u in range(U):
                    s = t * U + u
                    pe.wait_ge(onehot_ready, s + 1)
                    pe.wait_ge(copied, t * 2 + half_of(u) + 1)
                    nc.tensor.transpose(region(c, 0, u), onehot[:, u, :], c.ident[:]).then_inc(turned, 1)
                for u in range(U):
                    s = t * U + u
                    pe.wait_ge(copied, t * 2 + half_of(u) + 3)
                    pe.wait_ge(logits_out, t + 1)
                    for k in range(3):
                        last = nc.tensor.matmul(c.banks[2][:, u * H4:(u + 1) * H4], onehot_t[:, u, :],
                                                parts[k][:, js[u], :], start=k == 0, stop=k == 2)
                    last.then_inc(fetched, 1)

        @block.scalar
        def _(act):
            act.sem_inc(copied, 2)
            with act.Fori(0, TRIPS) as t:
                for k, (lo, hi) in enumerate(HALVES):
                    act.wait_ge(turned, t * U + hi + U)
                    act.wait_ge(fetched, t * U + hi)
                    nc.scalar.copy(onehot_t[:, lo:hi, :], half_bank(c, 0, k)).then_inc(copied, 1)
    gat_logits(nc, c, weighted)


def pass_a_hgt(nc, c, table, parts):
    with ExitStack() as st:
        def sb(name, shape, dt=F32):
            return st.enter_context(nc.sbuf_tensor(unique(c, name), shape, dt))

        rows = sb("rows", [P, U, 2 * D])
        idx = sb("idx", [P, U], I32)
        onehot = sb("onehot", [P, U, P])
        onehot_t = sb("onehot_t", [P, U, P], BF16)
        product = sb("product", [P, U, D])
        scores = sb("scores", [P, U, H8])
        gathered = [st.enter_context(semaphore(nc, c, f"gathered{u}")) for u in range(U)]
        stored = [st.enter_context(semaphore(nc, c, f"stored{u}")) for u in range(U)]
        idx_ready = st.enter_context(semaphore(nc, c, "idx_ready"))
        issue = st.enter_context(semaphore(nc, c, "issue"))
        onehot_ready = st.enter_context(semaphore(nc, c, "onehot_ready"))
        turned = st.enter_context(semaphore(nc, c, "onehot_turned"))
        copied = st.enter_context(semaphore(nc, c, "onehot_t_copied"))
        fetched = st.enter_context(semaphore(nc, c, "queries_ready"))
        product_ready = st.enter_context(semaphore(nc, c, "product_ready"))
        scores_ready = st.enter_context(semaphore(nc, c, "scores_ready"))
        scores_out = st.enter_context(semaphore(nc, c, "scores_out"))
        block = st.enter_context(nc.Block())

        @block.gpsimd
        def _(pool):
            with pool.Fori(0, TRIPS) as t:
                for u in range(U):
                    s = t * U + u
                    pool.wait_ge(idx_ready, s + 1)
                    pool.wait_ge(product_ready, t * 2 + half_of(u) + 1)
                    pool.wait_ge(stored[u], t * 16 + 16)
                    pool.sem_inc(issue, 1)
                    nc.gpsimd.indirect_dma_start(out=rows[:, u, :], out_offset=None, in_=table[:, :],
                                                 in_offset=bass.IndirectOffsetOnAxis(ap=idx[:, u:u + 1], axis=0)
                                                 ).then_inc(gathered[u], 16)

        @block.sync
        def _(sp):
            for u in range(U):
                sp.sem_inc(stored[u], 16)
            with sp.Fori(0, TRIPS) as t:
                for u in range(U):
                    s = t * U + u
                    sp.wait_ge(gathered[u], t * 16 + 16)
                    sp.dma_start(c.stash[:, bass.ds(s * D, D)], rows[:, u, D:2 * D]).then_inc(stored[u], 16)
            for u in range(U):
                sp.wait_ge(stored[u], 16 * (TRIPS + 1))

        @block.vector
        def _(dve):
            dve.sem_inc(product_ready, 2)
            dve.sem_inc(scores_out, 1)
            nc.vector.tensor_copy(idx[:], c.idx_typed[:, 0:U]).then_inc(idx_ready, U)
            with dve.Fori(0, TRIPS) as t:
                for u in range(U):
                    s = t * U + u
                    dve.wait_ge(turned, s + 1)
                    onehot_for_step(nc, c, onehot, u, s).then_inc(onehot_ready, 1)
                dve.wait_ge(scores_out, t + 1)
                for u in range(U):
                    s = t * U + u
                    dve.wait_ge(gathered[u], t * 16 + 16)
                    nc.vector.tensor_scalar(idx[:, u:u + 1], c.idx_typed[:, bass.ds(s + U, 1)], 0, None,
                                            ALU.add).then_inc(idx_ready, 1)
                for k, (lo, hi) in enumerate(HALVES):
                    dve.wait_ge(fetched, t * U + hi + U)
                    nc.vector.tensor_tensor(product[:, lo:hi, :], rows[:, lo:hi, 0:D], half_bank(c, 2, k),
                                            ALU.mult).then_inc(product_ready, 1)
                for k, (lo, hi) in enumerate(HALVES):
                    dve.wait_ge(product_ready, t * 2 + k + 3)
                    nc.vector.tensor_reduce(scores[:, lo:hi, :].rearrange("p u h -> p (u h)"),
                                            product[:, lo:hi, :].rearrange("p u (h k) -> p (u h) k", h=H8),
                                            AX.X, ALU.add).then_inc(scores_ready, 1)
                dve.wait_ge(scores_ready, t * 2 + 2)
                nc.vector.tensor_scalar(c.logits[:, :, bass.ds(t * U, U)], scores[:].rearrange("p u h -> p h u"), 0.0, None,
                                        ALU.add).then_inc(scores_out, 1)

        @block.tensor
        def _(pe):
            pe.sem_inc(turned, U)
            pe.sem_inc(fetched, U)
            with pe.Fori(0, TRIPS) as t:
                js = load_windows(pe, c, t)
                for u in range(U):
                    s = t * U + u
                    pe.wait_ge(onehot_ready, s + 1)
                    pe.wait_ge(copied, t * 2 + half_of(u) + 1)
                    nc.tensor.transpose(region(c, 0, u), onehot[:, u, :], c.ident[:]).then_inc(turned, 1)
                for u in range(U):
                    s = t * U + u
                    pe.wait_ge(copied, t * 2 + half_of(u) + 3)
                    pe.wait_ge(product_ready, t * 2 + half_of(u) + 1)
                    for k in range(3):
                        last = nc.tensor.matmul(region(c, 2, u), onehot_t[:, u, :],
                                                parts[k][:, js[u], :], start=k == 0, stop=k == 2)
                    last.then_inc(fetched, 1)

        @block.scalar
        def _(act):
            act.sem_inc(copied, 2)
            with act.Fori(0, TRIPS) as t:
                for k, (lo, hi) in enumerate(HALVES):
                    act.wait_ge(turned, t * U + hi + U)
                    act.wait_ge(fetched, t * U + hi)
                    nc.scalar.copy(onehot_t[:, lo:hi, :], half_bank(c, 0, k)).then_inc(copied, 1)


def pass_a_relational(nc, c, table, rel_table, parts, y_w, rel_acc):
    with ExitStack() as st:
        def sb(name, shape, dt=F32):
            return st.enter_context(nc.sbuf_tensor(unique(c, name), shape, dt))

        rows = sb("rows", [P, U, 2 * D])
        rel_rows = sb("rel_rows", [P, U, Z_ROW])
        values = sb("values", [P, U, D])
        idx = sb("idx", [P, 2, U], I32)
        onehot = sb("onehot", [P, U, P])
        onehot_t = sb("onehot_t", [P, U, P], BF16)
        leaky = sb("leaky", [P, U, 2, P])
        gathered = [st.enter_context(semaphore(nc, c, f"gathered{u}")) for u in range(U)]
        rel_gathered = [st.enter_context(semaphore(nc, c, f"rel_gathered{u}")) for u in range(U)]
        stored = [st.enter_context(semaphore(nc, c, f"stored{u}")) for u in range(U)]
        idx_ready = st.enter_context(semaphore(nc, c, "idx_ready"))
        issue = st.enter_context(semaphore(nc, c, "issue"))
        onehot_ready = st.enter_context(semaphore(nc, c, "onehot_ready"))
        turned = st.enter_context(semaphore(nc, c, "onehot_turned"))
        copied = st.enter_context(semaphore(nc, c, "onehot_t_copied"))
        pre_ready = st.enter_context(semaphore(nc, c, "pre_ready"))
        leaky_ready = st.enter_context(semaphore(nc, c, "leaky_ready"))
        values_ready = st.enter_context(semaphore(nc, c, "values_ready"))
        rel_summed = st.enter_context(semaphore(nc, c, "rel_summed"))
        rel_added = st.enter_context(semaphore(nc, c, "rel_added"))
        scored = st.enter_context(semaphore(nc, c, "scored"))
        logits_out = st.enter_context(semaphore(nc, c, "logits_written"))
        cleared = st.enter_context(semaphore(nc, c, "rel_cleared"))
        block = st.enter_context(nc.Block())

        @block.gpsimd
        def _(pool):
            with pool.Fori(0, TRIPS) as t:
                for u in range(U):
                    s = t * U + u
                    pool.wait_ge(idx_ready, s + 1)
                    pool.wait_ge(values_ready, s + 1)
                    pool.wait_ge(rel_summed, s + 1)
                    pool.sem_inc(issue, 1)
                    nc.gpsimd.indirect_dma_start(out=rows[:, u, :], out_offset=None, in_=table[:, :],
                                                 in_offset=bass.IndirectOffsetOnAxis(ap=idx[:, 0, u:u + 1], axis=0)
                                                 ).then_inc(gathered[u], 16)
                    nc.gpsimd.indirect_dma_start(out=rel_rows[:, u, :], out_offset=None, in_=rel_table[:, :],
                                                 in_offset=bass.IndirectOffsetOnAxis(ap=idx[:, 1, u:u + 1], axis=0)
                                                 ).then_inc(rel_gathered[u], 16)

        @block.sync
        def _(sp):
            for u in range(U):
                sp.sem_inc(stored[u], 16)
            with sp.Fori(0, TRIPS) as t:
                for u in range(U):
                    s = t * U + u
                    sp.wait_ge(values_ready, s + 1 + U)
                    sp.dma_start(c.stash[:, bass.ds(s * D, D)], values[:, u, :]).then_inc(stored[u], 16)
            for u in range(U):
                sp.wait_ge(stored[u], 16 * (TRIPS + 1))

        @block.vector
        def _(dve):
            nc.vector.memset(rel_acc[:], 0.0).then_inc(cleared, 1)
            dve.sem_inc(values_ready, U)
            dve.sem_inc(rel_added, 2)
            dve.sem_inc(logits_out, 1)
            nc.vector.tensor_copy(idx[:, 0], c.idx_src[:, 0:U]).then_inc(cleared, 1)
            dve.wait_ge(cleared, 2)
            nc.vector.tensor_copy(idx[:, 1], c.idx_rel[:, 0:U]).then_inc(idx_ready, U)
            with dve.Fori(0, TRIPS) as t:
                js = load_windows(dve, c, t)
                for u in range(U):
                    s = t * U + u
                    dve.wait_ge(rel_summed, s + 1)
                    onehot_for_step(nc, c, onehot, u, s).then_inc(onehot_ready, 1)
                for u in range(U):
                    s = t * U + u
                    dve.wait_ge(gathered[u], t * 16 + 16)
                    dve.wait_ge(rel_gathered[u], t * 16 + 16)
                    nc.vector.tensor_scalar(idx[:, 0, u:u + 1], c.idx_src[:, bass.ds(s + U, 1)], 0, None, ALU.add)
                    nc.vector.tensor_scalar(idx[:, 1, u:u + 1], c.idx_rel[:, bass.ds(s + U, 1)], 0, None,
                                            ALU.add).then_inc(idx_ready, 1)
                    dve.wait_ge(stored[u], t * 16 + 16)
                    nc.vector.tensor_tensor(values[:, u, :], rows[:, u, D:2 * D], rel_rows[:, u, D:2 * D],
                                            ALU.add).then_inc(values_ready, 1)
                for u in range(U):
                    s = t * U + u
                    dve.wait_ge(rel_summed, s + 1 + U)
                    dve.wait_ge(rel_added, s + 2)
                    nc.vector.tensor_tensor(rel_acc[:, js[u], :], rel_acc[:, js[u], :],
                                            c.banks[4 + u % 2 if u < 4 else 7][:, 0:Z_ROW], ALU.add).then_inc(rel_added, 1)
                dve.wait_ge(scored, t * U + 2 * U)
                nc.vector.tensor_scalar(c.logits[:, :, bass.ds(t * U, U)],
                                        c.banks[6][:, 0:U * H8].rearrange("p (u h) -> p h u", h=H8), 0.0, None,
                                        ALU.add).then_inc(logits_out, 1)

        @block.tensor
        def _(pe):
            pe.sem_inc(pre_ready, U)
            pe.sem_inc(rel_summed, U)
            pe.sem_inc(scored, U)
            with pe.Fori(0, TRIPS) as t:
                js = load_windows(pe, c, t)
                for u in range(U):
                    s = t * U + u
                    pe.wait_ge(onehot_ready, s + 1)
                    pe.wait_ge(copied, t * 2 + half_of(u) + 1)
                    nc.tensor.transpose(region(c, 0, u), onehot[:, u, :], c.ident[:]).then_inc(turned, 1)
                for u in range(U):
                    s = t * U + u
                    pre = region(c, 2, u)
                    pe.wait_ge(gathered[u], t * 16 + 16)
                    pe.wait_ge(leaky_ready, t * 2 + half_of(u) + 1)
                    nc.tensor.matmul(pre, rows[:, u, 0:D], c.ident[:], start=True, stop=False)
                    pe.wait_ge(rel_gathered[u], t * 16 + 16)
                    nc.tensor.matmul(pre, rel_rows[:, u, 0:D], c.ident[:], start=False, stop=False)
                    pe.wait_ge(copied, t * 2 + half_of(u) + 3)
                    pe.sem_inc(issue, 1)
                    for k in range(3):
                        last = nc.tensor.matmul(pre, parts[k][:, js[u], :], onehot_t[:, u, :], start=False, stop=k == 2)
                    last.then_inc(pre_ready, 1)
                    pe.wait_ge(rel_added, s + 1)
                    nc.tensor.matmul(c.banks[4 + u % 2 if u < 4 else 7][:, 0:Z_ROW], onehot[:, u, :], rel_rows[:, u, :],
                                     start=True, stop=True).then_inc(rel_summed, 1)
                for u in range(U):
                    s = t * U + u
                    pe.wait_ge(leaky_ready, t * 2 + half_of(u) + 3)
                    pe.wait_ge(logits_out, t + 1)
                    for k in range(2):
                        last = nc.tensor.matmul(c.banks[6][:, u * H8:(u + 1) * H8], leaky[:, u, k, :], y_w,
                                                start=k == 0, stop=k == 1)
                    last.then_inc(scored, 1)

        @block.scalar
        def _(act):
            act.sem_inc(copied, 2)
            act.sem_inc(leaky_ready, 2)
            with act.Fori(0, TRIPS) as t:
                for k, (lo, hi) in enumerate(HALVES):
                    act.wait_ge(turned, t * U + hi)
                    act.wait_ge(pre_ready, t * U + hi)
                    nc.scalar.copy(onehot_t[:, lo:hi, :], half_bank(c, 0, k)).then_inc(copied, 1)
                for k, (lo, hi) in enumerate(HALVES):
                    act.wait_ge(pre_ready, t * U + hi + U)
                    act.wait_ge(scored, t * U + hi)
                    nc.scalar.activation(leaky[:, lo:hi, 0, :], half_bank(c, 2, k), ACT.Copy, scale=SLOPE)
                    nc.scalar.activation(leaky[:, lo:hi, 1, :], half_bank(c, 2, k), ACT.Relu,
                                         scale=1.0 - SLOPE).then_inc(leaky_ready, 1)



def layer0(nc, c, a):
    wide, per_head = [P, WINDOWS, D], [P, WINDOWS, H8, D // H8]
    normalise(nc, c)
    with ExitStack() as st:
        def sb(name, shape, dt=F32):
            return st.enter_context(nc.sbuf_tensor(unique(c, name), shape, dt))

        rel_acc = sb("rel_acc", [P, WINDOWS, Z_ROW])
        y_w = sb("y_w", [D, H8])
        c.acc = sb("acc", [P, WINDOWS, D + 2 * H8])
        with ExitStack() as inner:
            def sbi(name, shape, dt=F32):
                return inner.enter_context(nc.sbuf_tensor(unique(c, name), shape, dt))
            parts = [sbi(f"dst_part{k}", [P, WINDOWS, D], BF16) for k in range(3)]
            c.h_t = sbi("h_t", [D, N_PAD])
            with ExitStack() as pre:
                def sbp(name, shape, dt=F32):
                    return pre.enter_context(nc.sbuf_tensor(unique(c, name), shape, dt))
                w_node = sbp("w_node", [D, 3, D])
                w_rel = sbp("w_rel", [D, 2, D])
                z = sbp("z", [RELS // 2, 2, D])
                z_t = sbp("z_t", [D, RELS])
                z_rows = sbp("z_rows", [RELS // 2, 2, Z_ROW])
                proj = sbp("proj", [P, WINDOWS, 3 * D])
                with semaphore(nc, c, "weights_in") as weights_in, nc.Block() as block:
                    @block.sync
                    def _(sp):
                        for to, source in ((w_node[:, 0], a["L0_gnn_P_w"][D:2 * D, :]), (w_node[:, 1], a["L0_gnn_Wc_w"][0:D, :]),
                                           (w_node[:, 2], a["L0_gnn_P_w"][0:D, :]), (w_rel[:, 0], a["L0_gnn_P_w"][2 * D:3 * D, :]),
                                           (w_rel[:, 1], a["L0_gnn_Wc_w"][D:2 * D, :]), (y_w[:], a["L0_gnn_y_w"]),
                                           (z[:], a["L0_gnn_z"].rearrange("(b r) d -> r b d", b=2))):
                            sp.dma_start(to, source).then_inc(weights_in, 16)
                        sp.wait_ge(weights_in, 16 * 7)
                transpose_windows(nc, c, c.h, c.h_t)
                project(nc, c, w_node[:].rearrange("p k d -> p (k d)"), 3 * D, proj)
                with semaphore(nc, c, "z_turned") as z_turned, semaphore(nc, c, "z_t_ready") as z_t_ready, \
                        semaphore(nc, c, "z_projected") as z_projected, semaphore(nc, c, "z_rows_ready") as z_rows_ready, \
                        semaphore(nc, c, "vec_done") as vec_done, semaphore(nc, c, "tables_out") as tables_out, nc.Block() as block:
                    @block.tensor
                    def _(pe):
                        for b in range(2):
                            last = nc.tensor.transpose(c.banks[0][:, b * 100:(b + 1) * 100], z[:, b, :], c.ident[0:100, 0:100])
                        last.then_inc(z_turned, 1)
                        pe.wait_ge(z_t_ready, 1)
                        for b in range(2):
                            last = nc.tensor.matmul(c.banks[1 + b][0:100, 0:2 * D], z_t[:, b * 100:(b + 1) * 100],
                                                    w_rel[:].rearrange("p k d -> p (k d)"), start=True, stop=True)
                        last.then_inc(z_projected, 1)

                    @block.scalar
                    def _(act):
                        act.wait_ge(z_turned, 1)
                        nc.scalar.copy(z_t[:], c.banks[0][:, 0:RELS]).then_inc(z_t_ready, 1)
                        act.wait_ge(z_projected, 1)
                        for b in range(2):
                            nc.scalar.copy(z_rows[:, b, 0:2 * D], c.banks[1 + b][0:100, 0:2 * D]).then_inc(z_rows_ready, 1)

                    @block.vector
                    def _(dve):
                        nc.vector.memset(z_rows[:, :, 2 * D:Z_ROW], 1.0).then_inc(z_rows_ready, 1)
                        split_three(nc, Chain(dve, vec_done), proj[:, :, 2 * D:3 * D], [p[:] for p in parts], c.wide_a[:])

                    @block.sync
                    def _(sp):
                        for k, (table, lo, hi) in enumerate(((c.rel_src_table, 0, 2 * D), (c.rel_dst_table, 2 * D, 3 * D))):
                            sp.dma_start(table.rearrange("(w n) d -> n w d", n=P), proj[:, :, lo:hi]).then_inc(tables_out, 16)
                        sp.wait_ge(z_rows_ready, 3)
                        sp.dma_start(c.z_table.rearrange("(b r) d -> r b d", b=2), z_rows[:]).then_inc(tables_out, 16)
                        sp.wait_ge(tables_out, 48)
            attention(nc, c, H8, lambda: pass_a_relational(nc, c, c.rel_src_table, c.z_table, parts, y_w[:], rel_acc))
        with ExitStack() as fin:
            def sbf(name, shape, dt=F32):
                return fin.enter_context(nc.sbuf_tensor(unique(c, name), shape, dt))
            c.h_t = sbf("pre_self_t", [D, N_PAD])
            src_terms = sbf("src_terms", [P, WINDOWS, 2 * D])
            dst_term = sbf("dst_term", [P, WINDOWS, D])
            resid = sbf("resid", [P, 1])
            small = [sbf(f"small{k}", [P, WINDOWS, H8]) for k in range(5)]
            deg = sbf("deg", [P, WINDOWS, 2])
            with semaphore(nc, c, "terms_in") as terms_in, semaphore(nc, c, "vec_done") as vec_done, nc.Block() as block:
                @block.sync
                def _(sp):
                    sp.dma_start(src_terms[:], c.rel_src_table.rearrange("(w n) d -> n w d", n=P)).then_inc(terms_in, 16)
                    sp.dma_start(dst_term[:], c.rel_dst_table.rearrange("(w n) d -> n w d", n=P)).then_inc(terms_in, 16)
                    sp.dma_start(resid[:], a["L0_gnn_residual_weight"].partition_broadcast(P)).then_inc(terms_in, 16)
                    sp.wait_ge(terms_in, 48)

                @block.vector
                def _(dve):
                    chain = Chain(dve, vec_done)
                    chain(nc.vector.tensor_single_scalar(deg[:, :, 0:1], rel_acc[:, :, 2 * D:Z_ROW], 1.0, ALU.max))
                    chain(nc.vector.reciprocal(deg[:, :, 0:1], deg[:, :, 0:1]))
                    chain(nc.vector.tensor_single_scalar(deg[:, :, 1:2], rel_acc[:, :, 2 * D:Z_ROW], 0.0, ALU.is_gt))
                    chain(nc.vector.tensor_tensor(rel_acc[:, :, 0:2 * D], rel_acc[:, :, 0:2 * D],
                                                  deg[:, :, 0:1].to_broadcast([P, WINDOWS, 2 * D]), ALU.mult))
                    dve.wait_ge(terms_in, 48)
                    chain(nc.vector.tensor_tensor(dst_term[:], dst_term[:], src_terms[:, :, 0:D], ALU.add))
                    chain(nc.vector.tensor_tensor(dst_term[:], dst_term[:], rel_acc[:, :, 0:D], ALU.add))
                    chain(nc.vector.scalar_tensor_tensor(dst_term[:], dst_term[:], SLOPE, dst_term[:], ALU.mult, ALU.max))
                    chain(nc.vector.tensor_tensor(src_terms[:, :, D:2 * D], src_terms[:, :, D:2 * D],
                                                  rel_acc[:, :, D:2 * D], ALU.add))
            transpose_windows(nc, c, dst_term, c.h_t)
            with semaphore(nc, c, "self_scored") as self_scored, semaphore(nc, c, "args_ready") as args_ready, \
                    semaphore(nc, c, "exps_ready") as exps_ready, semaphore(nc, c, "vec_done") as vec_done, nc.Block() as block:
                m_e, self_e, top, f, g = small
                scores = c.banks[0][:, 0:WINDOWS * H8].rearrange("p (w h) -> p w h", h=H8)

                @block.tensor
                def _(pe):
                    for w in range(WINDOWS):
                        last = nc.tensor.matmul(c.banks[0][:, w * H8:(w + 1) * H8], c.h_t[:, w * P:(w + 1) * P], y_w[:],
                                                start=True, stop=True)
                    last.then_inc(self_scored, 1)

                @block.scalar
                def _(act):
                    act.wait_ge(args_ready, 1)
                    nc.scalar.activation(f[:], f[:], ACT.Exp)
                    nc.scalar.activation(g[:], g[:], ACT.Exp).then_inc(exps_ready, 1)

                @block.vector
                def _(dve):
                    chain = Chain(dve, vec_done)
                    chain(nc.vector.tensor_scalar(m_e[:], deg[:, :, 1:2].to_broadcast([P, WINDOWS, H8]), 1.0, BIG,
                                                  ALU.subtract, ALU.mult))
                    chain(nc.vector.tensor_tensor(m_e[:], m_e[:], c.acc[:, :, D + H8:D + 2 * H8], ALU.add))
                    dve.wait_ge(self_scored, 1)
                    chain(nc.vector.tensor_copy(self_e[:], scores))
                    chain(nc.vector.tensor_tensor(top[:], m_e[:], self_e[:], ALU.max))
                    chain(nc.vector.tensor_tensor(f[:], m_e[:], top[:], ALU.subtract))
                    nc.vector.tensor_tensor(g[:], self_e[:], top[:], ALU.subtract).then_inc(args_ready, 1)
                    dve.wait_ge(exps_ready, 1)
                    chain(nc.vector.tensor_tensor(top[:], c.acc[:, :, D:D + H8], f[:], ALU.mult))
                    chain(nc.vector.tensor_tensor(top[:], top[:], g[:], ALU.add))
                    chain(nc.vector.reciprocal(top[:], top[:]))
                    chain(nc.vector.tensor_tensor(f[:], f[:], top[:], ALU.mult))
                    chain(nc.vector.tensor_tensor(g[:], g[:], top[:], ALU.mult))
                    for v, by in ((c.acc[:, :, 0:D], f), (src_terms[:, :, D:2 * D], g)):
                        v4 = v.rearrange("p w (h k) -> p w h k", h=H8)
                        for w in range(WINDOWS):
                            last = nc.vector.tensor_tensor(v4[:, w], v4[:, w],
                                                           by[:, w, :].unsqueeze(2).to_broadcast([P, H8, D // H8]), ALU.mult)
                        chain(last)
                    out = c.wide_a
                    chain(nc.vector.tensor_tensor(out[:], c.acc[:, :, 0:D], src_terms[:, :, D:2 * D], ALU.add))
                    chain(nc.vector.scalar_tensor_tensor(out[:], c.h[:], resid[:], out[:], ALU.mult, ALU.add))
                    chain(nc.vector.scalar_tensor_tensor(out[:], out[:], SLOPE, out[:], ALU.mult, ALU.max))
                    chain(nc.vector.tensor_tensor(out[:], out[:], c.h[:], ALU.subtract))
                    chain(nc.vector.tensor_tensor(out[:], out[:], deg[:, :, 1:2].to_broadcast(wide), ALU.mult))
                    chain(nc.vector.tensor_tensor(out[:], out[:], c.h[:], ALU.add))
                    chain(nc.vector.tensor_tensor(c.x[:], c.x[:], out[:], ALU.add))



def gat_node_phase(nc, c, weights, transpose_weights, att_src, att_dst, rows, a_dst, parts):
    with ExitStack() as st:
        w_in = st.enter_context(nc.sbuf_tensor(unique(c, "w_in"), [D, D], F32))
        w_use = st.enter_context(nc.sbuf_tensor(unique(c, "w_use"), [D, D], F32))
        att = st.enter_context(nc.sbuf_tensor(unique(c, "att"), [P, 2, D], F32))
        normalise(nc, c)
        with semaphore(nc, c, "weights_in") as weights_in, semaphore(nc, c, "w_turned") as w_turned, \
                semaphore(nc, c, "w_done") as w_done, nc.Block() as block:
            @block.sync
            def _(sp):
                sp.dma_start(w_in[:], weights).then_inc(weights_in, 16)
                sp.dma_start(att[:, 0, :], att_src.partition_broadcast(P)).then_inc(weights_in, 16)
                sp.dma_start(att[:, 1, :], att_dst.partition_broadcast(P)).then_inc(weights_in, 16)
                sp.wait_ge(weights_in, 48)

            @block.tensor
            def _(pe):
                pe.wait_ge(weights_in, 48)
                nc.tensor.transpose(c.banks[0][:, 0:D], w_in[:], c.ident[:]).then_inc(w_turned, 1)

            @block.vector
            def _(dve):
                dve.wait_ge(w_turned, 1)
                nc.vector.tensor_copy(w_use[:], c.banks[0][:, 0:D] if transpose_weights else w_in[:])
        transpose_windows(nc, c, c.h, c.h_t)
        project(nc, c, w_use[:], D, rows)
        with semaphore(nc, c, "vec_done") as vec_done, semaphore(nc, c, "rows_ready") as rows_ready, \
                semaphore(nc, c, "table_out") as table_out, nc.Block() as block:
            @block.vector
            def _(dve):
                chain = Chain(dve, vec_done)
                for k, to in ((0, rows[:, :, D:D + H4]), (1, a_dst[:])):
                    chain(nc.vector.tensor_tensor(c.wide_a[:], rows[:, :, 0:D],
                                                  att[:, k:k + 1, :].to_broadcast([P, WINDOWS, D]), ALU.mult))
                    chain(nc.vector.tensor_reduce(to, c.wide_a[:].rearrange("p w (h k) -> p w h k", h=H4), AX.X, ALU.add))
                    if k == 0:
                        dve.sem_inc(rows_ready, 1)
                split_three(nc, chain, a_dst[:], [p[:] for p in parts], c.wide_a[:, :, 0:H4])

            @block.sync
            def _(sp):
                sp.wait_ge(rows_ready, 1)
                sp.dma_start(c.gat_table.rearrange("(w n) d -> n w d", n=P), rows[:]).then_inc(table_out, 16)
                sp.wait_ge(table_out, 16)


def gat_logits(nc, c, weighted):
    with semaphore(nc, c, "vec_done") as vec_done, nc.Block() as block:
        @block.vector
        def _(dve):
            chain = Chain(dve, vec_done)
            lg = c.logits[:, 0:H4, :]
            chain(nc.vector.scalar_tensor_tensor(lg, lg, SLOPE, lg, ALU.mult, ALU.max))
            if weighted:
                chain(nc.vector.tensor_tensor(lg, lg, c.weight[:].unsqueeze(1).to_broadcast([P, H4, STEPS]), ALU.mult))


def scale_heads(nc, chain, v, by, heads):
    v4 = v.rearrange("p w (h k) -> p w h k", h=heads)
    for w in range(WINDOWS):
        last = nc.vector.tensor_tensor(v4[:, w], v4[:, w],
                                       by[:, w, :].unsqueeze(2).to_broadcast([P, heads, D // heads]), ALU.mult)
    chain(last)


def layer1(nc, c, a):
    wide = [P, WINDOWS, D]
    with ExitStack() as st:
        def sb(name, shape, dt=F32):
            return st.enter_context(nc.sbuf_tensor(unique(c, name), shape, dt))
        rows = sb("gat_rows", [P, WINDOWS, GAT_ROW])
        a_dst = sb("a_dst", [P, WINDOWS, H4])
        parts = [sb(f"dst_part{k}", [P, WINDOWS, H4], BF16) for k in range(3)]
        small = [sb(f"small{k}", [P, WINDOWS, H4]) for k in range(5)]
        vecs = sb("vecs", [P, 3, D])
        stat = sb("stat", [P, 2, D])
        c.h_t = sb("h_t", [D, N_PAD])
        c.acc = sb("acc", [P, WINDOWS, D + 2 * H4])
        gat_node_phase(nc, c, a["L1_gnn_W"], False, a["L1_gnn_att_src"].rearrange("h k -> (h k)"),
                       a["L1_gnn_att_dst"].rearrange("h k -> (h k)"), rows, a_dst, parts)
        attention(nc, c, H4, lambda: pass_a_gat(nc, c, c.gat_table, parts, weighted=False))
        with semaphore(nc, c, "vecs_in") as vecs_in, semaphore(nc, c, "args_ready") as args_ready, \
                semaphore(nc, c, "exps_ready") as exps_ready, semaphore(nc, c, "vec_done") as vec_done, \
                semaphore(nc, c, "sums_wanted") as sums_wanted, semaphore(nc, c, "sums_ready") as sums_ready, \
                semaphore(nc, c, "var_ready") as var_ready, semaphore(nc, c, "dev_ready") as dev_ready, nc.Block() as block:
            m_e, self_e, top, f, g = small
            out = c.wide_a

            @block.sync
            def _(sp):
                for k, v in enumerate((a["L1_gnn_bias"], a["L1_gnn_gamma"], a["L1_gnn_beta"])):
                    sp.dma_start(vecs[:, k, :], v.partition_broadcast(P)).then_inc(vecs_in, 16)
                sp.wait_ge(vecs_in, 48)

            @block.tensor
            def _(pe):
                for k, source in enumerate((out, c.h)):
                    pe.wait_ge(sums_wanted, k + 1)
                    for w in range(WINDOWS):
                        rows_in = P if w < WINDOWS - 1 else LAST_NODES
                        last = nc.tensor.matmul(c.banks[k][:, 0:D], c.ones[0:rows_in, :], source[0:rows_in, w, :],
                                                start=w == 0, stop=w == WINDOWS - 1)
                    last.then_inc(sums_ready, 1)

            @block.scalar
            def _(act):
                act.wait_ge(args_ready, 1)
                nc.scalar.activation(f[:], f[:], ACT.Exp)
                nc.scalar.activation(g[:], g[:], ACT.Exp).then_inc(exps_ready, 1)
                act.wait_ge(var_ready, 1)
                nc.scalar.activation(stat[:, 1, :], stat[:, 1, :], ACT.Sqrt).then_inc(dev_ready, 1)
                act.wait_ge(args_ready, 2)
                nc.scalar.activation(c.h[:], c.h[:], ACT.Exp).then_inc(exps_ready, 1)

            @block.vector
            def _(dve):
                chain = Chain(dve, vec_done)
                chain(nc.vector.tensor_tensor(self_e[:], a_dst[:], rows[:, :, D:D + H4], ALU.add))
                chain(nc.vector.scalar_tensor_tensor(self_e[:], self_e[:], SLOPE, self_e[:], ALU.mult, ALU.max))
                chain(nc.vector.tensor_scalar(m_e[:], c.acc[:, :, D:D + H4], 0.5, -BIG, ALU.is_lt, ALU.mult))
                chain(nc.vector.tensor_tensor(m_e[:], m_e[:], c.acc[:, :, D + H4:D + 2 * H4], ALU.add))
                chain(nc.vector.tensor_tensor(top[:], m_e[:], self_e[:], ALU.max))
                chain(nc.vector.tensor_tensor(f[:], m_e[:], top[:], ALU.subtract))
                nc.vector.tensor_tensor(g[:], self_e[:], top[:], ALU.subtract).then_inc(args_ready, 1)
                dve.wait_ge(exps_ready, 1)
                chain(nc.vector.tensor_tensor(top[:], c.acc[:, :, D:D + H4], f[:], ALU.mult))
                chain(nc.vector.tensor_tensor(top[:], top[:], g[:], ALU.add))
                chain(nc.vector.tensor_single_scalar(top[:], top[:], 1e-16, ALU.add))
                chain(nc.vector.reciprocal(top[:], top[:]))
                chain(nc.vector.tensor_tensor(f[:], f[:], top[:], ALU.mult))
                chain(nc.vector.tensor_tensor(g[:], g[:], top[:], ALU.mult))
                scale_heads(nc, chain, c.acc[:, :, 0:D], f, H4)
                scale_heads(nc, chain, rows[:, :, 0:D], g, H4)
                chain(nc.vector.tensor_tensor(out[:], c.acc[:, :, 0:D], rows[:, :, 0:D], ALU.add))
                dve.wait_ge(vecs_in, 48)
                nc.vector.tensor_tensor(out[:], out[:], vecs[:, 0:1, :].to_broadcast(wide), ALU.add).then_inc(sums_wanted, 1)
                dve.wait_ge(sums_ready, 1)
                chain(nc.vector.tensor_single_scalar(stat[:, 0, :], c.banks[0][:, 0:D], 1.0 / N_NODES, ALU.mult))
                chain(nc.vector.tensor_tensor(out[:], out[:], stat[:, 0:1, :].to_broadcast(wide), ALU.subtract))
                nc.vector.tensor_tensor(c.h[:], out[:], out[:], ALU.mult).then_inc(sums_wanted, 1)
                dve.wait_ge(sums_ready, 2)
                nc.vector.tensor_scalar(stat[:, 1, :], c.banks[1][:, 0:D], 1.0 / N_NODES, 1e-5, ALU.mult,
                                        ALU.add).then_inc(var_ready, 1)
                dve.wait_ge(dev_ready, 1)
                chain(nc.vector.reciprocal(stat[:, 1, :], stat[:, 1, :]))
                chain(nc.vector.tensor_tensor(stat[:, 1, :], stat[:, 1, :], vecs[:, 1, :], ALU.mult))
                chain(nc.vector.tensor_tensor(out[:], out[:], stat[:, 1:2, :].to_broadcast(wide), ALU.mult))
                chain(nc.vector.tensor_tensor(out[:], out[:], vecs[:, 2:3, :].to_broadcast(wide), ALU.add))
                nc.vector.tensor_single_scalar(c.h[:], out[:], 0.0, ALU.min).then_inc(args_ready, 1)
                chain(nc.vector.scalar_tensor_tensor(out[:], out[:], 0.0, c.x[:], ALU.max, ALU.add))
                dve.wait_ge(exps_ready, 2)
                chain(nc.vector.scalar_tensor_tensor(c.x[:], c.h[:], -1.0, out[:], ALU.add, ALU.add))


def layer2(nc, c, a):
    with ExitStack() as st:
        def sb(name, shape, dt=F32):
            return st.enter_context(nc.sbuf_tensor(unique(c, name), shape, dt))
        rows = sb("gat_rows", [P, WINDOWS, GAT_ROW])
        a_dst = sb("a_dst", [P, WINDOWS, H4])
        parts = [sb(f"dst_part{k}", [P, WINDOWS, H4], BF16) for k in range(3)]
        f = sb("f", [P, WINDOWS, H4])
        c.h_t = sb("h_t", [D, N_PAD])
        c.acc = sb("acc", [P, WINDOWS, D + 2 * H4])
        gat_node_phase(nc, c, a["L2_gnn_W"], True, a["L2_gnn_a_src"].rearrange("o h k -> (o h k)"),
                       a["L2_gnn_a_dst"].rearrange("o h k -> (o h k)"), rows, a_dst, parts)
        attention(nc, c, H4, lambda: pass_a_gat(nc, c, c.gat_table, parts, weighted=True))
        with semaphore(nc, c, "args_ready") as args_ready, semaphore(nc, c, "exps_ready") as exps_ready, \
                semaphore(nc, c, "vec_done") as vec_done, nc.Block() as block:
            @block.scalar
            def _(act):
                act.wait_ge(args_ready, 1)
                nc.scalar.activation(f[:], f[:], ACT.Exp).then_inc(exps_ready, 1)

            @block.vector
            def _(dve):
                chain = Chain(dve, vec_done)
                m_e, total = c.acc[:, :, D + H4:D + 2 * H4], c.acc[:, :, D:D + H4]
                nc.vector.tensor_single_scalar(f[:], m_e, 0.0, ALU.min).then_inc(args_ready, 1)
                dve.wait_ge(exps_ready, 1)
                chain(nc.vector.tensor_tensor(total, total, f[:], ALU.mult))
                chain(nc.vector.tensor_single_scalar(total, total, 1e-8, ALU.add))
                chain(nc.vector.reciprocal(total, total))
                chain(nc.vector.tensor_tensor(f[:], f[:], total, ALU.mult))
                scale_heads(nc, chain, c.acc[:, :, 0:D], f, H4)
                chain(nc.vector.tensor_tensor(c.x[:], c.x[:], c.acc[:, :, 0:D], ALU.add))



def typed_weights(nc, chain, comp, basis, to):
    for ty in range(TYPES):
        for b in range(BASES):
            s = comp[:, ty * BASES + b:ty * BASES + b + 1]
            if b == 0:
                last = nc.vector.tensor_scalar(to[:, ty, :], basis[:, b, :], s, None, ALU.mult)
            else:
                last = nc.vector.scalar_tensor_tensor(to[:, ty, :], basis[:, b, :], s, to[:, ty, :], ALU.mult, ALU.add)
            chain(last)


def mask_by_type(nc, c, dve, typed, typed_ready, group_used):
    for g, (n0, n) in enumerate(GROUPS):
        if g >= 2:
            dve.wait_ge(group_used, g - 1)
        for ty in range(TYPES):
            last = nc.vector.scalar_tensor_tensor(typed[:, g % 2, ty, 0:n], c.node_type[:, n0:n0 + n], float(ty),
                                                  c.h_t[:, n0:n0 + n], ALU.is_equal, ALU.mult)
        last.then_inc(typed_ready, 1)


def typed_projections(nc, c, w_k, w_v, w_q, k_t, v_t):
    with nc.sbuf_tensor(unique(c, "typed"), [D, 2, TYPES, GROUP], F32) as typed, semaphore(nc, c, "typed_ready") as typed_ready, \
            semaphore(nc, c, "group_used") as group_used, semaphore(nc, c, "job_ready") as job_ready, \
            semaphore(nc, c, "job_taken") as job_taken, nc.Block() as block:
        jobs = []
        for g, (n0, n) in enumerate(GROUPS):
            jobs += [(g, w_k, k_t[:, n0:n0 + n], 0, n), (g, w_v, v_t[:, n0:n0 + n], 0, n)]
            jobs += [(g, w_q, c.h[:, (n0 + at) // P, :], at, 0) for at in range(0, n, P)]

        @block.vector
        def _(dve):
            mask_by_type(nc, c, dve, typed, typed_ready, group_used)

        @block.tensor
        def _(pe):
            for n, (g, w, to, at, cols) in enumerate(jobs):
                pe.wait_ge(typed_ready, g + 1)
                if n >= 8:
                    pe.wait_ge(job_taken, n - 7)
                for ty in range(TYPES):
                    first, final = ty == 0, ty == TYPES - 1
                    if cols:
                        last = nc.tensor.matmul(c.banks[n % 8][:, 0:cols], w[:, ty, :], typed[:, g % 2, ty, 0:cols],
                                                start=first, stop=final)
                    else:
                        last = nc.tensor.matmul(c.banks[n % 8][:, 0:D], typed[:, g % 2, ty, at:at + P], w[:, ty, :],
                                                start=first, stop=final)
                last.then_inc(job_ready, 1)
                if n + 1 == len(jobs) or jobs[n + 1][0] != g:
                    pe.wait_ge(job_ready, n + 1)
                    pe.sem_inc(group_used, 1)

        @block.scalar
        def _(act):
            for n, (g, w, to, at, cols) in enumerate(jobs):
                act.wait_ge(job_ready, n + 1)
                nc.scalar.copy(to, c.banks[n % 8][:, 0:cols or D]).then_inc(job_taken, 1)


def layer3(nc, c, a):
    with ExitStack() as st:
        def sb(name, shape, dt=F32):
            return st.enter_context(nc.sbuf_tensor(unique(c, name), shape, dt))
        w_a = sb("w_a", [D, TYPES, D])
        loop_w = sb("loop_w", [D, D])
        bias = sb("bias", [P, D])
        c.node_type = sb("node_type", [P, N_PAD])
        c.h_t = sb("h_t", [D, N_PAD])
        normalise(nc, c)
        with ExitStack() as inner:
            def sbi(name, shape, dt=F32):
                return inner.enter_context(nc.sbuf_tensor(unique(c, name), shape, dt))
            parts = [sbi(f"dst_part{k}", [P, WINDOWS, D], BF16) for k in range(3)]
            with ExitStack() as pre:
                def sbp(name, shape, dt=F32):
                    return pre.enter_context(nc.sbuf_tensor(unique(c, name), shape, dt))
                w_k, w_v, w_q = (sbp(f"w_{n}", [D, TYPES, D]) for n in "kvq")
                blocks = [sbp(f"blocks_{n}", [D, TYPES, D]) for n in ("att", "msg")]
                k_t, v_t = sbp("k_t", [D, N_PAD]), sbp("v_t", [D, N_PAD])
                transpose_windows(nc, c, c.h, c.h_t)
                with ExitStack() as load:
                    def sbl(name, shape, dt=F32):
                        return load.enter_context(nc.sbuf_tensor(unique(c, name), shape, dt))
                    type_i = sbl("type_i", [P, N_PAD], I32)
                    comp = sbl("comp", [P, 4, TYPES * BASES])
                    basis = sbl("basis", [D, 4, BASES, D])
                    pri = sbl("pri", [P, TYPES, H8])
                    with semaphore(nc, c, "cleared") as cleared, semaphore(nc, c, "loaded") as loaded, \
                            semaphore(nc, c, "vec_done") as vec_done, nc.Block() as block:
                        names = [("k", w_k), ("v", w_v), ("q", w_q), ("a", w_a)]
                        comps = dict(k=a["L3_gnn_w_comp_k"], v=a["L3_gnn_w_comp_v"], q=a["L3_gnn_w_comp_q"], a=a["L3_gnn_w_comp_a"])
                        bases = dict(k=a["L3_gnn_w_basis_k"], v=a["L3_gnn_w_basis_v"], q=a["L3_gnn_w_basis_q"], a=a["L3_gnn_w_basis_a"])
                        N_LOADS = 1 + 8 + 16 + 1 + 2

                        @block.sync
                        def _(sp):
                            sp.wait_ge(cleared, 3)
                            sp.dma_start(type_i[:, 0:N_NODES], a["node_type_8"].partition_broadcast(P)).then_inc(loaded, 16)
                            for k, (n, _w) in enumerate(names):
                                sp.dma_start(comp[:, k, :], comps[n].rearrange("t b -> (t b)").partition_broadcast(P)).then_inc(loaded, 16)
                                sp.dma_start(basis[:, k], bases[n].rearrange("b (i o) -> i b o", o=D)).then_inc(loaded, 16)
                            hd = D // H8
                            for to, source in zip(blocks, (a["L3_gnn_relation_att"], a["L3_gnn_relation_msg"])):
                                for h in range(H8):
                                    sp.dma_start(to[h * hd:(h + 1) * hd, :, h * hd:(h + 1) * hd],
                                                 source[:, h].rearrange("t i j -> i t j")).then_inc(loaded, 16)
                            sp.dma_start(pri[:].rearrange("p t h -> p (t h)"),
                                         a["L3_gnn_relation_pri"].rearrange("t h -> (t h)").partition_broadcast(P)).then_inc(loaded, 16)
                            sp.dma_start(loop_w[:], a["L3_gnn_loop_weight"]).then_inc(loaded, 16)
                            sp.dma_start(bias[:], a["L3_gnn_bias"].partition_broadcast(P)).then_inc(loaded, 16)
                            sp.wait_ge(loaded, 16 * N_LOADS)

                        @block.vector
                        def _(dve):
                            nc.vector.memset(type_i[:], 0).then_inc(cleared, 1)
                            for t in blocks:
                                nc.vector.memset(t[:], 0.0).then_inc(cleared, 1)
                            dve.wait_ge(loaded, 16 * N_LOADS)
                            chain = Chain(dve, vec_done)
                            chain(nc.vector.tensor_copy(c.node_type[:], type_i[:]))
                            for k, (n, w) in enumerate(names):
                                typed_weights(nc, chain, comp[:, k], basis[:, k], w)
                            chain(nc.vector.tensor_single_scalar(pri[:], pri[:], (D // H8) ** -0.5, ALU.mult))
                            for ty in range(TYPES):
                                b4 = blocks[0][:, ty, :].rearrange("p (h k) -> p h k", h=H8)
                                chain(nc.vector.tensor_tensor(b4, b4, pri[:, ty, :].unsqueeze(2).to_broadcast([P, H8, D // H8]),
                                                              ALU.mult))
                typed_projections(nc, c, w_k, w_v, w_q, k_t, v_t)
                with semaphore(nc, c, "vec_done") as vec_done, nc.Block() as block:
                    @block.vector
                    def _(dve):
                        split_three(nc, Chain(dve, vec_done), c.h[:], [p[:] for p in parts], c.wide_a[:])
                with ExitStack() as tab:
                    ring = tab.enter_context(nc.sbuf_tensor(unique(c, "ring"), [P, 2, TYPES, 2, D], F32))
                    with semaphore(nc, c, "half_ready") as half_ready, semaphore(nc, c, "half_taken") as half_taken, \
                            semaphore(nc, c, "half_taken_dve") as half_taken_dve, \
                            semaphore(nc, c, "rows_out0") as rows_out0, semaphore(nc, c, "rows_out1") as rows_out1, nc.Block() as block:
                        rows_out = [rows_out0, rows_out1]
                        quads = [(k, g) for k in range(2) for g in range(2)]

                        @block.tensor
                        def _(pe):
                            for w in range(WINDOWS):
                                for q, (k, g) in enumerate(quads):
                                    if w >= 2:
                                        pe.wait_ge(half_taken if k == 0 else half_taken_dve, 2 * (w - 2) + g + 1)
                                    nc.tensor.matmul(c.banks[(w % 2) * 4 + q][:, :], (k_t, v_t)[k][:, w * P:(w + 1) * P],
                                                     blocks[k][:, 4 * g:4 * g + 4, :].rearrange("p t d -> p (t d)"),
                                                     start=True, stop=True).then_inc(half_ready, 1)

                        @block.scalar
                        def _(act):
                            for w in range(WINDOWS):
                                if w >= 2:
                                    act.wait_ge(rows_out[w % 2], 16 * (w // 2))
                                for g in range(2):
                                    act.wait_ge(half_ready, 4 * w + g + 1)
                                    nc.scalar.copy(ring[:, w % 2, 4 * g:4 * g + 4, 0, :],
                                                   c.banks[(w % 2) * 4 + g][:, :].rearrange("p (t d) -> p t d", t=4)
                                                   ).then_inc(half_taken, 1)

                        @block.vector
                        def _(dve):
                            for w in range(WINDOWS):
                                if w >= 2:
                                    dve.wait_ge(rows_out[w % 2], 16 * (w // 2))
                                for g in range(2):
                                    dve.wait_ge(half_ready, 4 * w + 2 + g + 1)
                                    nc.vector.tensor_copy(ring[:, w % 2, 4 * g:4 * g + 4, 1, :],
                                                          c.banks[(w % 2) * 4 + 2 + g][:, :].rearrange("p (t d) -> p t d", t=4)
                                                          ).then_inc(half_taken_dve, 1)

                        @block.sync
                        def _(sp):
                            for w in range(WINDOWS):
                                sp.wait_ge(half_taken, 2 * w + 2)
                                sp.wait_ge(half_taken_dve, 2 * w + 2)
                                sp.dma_start(c.typed_table[w * P * TYPES:(w + 1) * P * TYPES, :].rearrange("(n t) d -> n (t d)", t=TYPES),
                                             ring[:, w % 2].rearrange("p t k d -> p (t k d)")).then_inc(rows_out[w % 2], 16)
                            sp.wait_ge(rows_out[0], 16 * ((WINDOWS + 1) // 2))
                            sp.wait_ge(rows_out[1], 16 * (WINDOWS // 2))
            c.acc = sbi("acc", [P, WINDOWS, D + 2 * H8])
            attention(nc, c, H8, lambda: pass_a_hgt(nc, c, c.typed_table, parts))
            with ExitStack() as fin:
                hgt_output(nc, c, fin, w_a, loop_w, bias)

def hgt_output(nc, c, fin, w_a, loop_w, bias):
    rden = fin.enter_context(nc.sbuf_tensor(unique(c, "rden"), [P, WINDOWS, H8], F32))
    loop_term = fin.enter_context(nc.sbuf_tensor(unique(c, "loop_term"), [P, WINDOWS, D], F32))
    typed = fin.enter_context(nc.sbuf_tensor(unique(c, "typed"), [D, 2, TYPES, GROUP], F32))
    project(nc, c, loop_w[:], D, loop_term)
    with semaphore(nc, c, "vec_done") as vec_done, nc.Block() as block:
        @block.vector
        def _(dve):
            chain = Chain(dve, vec_done)
            chain(nc.vector.tensor_single_scalar(rden[:], c.acc[:, :, D:D + H8], 1e-30, ALU.max))
            chain(nc.vector.reciprocal(rden[:], rden[:]))
            scale_heads(nc, chain, c.acc[:, :, 0:D], rden, H8)
            chain(nc.vector.tensor_copy(c.h[:], c.acc[:, :, 0:D]))
    transpose_windows(nc, c, c.h, c.h_t)
    with semaphore(nc, c, "typed_ready") as typed_ready, semaphore(nc, c, "group_used") as group_used, \
            semaphore(nc, c, "window_ready") as window_ready, semaphore(nc, c, "window_taken") as window_taken, nc.Block() as block:
        @block.vector
        def _(dve):
            mask_by_type(nc, c, dve, typed, typed_ready, group_used)

        @block.tensor
        def _(pe):
            w = 0
            for g, (n0, n) in enumerate(GROUPS):
                pe.wait_ge(typed_ready, g + 1)
                for at in range(0, n, P):
                    if w >= 4:
                        pe.wait_ge(window_taken, w - 3)
                    for ty in range(TYPES):
                        last = nc.tensor.matmul(c.banks[w % 4][:, 0:D], typed[:, g % 2, ty, at:at + P], w_a[:, ty, :],
                                                start=ty == 0, stop=ty == TYPES - 1)
                    last.then_inc(window_ready, 1)
                    w += 1
                pe.wait_ge(window_ready, w)
                pe.sem_inc(group_used, 1)

        @block.scalar
        def _(act):
            for w in range(WINDOWS):
                act.wait_ge(window_ready, w + 1)
                nc.scalar.copy(c.wide_a[:, w, :], c.banks[w % 4][:, 0:D]).then_inc(window_taken, 1)
    with semaphore(nc, c, "vec_done") as vec_done, nc.Block() as block:
        @block.vector
        def _(dve):
            chain = Chain(dve, vec_done)
            o = c.wide_a
            chain(nc.vector.tensor_tensor(o[:], o[:], loop_term[:], ALU.add))
            chain(nc.vector.tensor_tensor(o[:], o[:], bias[:].unsqueeze(1).to_broadcast([P, WINDOWS, D]), ALU.add))
            chain(nc.vector.scalar_tensor_tensor(c.x[:], o[:], 0.0, c.x[:], ALU.max, ALU.add))


def store_output(nc, c, out):
    with semaphore(nc, c, "out_stored") as out_stored, nc.Block() as block:
        @block.sync
        def _(sp):
            whole = (WINDOWS - 1) * P
            sp.dma_start(out[0:whole, :].rearrange("(w n) d -> n w d", n=P), c.x[:, 0:WINDOWS - 1, :]).then_inc(out_stored, 16)
            sp.dma_start(out[whole:N_NODES, :], c.x[0:LAST_NODES, WINDOWS - 1, :]).then_inc(out_stored, 16)
            sp.wait_ge(out_stored, 32)


def build_program(nc, a, out, layers=4):
    c = State()
    with ExitStack() as st:
        def sb(name, shape, dt=F32):
            return st.enter_context(nc.sbuf_tensor(unique(c, name), shape, dt))

        c.banks = [st.enter_context(nc.psum_tensor(f"bank{k}", [P, 512], F32)) for k in range(8)]
        c.x = sb("x_nodes", [P, WINDOWS, D])
        c.h = sb("h_nodes", [P, WINDOWS, D])
        c.wide_a = sb("wide_a", [P, WINDOWS, D])
        c.ident = sb("ident", [P, P])
        c.ones = sb("ones", [P, P])
        c.iota = sb("iota", [P, 512])
        c.mean, c.rstd = sb("mean", [P, WINDOWS]), sb("rstd", [P, WINDOWS])
        c.window_i = sb("window_i", [1, STEPS], I32)
        c.dst_local = sb("dst_local", [P, STEPS])
        c.outside = sb("outside", [P, STEPS])
        c.is_end = sb("is_end", [P, STEPS])
        c.weight = sb("weight", [P, STEPS])
        c.idx_src = sb("idx_src", [P, STEPS + U], I32)
        c.idx_typed = sb("idx_typed", [P, STEPS + U], I32)
        c.idx_rel = sb("idx_rel", [P, STEPS + U], I32)
        c.border = sb("border", [CH, NCH, P + 1])
        c.not_first = sb("not_first", [CH, NCH, P])
        c.not_last = sb("not_last", [CH, NCH, P])
        c.new_dst = sb("new_dst", [H8, STEPS + 1])
        c.stop_forward = sb("stop_forward", [H8, STEPS])
        c.stop_backward = sb("stop_backward", [H8, STEPS])
        load_constants(nc, c, a)
        build_steps(nc, c, a)
        c.stash = nc.dram_tensor("stash", [P, STEPS * D], F32, kind="Internal").ap()
        c.rel_src_table = nc.dram_tensor("rel_src_table", [N_PAD, 2 * D], F32, kind="Internal").ap()
        c.rel_dst_table = nc.dram_tensor("rel_dst_table", [N_PAD, D], F32, kind="Internal").ap()
        c.z_table = nc.dram_tensor("z_table", [RELS, Z_ROW], F32, kind="Internal").ap()
        c.gat_table = nc.dram_tensor("gat_table", [N_PAD, GAT_ROW], F32, kind="Internal").ap()
        c.typed_table = nc.dram_tensor("typed_table", [N_PAD * TYPES, 2 * D], F32, kind="Internal").ap()
        for n, layer in enumerate((layer0, layer1, layer2, layer3)[0:layers]):
            c.layer = f"layer{n}"
            layer(nc, c, a)
            clear_semaphores(nc, c)
        store_output(nc, c, out)


_INS = ['x', 'src', 'dst', 'edge_type_200', 'edge_type_8', 'edge_weight', 'node_type_8', 'L0_gnn_z', 'L0_gnn_Wc_w',
        'L0_gnn_P_w', 'L0_gnn_y_w', 'L0_gnn_residual_weight', 'L1_gnn_W', 'L1_gnn_att_src', 'L1_gnn_att_dst',
        'L1_gnn_bias', 'L1_gnn_gamma', 'L1_gnn_beta', 'L2_gnn_W', 'L2_gnn_a_src', 'L2_gnn_a_dst', 'L3_gnn_w_comp_k',
        'L3_gnn_w_basis_k', 'L3_gnn_w_comp_q', 'L3_gnn_w_basis_q', 'L3_gnn_w_comp_v', 'L3_gnn_w_basis_v',
        'L3_gnn_w_comp_a', 'L3_gnn_w_basis_a', 'L3_gnn_relation_pri', 'L3_gnn_relation_att', 'L3_gnn_relation_msg',
        'L3_gnn_loop_weight', 'L3_gnn_bias']


def kernel(**inputs):
    import concourse.bacc as bacc
    from concourse.bass_utils import run_bass_kernel_spmd

    nc = bacc.Bacc("TRN2", target_bir_lowering=False, num_devices=1)
    arrays = {f"in_{n}": np.ascontiguousarray(inputs[n]) for n in _INS}
    a = {n: nc.dram_tensor(f"in_{n}", arrays[f"in_{n}"].shape, mybir.dt.from_np(arrays[f"in_{n}"].dtype),
                                             kind="ExternalInput").ap() for n in _INS}
    out = nc.dram_tensor("out", (N_NODES, D), F32, kind="ExternalOutput").ap()
    build_program(nc, a, out)
    r = run_bass_kernel_spmd(nc, [arrays], core_ids=[0])
    return r.results[0]["out"]
```

```python
import numpy as np
import concourse.bass as bass
import concourse.mybir as mybir
from contextlib import ExitStack, contextmanager

F32 = mybir.dt.float32
BF16 = mybir.dt.bfloat16
I32 = mybir.dt.int32
ALU = mybir.AluOpType
ACT = mybir.ActivationFunctionType
AX = mybir.AxisListType

P = 128
N_NODES = 3125
N_EDGES = 50000
D = 128
WINDOWS = -(-N_NODES // P)
LAST_NODES = N_NODES - (WINDOWS - 1) * P
N_PAD = WINDOWS * P
EDGE_TILES = -(-N_EDGES // P)
GROUP = 4
RING = 2
USED_STEPS = EDGE_TILES + WINDOWS - 1
TRIPS = -(-USED_STEPS // (GROUP * RING))
STEPS = TRIPS * GROUP * RING
SUM_RING = 4
SUM_TRIPS = STEPS // (GROUP * SUM_RING)
CH = 104
NCH = STEPS // CH
assert NCH * CH == STEPS and SUM_TRIPS * SUM_RING * GROUP == STEPS
IC = 4
IP = 98
FULL_TILES = N_EDGES // P
TAIL = N_EDGES - FULL_TILES * P
LAST_ROWS = FULL_TILES - (IC - 1) * IP
SENTINEL = 4000
BIG = 1e30
RELS = 200
HALF_RELS = RELS // 2
TYPES = 8
BASES = 4
NODE_GROUP = 512
GROUPS = [(n, min(NODE_GROUP, N_PAD - n)) for n in range(0, N_PAD, NODE_GROUP)]
SLOPE = 0.2
GAT_ROW = D + 4
H8, H4 = 8, 4


class State:

    def __init__(self):
        self.serial = 0
        self.semaphores = []
        self.layer = ""


def unique(c, name):
    c.serial += 1
    return f"{name}_{c.serial}"


@contextmanager
def semaphore(nc, c, name):
    handle = nc.alloc_semaphore(unique(c, name))
    c.semaphores.append(handle)
    yield handle


def clear_semaphores(nc, c):
    nc.all_engine_barrier()
    nc.clear_and_free_semaphores(c.semaphores)
    nc.all_engine_barrier()
    c.semaphores = []


class Chain:

    def __init__(self, engine, sem):
        self.engine, self.sem, self.n = engine, sem, 0

    def __call__(self, instruction):
        self.n += 1
        instruction.then_inc(self.sem, 1)
        self.engine.wait_ge(self.sem, self.n)


def in_bank(bank, n, width):
    return bank[:, n * width:(n + 1) * width]



def load_constants(nc, c, a):
    with semaphore(nc, c, "const_done") as const_done, semaphore(nc, c, "x_loaded") as x_loaded, \
            semaphore(nc, c, "vec_done") as vec_done, nc.sbuf_tensor(unique(c, "iota_i"), [P, 512], I32) as iota_i, \
            nc.Block() as block:

        @block.gpsimd
        def _(pool):
            nc.gpsimd.memset(c.ident[:], 0.0).then_inc(const_done, 1)
            pool.wait_ge(const_done, 1)
            nc.gpsimd.affine_select(out=c.ident[:], in_=c.ident[:], compare_op=ALU.not_equal, fill=1.0, base=0,
                                    pattern=[[-1, P]], channel_multiplier=1).then_inc(const_done, 1)
            nc.gpsimd.iota(iota_i[:], pattern=[[1, 512]], base=0, channel_multiplier=0).then_inc(const_done, 1)

        @block.vector
        def _(dve):
            chain = Chain(dve, vec_done)
            chain(nc.vector.memset(c.x[:], 0.0))
            chain(nc.vector.memset(c.ones[:], 1.0))
            dve.wait_ge(const_done, 3)
            chain(nc.vector.tensor_copy(c.ident_b[:], c.ident[:]))
            chain(nc.vector.tensor_copy(c.iota[:], iota_i[:]))

        @block.sync
        def _(sp):
            sp.wait_ge(vec_done, 1)
            whole = (WINDOWS - 1) * P
            sp.dma_start(c.x[:, 0:WINDOWS - 1, :], a["x"][0:whole, :].rearrange("(w n) d -> n w d", n=P)).then_inc(x_loaded, 16)
            sp.dma_start(c.x[0:LAST_NODES, WINDOWS - 1, :], a["x"][whole:N_NODES, :]).then_inc(x_loaded, 16)
            sp.wait_ge(x_loaded, 32)


def build_steps(nc, c, a):
    with ExitStack() as st:
        def sb(name, shape, dt=F32):
            return st.enter_context(nc.sbuf_tensor(unique(c, name), shape, dt))

        nat_i = sb("nat_i", [IP, 5, IC, P], I32)
        nat = sb("nat", [IP, 6, IC, P])
        tile_i = sb("tile_i", [IP, IC], I32)
        tile_no = sb("tile_no", [IP, IC])
        tile_row = sb("tile_row", [IP, IC, P])
        win_i = sb("win_i", [IP, 2, IC], I32)
        key = sb("key", [IP, 2, IC])
        after = sb("after", [IP, STEPS])
        pick = sb("pick", [IP, IC, STEPS])
        ends = sb("ends", [IP, 2, IC, H8])
        tmp = sb("tmp", [P, STEPS])
        window = sb("window", [P, STEPS])
        dst_t = sb("dst_t", [CH, NCH, P])
        fl = sb("fl", [H8, 2, STEPS])
        single = sb("single", [H8, STEPS])
        loaded = st.enter_context(semaphore(nc, c, "edges_loaded"))
        cleared = st.enter_context(semaphore(nc, c, "nat_cleared"))
        tiles_numbered = st.enter_context(semaphore(nc, c, "tiles_numbered"))
        vec_done = st.enter_context(semaphore(nc, c, "vec_done"))
        picked = st.enter_context(semaphore(nc, c, "picked"))
        by_step = st.enter_context(semaphore(nc, c, "by_step"))
        taken = st.enter_context(semaphore(nc, c, "by_step_taken"))
        by_chunk = st.enter_context(semaphore(nc, c, "by_chunk"))
        block = st.enter_context(nc.Block())
        sources = [(a["dst"], 0), (a["dst"], 1), (a["src"], 0), (a["edge_type_200"], 0), (a["edge_type_8"], 0)]

        @block.sync
        def _(sp):
            sp.wait_ge(cleared, 6)
            n = 0
            for k in range(6):
                source, off = (a["edge_weight"], 0) if k == 5 else sources[k]
                to = nat[:, 5] if k == 5 else nat_i[:, k]
                rows = (IC - 1) * IP
                sp.dma_start(to[:, 0:IC - 1, :],
                             source[off:off + rows * P].rearrange("(c p e) -> p c e", p=IP, e=P)).then_inc(loaded, 16)
                sp.dma_start(to[0:LAST_ROWS, IC - 1, :],
                             source[off + rows * P:off + FULL_TILES * P].rearrange("(p e) -> p e", e=P)).then_inc(loaded, 16)
                sp.dma_start(to[LAST_ROWS:LAST_ROWS + 1, IC - 1, 0:TAIL - off],
                             source[off + FULL_TILES * P:N_EDGES].rearrange("(p e) -> p e", p=1)).then_inc(loaded, 16)
                n += 3
            sp.wait_ge(loaded, 16 * n)

        @block.gpsimd
        def _(pool):
            nc.gpsimd.iota(tile_i[:], pattern=[[IP, IC]], base=0, channel_multiplier=1).then_inc(tiles_numbered, 1)

        @block.vector
        def _(dve):
            for k in range(5):
                nc.vector.memset(nat_i[:, k], SENTINEL if k < 2 else 0).then_inc(cleared, 1)
            nc.vector.memset(nat[:, 5], 0.0).then_inc(cleared, 1)
            chain = Chain(dve, vec_done)
            dve.wait_ge(tiles_numbered, 1)
            chain(nc.vector.tensor_copy(tile_no[:], tile_i[:]))
            chain(nc.vector.tensor_copy(tile_row[:], tile_no[:].unsqueeze(2).to_broadcast([IP, IC, P])))
            dve.wait_ge(loaded, 16 * 18)
            chain(nc.vector.tensor_copy(nat[:, 0:5], nat_i[:]))
            nc.vector.tensor_single_scalar(win_i[:, 0], nat_i[:, 0, :, 0], 7, ALU.arith_shift_right)
            chain(nc.vector.tensor_single_scalar(win_i[:, 1], nat_i[:, 1, :, P - 1], 7, ALU.arith_shift_right))
            chain(nc.vector.tensor_copy(key[:], win_i[:]))
            chain(nc.vector.tensor_tensor(key[:, 0], key[:, 0], tile_no[:], ALU.add))
            chain(nc.vector.scalar_tensor_tensor(key[:, 1], key[:, 1], 1.0, tile_no[:], ALU.add, ALU.add))
            chain(nc.vector.memset(key[0:1, 0, 0:1], 0.0))
            for k in range(IC):
                chain(nc.vector.tensor_scalar(after[:], c.iota[0:IP, 0:STEPS], key[:, 1, k:k + 1], None, ALU.is_ge))
                chain(nc.vector.scalar_tensor_tensor(pick[:, k, :], c.iota[0:IP, 0:STEPS], key[:, 0, k:k + 1], after[:],
                                                     ALU.is_ge, ALU.subtract))
            chain(nc.vector.tensor_copy(ends[:, 0], nat[:, 0, :, 0:1].to_broadcast([IP, IC, H8])))
            chain(nc.vector.tensor_copy(ends[:, 1], nat[:, 0, :, P - 1:P].to_broadcast([IP, IC, H8])))
            nc.vector.tensor_tensor(nat[:, 1], nat[:, 0], nat[:, 1], ALU.not_equal).then_inc(picked, 1)
            dve.wait_ge(by_step, 7)
            chain(nc.vector.tensor_tensor(window[:], c.iota[:, 0:STEPS], c.banks[6][:, 0:STEPS], ALU.subtract))
            chain(nc.vector.tensor_scalar(window[:], window[:], float(WINDOWS - 1), 0.0, ALU.min, ALU.max))
            chain(nc.vector.tensor_copy(c.window_i[:], window[0:1, :]))
            chain(nc.vector.scalar_tensor_tensor(c.dst_local[:], window[:], -float(P), c.banks[0][:, 0:STEPS],
                                                 ALU.mult, ALU.add))
            chain(nc.vector.memset(c.dst_local[:, USED_STEPS:STEPS], -1.0))
            chain(nc.vector.tensor_single_scalar(tmp[:], c.dst_local[:], 0.0, ALU.is_ge))
            chain(nc.vector.scalar_tensor_tensor(tmp[:], c.dst_local[:], float(P), tmp[:], ALU.is_lt, ALU.mult))
            chain(nc.vector.tensor_scalar(c.outside[:], tmp[:], 1.0, BIG, ALU.subtract, ALU.mult))
            chain(nc.vector.tensor_copy(c.is_end[:], c.banks[1][:, 0:STEPS]))
            chain(nc.vector.tensor_copy(tmp[:], c.banks[2][:, 0:STEPS]))
            chain(nc.vector.tensor_copy(c.idx_src[:, 0:STEPS], tmp[:]))
            chain(nc.vector.scalar_tensor_tensor(tmp[:], tmp[:], float(TYPES), c.banks[4][:, 0:STEPS],
                                                 ALU.mult, ALU.add))
            chain(nc.vector.tensor_copy(c.idx_typed[:, 0:STEPS], tmp[:]))
            chain(nc.vector.tensor_copy(c.relation[:], c.banks[3][:, 0:STEPS]))
            chain(nc.vector.tensor_copy(c.weight[:], c.banks[5][:, 0:STEPS]))
            for t in (c.idx_src, c.idx_typed):
                chain(nc.vector.memset(t[:, STEPS:STEPS + RING * GROUP], 0))
            dve.sem_inc(taken, 1)
            dve.wait_ge(by_chunk, 2)
            for k in range(NCH):
                chain(nc.vector.tensor_copy(dst_t[:, k], c.banks[k // 4][0:CH, (k % 4) * P:(k % 4 + 1) * P]))
            chain(nc.vector.memset(c.border[:], -BIG))
            chain(nc.vector.tensor_tensor(c.border[:, :, 1:P], dst_t[:, :, 1:P], dst_t[:, :, 0:P - 1], ALU.not_equal))
            chain(nc.vector.tensor_single_scalar(c.border[:, :, 1:P], c.border[:, :, 1:P], -BIG, ALU.mult))
            for k in range(NCH):
                chain(nc.vector.tensor_scalar(c.not_first[:, k], dst_t[:, k], dst_t[:, k, 0:1], -BIG,
                                              ALU.not_equal, ALU.mult))
                chain(nc.vector.tensor_scalar(c.not_last[:, k], dst_t[:, k], dst_t[:, k, P - 1:P], -BIG,
                                              ALU.not_equal, ALU.mult))
            for k in range(2):
                chain(nc.vector.tensor_copy(fl[:, k], c.banks[2 + k][0:H8, 0:STEPS]))
            chain(nc.vector.memset(c.new_dst[:], -BIG))
            chain(nc.vector.tensor_tensor(c.new_dst[:, 1:STEPS], fl[:, 0, 1:STEPS], fl[:, 1, 0:STEPS - 1], ALU.not_equal))
            chain(nc.vector.tensor_single_scalar(c.new_dst[:, 1:STEPS], c.new_dst[:, 1:STEPS], -BIG, ALU.mult))
            chain(nc.vector.tensor_tensor(single[:], fl[:, 0], fl[:, 1], ALU.not_equal))
            chain(nc.vector.scalar_tensor_tensor(c.stop_forward[:], single[:], -BIG, c.new_dst[:, 0:STEPS], ALU.mult, ALU.add))
            chain(nc.vector.scalar_tensor_tensor(c.stop_backward[:], single[:], -BIG, c.new_dst[:, 1:STEPS + 1], ALU.mult, ALU.add))

        @block.tensor
        def _(pe):
            pe.wait_ge(picked, 1)
            for k in range(7):
                for i in range(IC):
                    lhs = tile_row[:, i, :] if k == 6 else nat[:, k, i, :]
                    last = nc.tensor.matmul(c.banks[k][:, 0:STEPS], lhs, pick[:, i, :], start=i == 0, stop=i == IC - 1)
                last.then_inc(by_step, 1)
            pe.wait_ge(taken, 1)
            for k in range(NCH):
                for i in range(IC):
                    last = nc.tensor.matmul(c.banks[k // 4][0:CH, (k % 4) * P:(k % 4 + 1) * P],
                                            pick[:, i, k * CH:(k + 1) * CH], nat[:, 0, i, :],
                                            start=i == 0, stop=i == IC - 1)
            last.then_inc(by_chunk, 1)
            for k in range(2):
                for i in range(IC):
                    last = nc.tensor.matmul(c.banks[2 + k][0:H8, 0:STEPS], ends[:, k, i, :], pick[:, i, :],
                                            start=i == 0, stop=i == IC - 1)
            last.then_inc(by_chunk, 1)



def layernorm(nc, c, chain):
    wide = [P, WINDOWS, D]
    chain(nc.vector.tensor_reduce(c.mean[:], c.x[:], AX.X, ALU.add))
    chain(nc.vector.tensor_single_scalar(c.mean[:], c.mean[:], 1.0 / D, ALU.mult))
    chain(nc.vector.tensor_tensor(c.h[:], c.x[:], c.mean[:].unsqueeze(2).to_broadcast(wide), ALU.subtract))
    chain(nc.vector.tensor_tensor(c.wide_a[:], c.h[:], c.h[:], ALU.mult))
    chain(nc.vector.tensor_reduce(c.rstd[:], c.wide_a[:], AX.X, ALU.add))
    nc.vector.tensor_scalar(c.rstd[:], c.rstd[:], 1.0 / D, 1e-5, ALU.mult, ALU.add).then_inc(c.stats_ready, 1)
    chain.engine.wait_ge(c.root_ready, 1)
    chain(nc.vector.reciprocal(c.rstd[:], c.rstd[:]))
    chain(nc.vector.tensor_tensor(c.h[:], c.h[:], c.rstd[:].unsqueeze(2).to_broadcast(wide), ALU.mult))
    chain(nc.vector.tensor_single_scalar(c.h[:], c.h[:], 0.0, ALU.max))


def normalise(nc, c):
    with semaphore(nc, c, "stats_ready") as c.stats_ready, semaphore(nc, c, "root_ready") as c.root_ready, \
            semaphore(nc, c, "vec_done") as vec_done, nc.Block() as block:

        @block.vector
        def _(dve):
            layernorm(nc, c, Chain(dve, vec_done))

        @block.scalar
        def _(act):
            act.wait_ge(c.stats_ready, 1)
            nc.scalar.activation(c.rstd[:], c.rstd[:], ACT.Sqrt).then_inc(c.root_ready, 1)


def transpose_windows(nc, c, source, to):
    groups = -(-WINDOWS // 4)
    with semaphore(nc, c, "group_ready") as group_ready, semaphore(nc, c, "group_taken") as group_taken, nc.Block() as block:

        @block.tensor
        def _(pe):
            for g in range(groups):
                if g >= 4:
                    pe.wait_ge(group_taken, g - 3)
                for w in range(4 * g, min(4 * g + 4, WINDOWS)):
                    last = nc.tensor.transpose(c.banks[g % 4][:, (w % 4) * P:(w % 4 + 1) * P], source[:, w, :], c.ident[:])
                last.then_inc(group_ready, 1)

        @block.scalar
        def _(act):
            for g in range(groups):
                n = (min(4 * g + 4, WINDOWS) - 4 * g) * P
                act.wait_ge(group_ready, g + 1)
                nc.scalar.copy(to[:, 4 * g * P:4 * g * P + n], c.banks[g % 4][:, 0:n]).then_inc(group_taken, 1)


def project(nc, c, weights, width, to):
    with semaphore(nc, c, "window_ready") as window_ready, semaphore(nc, c, "window_taken") as window_taken, nc.Block() as block:

        @block.tensor
        def _(pe):
            for w in range(WINDOWS):
                if w >= 4:
                    pe.wait_ge(window_taken, w - 3)
                nc.tensor.matmul(c.banks[w % 4][:, 0:width], c.h_t[:, w * P:(w + 1) * P], weights,
                                 start=True, stop=True).then_inc(window_ready, 1)

        @block.scalar
        def _(act):
            for w in range(WINDOWS):
                act.wait_ge(window_ready, w + 1)
                nc.scalar.copy(to[:, w, 0:width], c.banks[w % 4][:, 0:width]).then_inc(window_taken, 1)


def split_three(nc, chain, value, parts, rest):
    chain(nc.vector.tensor_copy(parts[0], value))
    chain(nc.vector.tensor_tensor(rest, value, parts[0], ALU.subtract))
    chain(nc.vector.tensor_copy(parts[1], rest))
    chain(nc.vector.tensor_tensor(rest, rest, parts[1], ALU.subtract))
    chain(nc.vector.tensor_copy(parts[2], rest))



def edge_softmax(nc, c, heads):
    hd = heads
    with ExitStack() as st:
        seg_max = st.enter_context(nc.sbuf_tensor(unique(c, "seg_max"), [CH, NCH, hd, P], F32))
        run = st.enter_context(nc.sbuf_tensor(unique(c, "run"), [CH, hd, P], F32))
        edge_vals = st.enter_context(nc.sbuf_tensor(unique(c, "edge_vals"), [CH, 2, NCH, hd], F32))
        chains = st.enter_context(nc.sbuf_tensor(unique(c, "chains"), [H8, 2, STEPS], F32))
        carry = st.enter_context(nc.sbuf_tensor(unique(c, "carry"), [H8, 2, STEPS], F32))
        carry_t = st.enter_context(nc.sbuf_tensor(unique(c, "carry_t"), [CH, NCH, 2, hd], F32))
        masked = st.enter_context(semaphore(nc, c, "logits_masked"))
        vec_done = st.enter_context(semaphore(nc, c, "vec_done"))
        turned = st.enter_context(semaphore(nc, c, "logits_turned"))
        scanned = st.enter_context(semaphore(nc, c, "chunk_scanned"))
        edges_out = st.enter_context(semaphore(nc, c, "edge_vals_ready"))
        edges_turned = st.enter_context(semaphore(nc, c, "edge_vals_turned"))
        carries = st.enter_context(semaphore(nc, c, "carries_ready"))
        carries_turned = st.enter_context(semaphore(nc, c, "carries_turned"))
        maxima = st.enter_context(semaphore(nc, c, "maxima_ready"))
        back = st.enter_context(semaphore(nc, c, "maxima_back"))
        args = st.enter_context(semaphore(nc, c, "exp_args_ready"))
        block = st.enter_context(nc.Block())

        def turned_logits(k, h):
            n = (k % 2) * 2 * 4 + h
            return c.banks[n // 4][0:CH, (n % 4) * P:(n % 4 + 1) * P]

        @block.tensor
        def _(pe):
            pe.wait_ge(masked, 1)
            for k in range(NCH):
                if k >= 2:
                    pe.wait_ge(scanned, k - 1)
                for h in range(hd):
                    last = nc.tensor.transpose(turned_logits(k, h), c.logits[:, h, k * CH:(k + 1) * CH], c.ident[:])
                last.then_inc(turned, 1)
            pe.wait_ge(edges_out, 1)
            for b in range(2):
                for k in range(NCH):
                    last = nc.tensor.transpose(c.banks[4 + b][0:hd, k * CH:(k + 1) * CH], edge_vals[:, b, k, :],
                                               c.ident[0:CH, 0:CH])
            last.then_inc(edges_turned, 1)
            pe.wait_ge(carries, 1)
            for k in range(NCH):
                for b in range(2):
                    n = (k * 2 + b) * hd
                    last = nc.tensor.transpose(c.banks[6][0:CH, n:n + hd], carry[0:hd, b, k * CH:(k + 1) * CH],
                                               c.ident[0:hd, 0:hd])
            last.then_inc(carries_turned, 1)
            pe.wait_ge(maxima, 1)
            for h in range(hd):
                for k in range(NCH):
                    last = nc.tensor.transpose(c.banks[h][:, k * CH:(k + 1) * CH], seg_max[:, k, h, :],
                                               c.ident[0:CH, 0:CH])
                last.then_inc(back, 1)

        @block.vector
        def _(dve):
            chain = Chain(dve, vec_done)
            nc.vector.tensor_tensor(c.logits[:, 0:hd, :], c.logits[:, 0:hd, :],
                                    c.outside[:].unsqueeze(1).to_broadcast([P, hd, STEPS]), ALU.add).then_inc(masked, 1)
            for k in range(NCH):
                dve.wait_ge(turned, k + 1)
                for h in range(hd):
                    last = nc.vector.tensor_tensor_scan(run[:, h, :], c.border[:, k, 0:P], turned_logits(k, h),
                                                        -BIG, ALU.add, ALU.max)
                chain(last)
                for h in range(hd):
                    last = nc.vector.tensor_tensor_scan(seg_max[:, k, h, ::-1], c.border[:, k, 1:P + 1][:, ::-1],
                                                        run[:, h, ::-1], -BIG, ALU.add, ALU.max)
                last.then_inc(scanned, 1)
                dve.wait_ge(scanned, k + 1)
            chain(nc.vector.tensor_copy(edge_vals[:, 0], seg_max[:, :, :, 0]))
            nc.vector.tensor_copy(edge_vals[:, 1], seg_max[:, :, :, P - 1]).then_inc(edges_out, 1)
            dve.wait_ge(edges_turned, 1)
            chain(nc.vector.tensor_tensor_scan(chains[0:hd, 0], c.stop_forward[0:hd, :], c.banks[5][0:hd, 0:STEPS],
                                               -BIG, ALU.add, ALU.max))
            chain(nc.vector.tensor_tensor_scan(chains[0:hd, 1, ::-1], c.stop_backward[0:hd, ::-1],
                                               c.banks[4][0:hd, 0:STEPS][:, ::-1], -BIG, ALU.add, ALU.max))
            chain(nc.vector.memset(carry[:], -BIG))
            chain(nc.vector.tensor_tensor(carry[0:hd, 0, 1:STEPS], chains[0:hd, 0, 0:STEPS - 1],
                                          c.new_dst[0:hd, 1:STEPS], ALU.add))
            nc.vector.tensor_tensor(carry[0:hd, 1, 0:STEPS - 1], chains[0:hd, 1, 1:STEPS],
                                    c.new_dst[0:hd, 1:STEPS], ALU.add).then_inc(carries, 1)
            dve.wait_ge(carries_turned, 1)
            chain(nc.vector.tensor_copy(carry_t[:].rearrange("p k b h -> p (k b h)"),
                                        c.banks[6][0:CH, 0:NCH * 2 * hd]))
            for b, off in ((0, c.not_first), (1, c.not_last)):
                for k in range(NCH):
                    for h in range(hd):
                        last = nc.vector.scalar_tensor_tensor(seg_max[:, k, h, :], off[:, k, :], carry_t[:, k, b, h:h + 1],
                                                              seg_max[:, k, h, :], ALU.add, ALU.max)
                chain(last)
            dve.sem_inc(maxima, 1)
            for h in range(hd):
                dve.wait_ge(back, h + 1)
                m = c.banks[h][:, 0:STEPS]
                nc.vector.tensor_tensor(c.shares[:, :, hd + h], m, c.is_end[:], ALU.mult)
                nc.vector.tensor_tensor(c.logits[:, h, :], c.logits[:, h, :], m, ALU.subtract).then_inc(args, 1)

        @block.scalar
        def _(act):
            for h in range(hd):
                act.wait_ge(args, h + 1)
                nc.scalar.activation(c.shares[:, :, h], c.logits[:, h, :], ACT.Exp)



def onehots_for_group(nc, c, onehot, g, q):
    return nc.vector.tensor_tensor(onehot[:, g], c.iota[:, 0:P].unsqueeze(1).to_broadcast([P, GROUP, P]),
                                   c.dst_local[:, bass.ds(q * GROUP, GROUP)].unsqueeze(2).to_broadcast([P, GROUP, P]),
                                   ALU.is_equal)


def load_windows(nc, c, engine, q):
    _, windows = nc.values_load_multi_w_load_instructions(
        c.window_i[0:1, bass.ds(q * GROUP, GROUP)], engines=[engine.engine], min_val=0, max_val=WINDOWS - 1,
        skip_runtime_bounds_check_because="build_steps clamps every window to 0..WINDOWS - 1")
    return windows


def pass_b(nc, c, heads):
    width = D + 2 * heads
    with ExitStack() as st:
        def sb(name, shape, dt=F32):
            return st.enter_context(nc.sbuf_tensor(unique(c, name), shape, dt))

        values = sb("values", [P, SUM_RING, GROUP, D])
        weighted = c.wide_a[:].rearrange("p w d -> p (w d)")[:, 0:SUM_RING * GROUP * width].rearrange(
            "p (g u d) -> p g u d", g=SUM_RING, u=GROUP)
        rest = sb("rest", [P, SUM_RING, GROUP, width])
        parts = [sb(f"part{k}", [P, SUM_RING, GROUP, width], BF16) for k in range(3)]
        onehot = sb("onehot", [P, SUM_RING, GROUP, P], BF16)
        zeros = sb("zeros", [P, P], BF16)
        wide_zeros = zeros[:].unsqueeze(1).to_broadcast([P, 4, P])
        values_in = [st.enter_context(semaphore(nc, c, f"values_in{g}")) for g in range(SUM_RING)]
        weighted_ready = st.enter_context(semaphore(nc, c, "weighted_ready"))
        shares_ready = st.enter_context(semaphore(nc, c, "shares_ready"))
        part0_ready = st.enter_context(semaphore(nc, c, "part0_ready"))
        rest_ready = st.enter_context(semaphore(nc, c, "rest_ready"))
        part1_ready = st.enter_context(semaphore(nc, c, "part1_ready"))
        part2_ready = st.enter_context(semaphore(nc, c, "part2_ready"))
        onehot_ready = st.enter_context(semaphore(nc, c, "onehot_ready"))
        summed = st.enter_context(semaphore(nc, c, "summed"))
        zeros_ready = st.enter_context(semaphore(nc, c, "zeros_ready"))
        issue = st.enter_context(semaphore(nc, c, "issue"))
        block = st.enter_context(nc.Block())
        value_sums = c.psum[:, 0:7, :].rearrange("p b d -> p (b d)").rearrange("p (w d) -> p w d", d=D)
        share_sums = c.psum[:, 7, :].rearrange("p (w h) -> p w h", h=2 * heads)

        @block.sync
        def _(sp):
            with sp.Fori(0, SUM_TRIPS) as t:
                for g in range(SUM_RING):
                    q = t * SUM_RING + g
                    sp.wait_ge(weighted_ready, q + 1)
                    sp.dma_start(values[:, g].rearrange("p u d -> p (u d)"),
                                 c.stash[:, bass.ds(q * (GROUP * D), GROUP * D)]).then_inc(values_in[g], 16)

        @block.gpsimd
        def _(pool):
            pool.sem_inc(part2_ready, SUM_RING)
            with pool.Fori(0, SUM_TRIPS) as t:
                for g in range(SUM_RING):
                    q = t * SUM_RING + g
                    pool.wait_ge(part1_ready, q + 1 + SUM_RING)
                    pool.sem_inc(issue, 1)
                    nc.gpsimd.tensor_tensor(parts[2][:, g], rest[:, g], parts[1][:, g], ALU.subtract).then_inc(part2_ready, 1)

        @block.vector
        def _(dve):
            nc.vector.memset(zeros[:], 0.0).then_inc(zeros_ready, 1)
            dve.sem_inc(weighted_ready, SUM_RING)
            dve.sem_inc(rest_ready, SUM_RING)
            dve.sem_inc(onehot_ready, SUM_RING)

            def weigh(t, g):
                q = t * SUM_RING + g
                dve.wait_ge(rest_ready, q + 1)
                dve.wait_ge(values_in[g], t * 16 + 16)
                nc.vector.tensor_tensor(
                    weighted[:, g, :, 0:D].rearrange("p u (h k) -> p u h k", h=heads),
                    values[:, g].rearrange("p u (h k) -> p u h k", h=heads),
                    c.shares[:, bass.ds(q * GROUP, GROUP), 0:heads].unsqueeze(3).to_broadcast([P, GROUP, heads, D // heads]),
                    ALU.mult).then_inc(weighted_ready, 1)

            with dve.Fori(0, SUM_TRIPS) as t:
                weigh(t, 0)
                for g in range(SUM_RING):
                    q = t * SUM_RING + g
                    if g + 1 < SUM_RING:
                        weigh(t, g + 1)
                    dve.wait_ge(summed, q + 1)
                    onehots_for_group(nc, c, onehot, g, q).then_inc(onehot_ready, 1)
                    dve.wait_ge(part0_ready, q + 1 + SUM_RING)
                    dve.wait_ge(part2_ready, q + 1)
                    nc.vector.tensor_tensor(rest[:, g], weighted[:, g], parts[0][:, g], ALU.subtract).then_inc(rest_ready, 1)

        @block.scalar
        def _(act):
            act.sem_inc(part0_ready, SUM_RING)
            act.sem_inc(part1_ready, SUM_RING)
            act.sem_inc(shares_ready, SUM_RING)

            def first_part(t, g):
                q = t * SUM_RING + g
                act.wait_ge(rest_ready, q + 1)
                act.sem_inc(issue, 1)
                nc.scalar.copy(weighted[:, g, :, D:width], c.shares[:, bass.ds(q * GROUP, GROUP), :]).then_inc(shares_ready, 1)
                act.wait_ge(weighted_ready, q + 1 + SUM_RING)
                act.wait_ge(shares_ready, q + 1 + SUM_RING)
                act.wait_ge(summed, q + 1)
                nc.scalar.copy(parts[0][:, g], weighted[:, g]).then_inc(part0_ready, 1)

            with act.Fori(0, SUM_TRIPS) as t:
                first_part(t, 0)
                for g in range(SUM_RING):
                    q = t * SUM_RING + g
                    if g + 1 < SUM_RING:
                        first_part(t, g + 1)
                    act.wait_ge(rest_ready, q + 1 + SUM_RING)
                    nc.scalar.copy(parts[1][:, g], rest[:, g]).then_inc(part1_ready, 1)
            act.wait_ge(summed, STEPS // GROUP + SUM_RING + 1)
            for w in range(0, WINDOWS, 4):
                n = min(4, WINDOWS - w)
                nc.scalar.copy(c.acc[:, w:w + n, 0:D], value_sums[:, w:w + n, :])
            nc.scalar.copy(c.acc[:, :, D:width], share_sums[:, 0:WINDOWS, :])

        @block.tensor
        def _(pe):
            pe.wait_ge(zeros_ready, 1)
            for k in range(8):
                last = nc.tensor.matmul(c.banks[k][:, :], zeros[:], wide_zeros, start=True, stop=False)
            pe.sem_inc(summed, SUM_RING)
            with pe.Fori(0, SUM_TRIPS) as t:
                for g in range(SUM_RING):
                    q = t * SUM_RING + g
                    js = load_windows(nc, c, pe, q)
                    pe.wait_ge(onehot_ready, q + 1 + SUM_RING)
                    pe.wait_ge(part2_ready, q + 1 + SUM_RING)
                    for u in range(GROUP):
                        for k in range(3):
                            nc.tensor.matmul(value_sums[:, js[u], :], onehot[:, g, u, :], parts[k][:, g, u, 0:D],
                                             start=False, stop=False)
                        for k in range(3):
                            last = nc.tensor.matmul(share_sums[:, js[u], :], onehot[:, g, u, :],
                                                    parts[k][:, g, u, D:width], start=False, stop=False)
                    last.then_inc(summed, 1)
            for k in range(8):
                last = nc.tensor.matmul(c.banks[k][:, :], zeros[:], wide_zeros, start=False, stop=True)
            last.then_inc(summed, 1)


def attention(nc, c, heads, pass_a):
    with nc.sbuf_tensor(unique(c, c.layer + "_logits"), [P, heads, STEPS], F32) as c.logits:
        pass_a()
        with nc.sbuf_tensor(unique(c, c.layer + "_shares"), [P, STEPS, 2 * heads], F32) as c.shares:
            edge_softmax(nc, c, heads)
            pass_b(nc, c, heads)



def gather_group(nc, rows, g, table, idx, sem):
    for u in range(GROUP):
        nc.gpsimd.indirect_dma_start(out=rows[:, g, u, :], out_offset=None, in_=table[:, :],
                                     in_offset=bass.IndirectOffsetOnAxis(ap=idx[:, g * GROUP + u:g * GROUP + u + 1], axis=0)
                                     ).then_inc(sem, 16)


def transposed_bank(c, g):
    return c.banks[g][:, 0:GROUP * P // 2].bitcast(BF16)


def pass_a_gat(nc, c, table, parts, weighted):
    with ExitStack() as st:
        def sb(name, shape, dt=F32):
            return st.enter_context(nc.sbuf_tensor(unique(c, name), shape, dt))

        rows = sb("rows", [P, RING, GROUP, GAT_ROW])
        dst_term = sb("dst_term", [P, RING, GROUP, H4])
        idx = sb("idx", [P, RING * GROUP], I32)
        onehot = sb("onehot", [P, RING, GROUP, P], BF16)
        onehot_t = sb("onehot_t", [P, RING, GROUP, P], BF16)
        gathered = [st.enter_context(semaphore(nc, c, f"gathered{g}")) for g in range(RING)]
        stored = [st.enter_context(semaphore(nc, c, f"stored{g}")) for g in range(RING)]
        idx_ready = st.enter_context(semaphore(nc, c, "idx_ready"))
        issue = st.enter_context(semaphore(nc, c, "issue"))
        onehot_ready = st.enter_context(semaphore(nc, c, "onehot_ready"))
        turned = st.enter_context(semaphore(nc, c, "onehot_turned"))
        copied = st.enter_context(semaphore(nc, c, "onehot_t_copied"))
        fetched = st.enter_context(semaphore(nc, c, "dst_term_ready"))
        dst_summed = st.enter_context(semaphore(nc, c, "dst_parts_summed"))
        logits_out = st.enter_context(semaphore(nc, c, "logits_written"))
        block = st.enter_context(nc.Block())

        @block.gpsimd
        def _(pool):
            with pool.Fori(0, TRIPS) as t:
                for g in range(RING):
                    q = t * RING + g
                    pool.wait_ge(idx_ready, q + 1)
                    pool.wait_ge(logits_out, q + 1)
                    pool.wait_ge(stored[g], t * 16 + 16)
                    pool.sem_inc(issue, 1)
                    gather_group(nc, rows, g, table, idx, gathered[g])

        @block.sync
        def _(sp):
            for g in range(RING):
                sp.sem_inc(stored[g], 16)
            with sp.Fori(0, TRIPS) as t:
                for g in range(RING):
                    q = t * RING + g
                    sp.wait_ge(gathered[g], t * (16 * GROUP) + 16 * GROUP)
                    sp.dma_start(c.stash[:, bass.ds(q * (GROUP * D), GROUP * D)].rearrange("p (u d) -> p u d", d=D),
                                 rows[:, g, :, 0:D]).then_inc(stored[g], 16)
            for g in range(RING):
                sp.wait_ge(stored[g], 16 * (TRIPS + 1))

        @block.vector
        def _(dve):
            dve.sem_inc(logits_out, RING)
            nc.vector.tensor_copy(idx[:], c.idx_src[:, 0:RING * GROUP]).then_inc(idx_ready, RING)
            with dve.Fori(0, TRIPS) as t:
                for g in range(RING):
                    q = t * RING + g
                    dve.wait_ge(turned, q + 1)
                    onehots_for_group(nc, c, onehot, g, q).then_inc(onehot_ready, 1)
                for g in range(RING):
                    q = t * RING + g
                    dve.wait_ge(gathered[g], t * (16 * GROUP) + 16 * GROUP)
                    nc.vector.tensor_scalar(idx[:, g * GROUP:(g + 1) * GROUP], c.idx_src[:, bass.ds((q + RING) * GROUP, GROUP)],
                                            0, None, ALU.add).then_inc(idx_ready, 1)
                    dve.wait_ge(fetched, q + 1 + RING)
                    nc.vector.tensor_reduce(dst_term[:, g], c.banks[2 + g][:, 0:GROUP * 3 * H4].rearrange("p (u k h) -> p u h k", k=3, h=H4),
                                            AX.X, ALU.add).then_inc(dst_summed, 1)
                for g in range(RING):
                    q = t * RING + g
                    dve.wait_ge(dst_summed, q + 1)
                    nc.vector.tensor_tensor(c.logits[:, :, bass.ds(q * GROUP, GROUP)],
                                            rows[:, g, :, D:D + H4].rearrange("p u h -> p h u"),
                                            dst_term[:, g].rearrange("p u h -> p h u"), ALU.add).then_inc(logits_out, 1)

        @block.tensor
        def _(pe):
            pe.sem_inc(turned, RING)
            pe.sem_inc(fetched, RING)
            with pe.Fori(0, TRIPS) as t:
                for g in range(RING):
                    q = t * RING + g
                    pe.wait_ge(onehot_ready, q + 1)
                    pe.wait_ge(copied, q + 1)
                    for u in range(GROUP):
                        last = nc.tensor.transpose(in_bank(transposed_bank(c, g), u, P), onehot[:, g, u, :], c.ident_b[:])
                    last.then_inc(turned, 1)
                for g in range(RING):
                    q = t * RING + g
                    js = load_windows(nc, c, pe, q)
                    pe.wait_ge(copied, q + 1 + RING)
                    pe.wait_ge(logits_out, q + 1)
                    for u in range(GROUP):
                        last = nc.tensor.matmul(in_bank(c.banks[2 + g], u, 3 * H4), onehot_t[:, g, u, :],
                                                parts[:, js[u], :], start=True, stop=True)
                    last.then_inc(fetched, 1)

        @block.scalar
        def _(act):
            act.sem_inc(copied, RING)
            with act.Fori(0, TRIPS) as t:
                for g in range(RING):
                    q = t * RING + g
                    act.wait_ge(turned, q + 1 + RING)
                    act.wait_ge(fetched, q + 1)
                    nc.scalar.copy(onehot_t[:, g].rearrange("p u e -> p (u e)"), transposed_bank(c, g)).then_inc(copied, 1)
    gat_logits(nc, c, weighted)


def pass_a_hgt(nc, c, table, parts):
    with ExitStack() as st:
        def sb(name, shape, dt=F32):
            return st.enter_context(nc.sbuf_tensor(unique(c, name), shape, dt))

        rows = sb("rows", [P, RING, GROUP, 2 * D])
        idx = sb("idx", [P, RING * GROUP], I32)
        onehot = sb("onehot", [P, RING, GROUP, P], BF16)
        onehot_t = sb("onehot_t", [P, RING, GROUP, P], BF16)
        product = sb("product", [P, RING, GROUP, D])
        scores = sb("scores", [P, RING, GROUP, H8])
        gathered = [st.enter_context(semaphore(nc, c, f"gathered{g}")) for g in range(RING)]
        stored = [st.enter_context(semaphore(nc, c, f"stored{g}")) for g in range(RING)]
        idx_ready = st.enter_context(semaphore(nc, c, "idx_ready"))
        issue = st.enter_context(semaphore(nc, c, "issue"))
        onehot_ready = st.enter_context(semaphore(nc, c, "onehot_ready"))
        turned = st.enter_context(semaphore(nc, c, "onehot_turned"))
        copied = st.enter_context(semaphore(nc, c, "onehot_t_copied"))
        fetched = st.enter_context(semaphore(nc, c, "queries_ready"))
        product_ready = st.enter_context(semaphore(nc, c, "product_ready"))
        scores_ready = st.enter_context(semaphore(nc, c, "scores_ready"))
        scores_out = st.enter_context(semaphore(nc, c, "scores_out"))
        block = st.enter_context(nc.Block())

        @block.gpsimd
        def _(pool):
            with pool.Fori(0, TRIPS) as t:
                for g in range(RING):
                    q = t * RING + g
                    pool.wait_ge(idx_ready, q + 1)
                    pool.wait_ge(product_ready, q + 1)
                    pool.wait_ge(stored[g], t * 16 + 16)
                    pool.sem_inc(issue, 1)
                    gather_group(nc, rows, g, table, idx, gathered[g])

        @block.sync
        def _(sp):
            for g in range(RING):
                sp.sem_inc(stored[g], 16)
            with sp.Fori(0, TRIPS) as t:
                for g in range(RING):
                    q = t * RING + g
                    sp.wait_ge(gathered[g], t * (16 * GROUP) + 16 * GROUP)
                    sp.dma_start(c.stash[:, bass.ds(q * (GROUP * D), GROUP * D)].rearrange("p (u d) -> p u d", d=D),
                                 rows[:, g, :, D:2 * D]).then_inc(stored[g], 16)
            for g in range(RING):
                sp.wait_ge(stored[g], 16 * (TRIPS + 1))

        @block.vector
        def _(dve):
            dve.sem_inc(product_ready, RING)
            dve.sem_inc(scores_out, RING)
            nc.vector.tensor_copy(idx[:], c.idx_typed[:, 0:RING * GROUP]).then_inc(idx_ready, RING)
            with dve.Fori(0, TRIPS) as t:
                for g in range(RING):
                    q = t * RING + g
                    dve.wait_ge(turned, q + 1)
                    onehots_for_group(nc, c, onehot, g, q).then_inc(onehot_ready, 1)
                for g in range(RING):
                    q = t * RING + g
                    dve.wait_ge(gathered[g], t * (16 * GROUP) + 16 * GROUP)
                    nc.vector.tensor_scalar(idx[:, g * GROUP:(g + 1) * GROUP], c.idx_typed[:, bass.ds((q + RING) * GROUP, GROUP)],
                                            0, None, ALU.add).then_inc(idx_ready, 1)
                    dve.wait_ge(fetched, q + 1 + RING)
                    nc.vector.tensor_tensor(product[:, g], rows[:, g, :, 0:D],
                                            c.banks[2 + g][:, :].rearrange("p (u d) -> p u d", d=D),
                                            ALU.mult).then_inc(product_ready, 1)
                for g in range(RING):
                    q = t * RING + g
                    dve.wait_ge(product_ready, q + 1 + RING)
                    dve.wait_ge(scores_out, q + 1)
                    nc.vector.tensor_reduce(scores[:, g].rearrange("p u h -> p (u h)"),
                                            product[:, g].rearrange("p u (h k) -> p (u h) k", h=H8),
                                            AX.X, ALU.add).then_inc(scores_ready, 1)
                for g in range(RING):
                    q = t * RING + g
                    dve.wait_ge(scores_ready, q + 1)
                    nc.vector.tensor_scalar(c.logits[:, :, bass.ds(q * GROUP, GROUP)], scores[:, g].rearrange("p u h -> p h u"),
                                            0.0, None, ALU.add).then_inc(scores_out, 1)

        @block.tensor
        def _(pe):
            pe.sem_inc(turned, RING)
            pe.sem_inc(fetched, RING)
            with pe.Fori(0, TRIPS) as t:
                for g in range(RING):
                    q = t * RING + g
                    pe.wait_ge(onehot_ready, q + 1)
                    pe.wait_ge(copied, q + 1)
                    for u in range(GROUP):
                        last = nc.tensor.transpose(in_bank(transposed_bank(c, g), u, P), onehot[:, g, u, :], c.ident_b[:])
                    last.then_inc(turned, 1)
                for g in range(RING):
                    q = t * RING + g
                    js = load_windows(nc, c, pe, q)
                    pe.wait_ge(copied, q + 1 + RING)
                    pe.wait_ge(product_ready, q + 1)
                    for u in range(GROUP):
                        for k in range(3):
                            last = nc.tensor.matmul(in_bank(c.banks[2 + g], u, D), onehot_t[:, g, u, :],
                                                    parts[k][:, js[u], :], start=k == 0, stop=k == 2)
                    last.then_inc(fetched, 1)

        @block.scalar
        def _(act):
            act.sem_inc(copied, RING)
            with act.Fori(0, TRIPS) as t:
                for g in range(RING):
                    q = t * RING + g
                    act.wait_ge(turned, q + 1 + RING)
                    act.wait_ge(fetched, q + 1)
                    nc.scalar.copy(onehot_t[:, g].rearrange("p u e -> p (u e)"), transposed_bank(c, g)).then_inc(copied, 1)


def pass_a_relational(nc, c, table, z_parts, dst_parts, y_w, rel_count):
    with ExitStack() as st:
        def sb(name, shape, dt=F32):
            return st.enter_context(nc.sbuf_tensor(unique(c, name), shape, dt))

        rows = sb("rows", [P, RING, GROUP, 2 * D])
        values = sb("values", [P, RING, GROUP, D])
        idx = sb("idx", [P, RING * GROUP], I32)
        onehot = sb("onehot", [P, RING, GROUP, P], BF16)
        onehot_t = sb("onehot_t", [P, RING, GROUP, P], BF16)
        rel_hot = sb("rel_hot", [P, RING, GROUP, RELS], BF16)
        rel_hot_t = sb("rel_hot_t", [HALF_RELS, RING, GROUP, 2, P], BF16)
        leaky = sb("leaky", [P, RING, 2, GROUP, P])
        gathered = [st.enter_context(semaphore(nc, c, f"gathered{g}")) for g in range(RING)]
        stored = [st.enter_context(semaphore(nc, c, f"stored{g}")) for g in range(RING)]
        idx_ready = st.enter_context(semaphore(nc, c, "idx_ready"))
        issue = st.enter_context(semaphore(nc, c, "issue"))
        onehot_ready = st.enter_context(semaphore(nc, c, "onehot_ready"))
        turned = st.enter_context(semaphore(nc, c, "onehot_turned"))
        copied = st.enter_context(semaphore(nc, c, "onehot_t_copied"))
        rel_turned = st.enter_context(semaphore(nc, c, "rel_hot_turned"))
        rel_copied = st.enter_context(semaphore(nc, c, "rel_hot_t_copied"))
        pre_ready = st.enter_context(semaphore(nc, c, "pre_ready"))
        leaky_ready = st.enter_context(semaphore(nc, c, "leaky_ready"))
        rel_values = st.enter_context(semaphore(nc, c, "rel_values"))
        values_ready = st.enter_context(semaphore(nc, c, "values_ready"))
        counted = st.enter_context(semaphore(nc, c, "rel_counted"))
        added = st.enter_context(semaphore(nc, c, "counts_added"))
        scored = st.enter_context(semaphore(nc, c, "scored"))
        logits_out = st.enter_context(semaphore(nc, c, "logits_written"))
        cleared = st.enter_context(semaphore(nc, c, "counts_cleared"))
        block = st.enter_context(nc.Block())
        turned_bank = transposed_bank(c, 0)
        rel_bank = c.banks[1][0:HALF_RELS, :].bitcast(BF16)
        pre_bank, value_bank, logit_bank = c.banks[2], c.banks[3], c.banks[6]
        count_banks = c.banks[4:6]

        @block.gpsimd
        def _(pool):
            with pool.Fori(0, TRIPS) as t:
                for g in range(RING):
                    q = t * RING + g
                    pool.wait_ge(idx_ready, q + 1)
                    pool.wait_ge(values_ready, q + 1)
                    pool.wait_ge(pre_ready, q + 1)
                    pool.sem_inc(issue, 1)
                    gather_group(nc, rows, g, table, idx, gathered[g])

        @block.sync
        def _(sp):
            for g in range(RING):
                sp.sem_inc(stored[g], 16)
            with sp.Fori(0, TRIPS) as t:
                for g in range(RING):
                    q = t * RING + g
                    sp.wait_ge(values_ready, q + 1 + RING)
                    sp.dma_start(c.stash[:, bass.ds(q * (GROUP * D), GROUP * D)],
                                 values[:, g].rearrange("p u d -> p (u d)")).then_inc(stored[g], 16)
            for g in range(RING):
                sp.wait_ge(stored[g], 16 * (TRIPS + 1))

        @block.vector
        def _(dve):
            nc.vector.memset(rel_count[:], 0.0).then_inc(cleared, 1)
            dve.sem_inc(values_ready, RING)
            dve.sem_inc(added, GROUP)
            dve.sem_inc(logits_out, 1)
            dve.wait_ge(cleared, 1)
            nc.vector.tensor_copy(idx[:], c.idx_src[:, 0:RING * GROUP]).then_inc(idx_ready, RING)

            def hots(t, g):
                q = t * RING + g
                dve.wait_ge(counted, 2 * q + 2)
                nc.vector.tensor_tensor(rel_hot[:, g], c.iota[:, 0:RELS].unsqueeze(1).to_broadcast([P, GROUP, RELS]),
                                        c.relation[:, bass.ds(q * GROUP, GROUP)].unsqueeze(2).to_broadcast([P, GROUP, RELS]),
                                        ALU.is_equal)
                onehots_for_group(nc, c, onehot, g, q).then_inc(onehot_ready, 1)

            with dve.Fori(0, TRIPS) as t:
                for g in range(RING):
                    hots(t, g)
                for g in range(RING):
                    q = t * RING + g
                    js = load_windows(nc, c, dve, q)
                    dve.wait_ge(gathered[g], t * (16 * GROUP) + 16 * GROUP)
                    nc.vector.tensor_scalar(idx[:, g * GROUP:(g + 1) * GROUP], c.idx_src[:, bass.ds((q + RING) * GROUP, GROUP)],
                                            0, None, ALU.add).then_inc(idx_ready, 1)
                    dve.wait_ge(rel_values, q + 1 + RING)
                    dve.wait_ge(stored[g], t * 16 + 16)
                    nc.vector.tensor_tensor(values[:, g], rows[:, g, :, D:2 * D],
                                            value_bank[:, :].rearrange("p (u d) -> p u d", d=D),
                                            ALU.add).then_inc(values_ready, 1)
                    for u in range(GROUP):
                        dve.wait_ge(counted, 2 * q + u // 2 + 1 + 2 * RING)
                        dve.wait_ge(added, q * GROUP + u + GROUP)
                        nc.vector.tensor_tensor(rel_count[:, js[u], :], rel_count[:, js[u], :],
                                                in_bank(count_banks[u // 2], u % 2, RELS), ALU.add).then_inc(added, 1)
                    dve.wait_ge(scored, q + 1 + RING)
                    nc.vector.tensor_scalar(c.logits[:, :, bass.ds(q * GROUP, GROUP)],
                                            logit_bank[:, 0:GROUP * H8].rearrange("p (u h) -> p h u", h=H8), 0.0, None,
                                            ALU.add).then_inc(logits_out, 1)

        @block.tensor
        def _(pe):
            pe.sem_inc(pre_ready, RING)
            pe.sem_inc(rel_values, RING)
            pe.sem_inc(counted, 2 * RING)
            pe.sem_inc(scored, RING)
            with pe.Fori(0, TRIPS) as t:
                for g in range(RING):
                    q = t * RING + g
                    js = load_windows(nc, c, pe, q)
                    pe.wait_ge(onehot_ready, q + 1)
                    pe.wait_ge(copied, q + 1)
                    for u in range(GROUP):
                        last = nc.tensor.transpose(in_bank(turned_bank, u, P), onehot[:, g, u, :], c.ident_b[:])
                    last.then_inc(turned, 1)
                    pe.wait_ge(rel_copied, q + 1)
                    for u in range(GROUP):
                        for b in range(2):
                            last = nc.tensor.transpose(in_bank(rel_bank, 2 * u + b, P),
                                                       rel_hot[:, g, u, b * HALF_RELS:(b + 1) * HALF_RELS], c.ident_b[:])
                    last.then_inc(rel_turned, 1)
                    for u in range(GROUP):
                        if u % 2 == 0:
                            pe.wait_ge(added, q * GROUP + u + 2)
                        last = nc.tensor.matmul(in_bank(count_banks[u // 2], u % 2, RELS), onehot[:, g, u, :],
                                                rel_hot[:, g, u, :], start=True, stop=True)
                        if u % 2 == 1:
                            last.then_inc(counted, 1)
                    pe.wait_ge(gathered[g], t * (16 * GROUP) + 16 * GROUP)
                    pe.wait_ge(leaky_ready, q + 1)
                    for u in range(GROUP):
                        pre = in_bank(pre_bank, u, P)
                        nc.tensor.matmul(pre, rows[:, g, u, 0:D], c.ident[:], start=True, stop=False)
                        if u == 0:
                            pe.wait_ge(rel_copied, q + 2)
                        for b in range(2):
                            for k in range(3):
                                nc.tensor.matmul(pre, z_parts[k][:, b, 0:D], rel_hot_t[:, g, u, b, :], start=False, stop=False)
                                if u == 0 and b == 1 and k == 2:
                                    pe.wait_ge(copied, q + 2)
                                    pe.sem_inc(issue, 1)
                        for k in range(3):
                            last = nc.tensor.matmul(pre, dst_parts[k][:, js[u], :], onehot_t[:, g, u, :],
                                                    start=False, stop=k == 2)
                    last.then_inc(pre_ready, 1)
                    pe.wait_ge(values_ready, q + 2)
                    for u in range(GROUP):
                        for b in range(2):
                            for k in range(3):
                                last = nc.tensor.matmul(in_bank(value_bank, u, D), rel_hot_t[:, g, u, b, :],
                                                        z_parts[k][:, b, D:2 * D], start=b + k == 0, stop=b + k == 3)
                    last.then_inc(rel_values, 1)
                    pe.wait_ge(leaky_ready, q + 2)
                    pe.wait_ge(logits_out, q + 1)
                    for u in range(GROUP):
                        for k in range(2):
                            last = nc.tensor.matmul(in_bank(logit_bank, u, H8), leaky[:, g, k, u, :], y_w,
                                                    start=k == 0, stop=k == 1)
                    last.then_inc(scored, 1)

        @block.scalar
        def _(act):
            act.sem_inc(copied, 1)
            act.sem_inc(rel_copied, 1)
            act.sem_inc(leaky_ready, 1)
            with act.Fori(0, TRIPS) as t:
                for g in range(RING):
                    q = t * RING + g
                    act.wait_ge(turned, q + 1)
                    act.wait_ge(pre_ready, q + 1)
                    nc.scalar.copy(onehot_t[:, g].rearrange("p u e -> p (u e)"), turned_bank).then_inc(copied, 1)
                    act.wait_ge(rel_turned, q + 1)
                    act.wait_ge(rel_values, q + 1)
                    nc.scalar.copy(rel_hot_t[:, g].rearrange("p u b e -> p (u b e)"), rel_bank).then_inc(rel_copied, 1)
                    act.wait_ge(pre_ready, q + 1 + RING)
                    act.wait_ge(scored, q + 1)
                    nc.scalar.activation(leaky[:, g, 0].rearrange("p u e -> p (u e)"), pre_bank[:, :], ACT.Copy, scale=SLOPE)
                    nc.scalar.activation(leaky[:, g, 1].rearrange("p u e -> p (u e)"), pre_bank[:, :], ACT.Relu,
                                         scale=1.0 - SLOPE).then_inc(leaky_ready, 1)



def relation_sums(nc, c, rel_count, z_rows, to):
    with nc.sbuf_tensor(unique(c, "count_t"), [HALF_RELS, 2, 2, P], F32) as count_t, \
            semaphore(nc, c, "counts_turned") as turned, semaphore(nc, c, "counts_copied") as copied, \
            semaphore(nc, c, "window_ready") as window_ready, semaphore(nc, c, "window_taken") as window_taken, \
            nc.Block() as block:

        def turned_bank(w):
            return c.banks[w % 2][0:HALF_RELS, 0:2 * P]

        @block.tensor
        def _(pe):
            def turn(w):
                if w >= 2:
                    pe.wait_ge(copied, w - 1)
                for b in range(2):
                    last = nc.tensor.transpose(turned_bank(w)[:, b * P:(b + 1) * P],
                                               rel_count[:, w, b * HALF_RELS:(b + 1) * HALF_RELS], c.ident[:])
                last.then_inc(turned, 1)

            turn(0)
            for w in range(WINDOWS):
                if w + 1 < WINDOWS:
                    turn(w + 1)
                pe.wait_ge(copied, w + 1)
                if w >= 4:
                    pe.wait_ge(window_taken, w - 3)
                for b in range(2):
                    last = nc.tensor.matmul(c.banks[4 + w % 4][:, 0:2 * D], count_t[:, w % 2, b, :], z_rows[:, b, :],
                                            start=b == 0, stop=b == 1)
                last.then_inc(window_ready, 1)

        @block.scalar
        def _(act):
            for w in range(WINDOWS):
                act.wait_ge(turned, w + 1)
                if w >= 2:
                    act.wait_ge(window_ready, w - 1)
                nc.scalar.copy(count_t[:, w % 2].rearrange("p b n -> p (b n)"), turned_bank(w)).then_inc(copied, 1)

        @block.vector
        def _(dve):
            for w in range(WINDOWS):
                dve.wait_ge(window_ready, w + 1)
                nc.vector.tensor_copy(to[:, w, :], c.banks[4 + w % 4][:, 0:2 * D]).then_inc(window_taken, 1)


def layer0(nc, c, a):
    wide, per_head = [P, WINDOWS, D], [P, WINDOWS, H8, D // H8]
    normalise(nc, c)
    with ExitStack() as st:
        def sb(name, shape, dt=F32):
            return st.enter_context(nc.sbuf_tensor(unique(c, name), shape, dt))

        rel_count = sb("rel_count", [P, WINDOWS, RELS])
        z_rows = sb("z_rows", [HALF_RELS, 2, 2 * D])
        y_w = sb("y_w", [D, H8])
        c.acc = sb("acc", [P, WINDOWS, D + 2 * H8])
        with ExitStack() as inner:
            def sbi(name, shape, dt=F32):
                return inner.enter_context(nc.sbuf_tensor(unique(c, name), shape, dt))
            parts = [sbi(f"dst_part{k}", [P, WINDOWS, D], BF16) for k in range(3)]
            z_parts = [sbi(f"z_part{k}", [HALF_RELS, 2, 2 * D], BF16) for k in range(3)]
            with ExitStack() as pre:
                def sbp(name, shape, dt=F32):
                    return pre.enter_context(nc.sbuf_tensor(unique(c, name), shape, dt))
                c.h_t = sbp("h_t", [D, N_PAD])
                w_node = sbp("w_node", [D, 3, D])
                w_rel = sbp("w_rel", [D, 2, D])
                z = sbp("z", [RELS // 2, 2, D])
                z_t = sbp("z_t", [D, RELS])
                proj = sbp("proj", [P, WINDOWS, 3 * D])
                with semaphore(nc, c, "weights_in") as weights_in, nc.Block() as block:
                    @block.sync
                    def _(sp):
                        for to, source in ((w_node[:, 0], a["L0_gnn_P_w"][D:2 * D, :]), (w_node[:, 1], a["L0_gnn_Wc_w"][0:D, :]),
                                           (w_node[:, 2], a["L0_gnn_P_w"][0:D, :]), (w_rel[:, 0], a["L0_gnn_P_w"][2 * D:3 * D, :]),
                                           (w_rel[:, 1], a["L0_gnn_Wc_w"][D:2 * D, :]), (y_w[:], a["L0_gnn_y_w"]),
                                           (z[:], a["L0_gnn_z"].rearrange("(b r) d -> r b d", b=2))):
                            sp.dma_start(to, source).then_inc(weights_in, 16)
                        sp.wait_ge(weights_in, 16 * 7)
                transpose_windows(nc, c, c.h, c.h_t)
                project(nc, c, w_node[:].rearrange("p k d -> p (k d)"), 3 * D, proj)
                with semaphore(nc, c, "z_turned") as z_turned, semaphore(nc, c, "z_t_ready") as z_t_ready, \
                        semaphore(nc, c, "z_projected") as z_projected, semaphore(nc, c, "z_rows_ready") as z_rows_ready, \
                        semaphore(nc, c, "vec_done") as vec_done, semaphore(nc, c, "tables_out") as tables_out, nc.Block() as block:
                    @block.tensor
                    def _(pe):
                        for b in range(2):
                            last = nc.tensor.transpose(c.banks[0][:, b * 100:(b + 1) * 100], z[:, b, :], c.ident[0:100, 0:100])
                        last.then_inc(z_turned, 1)
                        pe.wait_ge(z_t_ready, 1)
                        for b in range(2):
                            last = nc.tensor.matmul(c.banks[1 + b][0:100, 0:2 * D], z_t[:, b * 100:(b + 1) * 100],
                                                    w_rel[:].rearrange("p k d -> p (k d)"), start=True, stop=True)
                        last.then_inc(z_projected, 1)

                    @block.scalar
                    def _(act):
                        act.wait_ge(z_turned, 1)
                        nc.scalar.copy(z_t[:], c.banks[0][:, 0:RELS]).then_inc(z_t_ready, 1)
                        act.wait_ge(z_projected, 1)
                        for b in range(2):
                            nc.scalar.copy(z_rows[:, b, 0:2 * D], c.banks[1 + b][0:100, 0:2 * D]).then_inc(z_rows_ready, 1)

                    @block.vector
                    def _(dve):
                        chain = Chain(dve, vec_done)
                        split_three(nc, chain, proj[:, :, 2 * D:3 * D], [p[:] for p in parts], c.wide_a[:])
                        dve.wait_ge(z_rows_ready, 2)
                        split_three(nc, chain, z_rows[:], [p[:] for p in z_parts],
                                    c.wide_a[0:HALF_RELS, 0:4, :].rearrange("p (b k) d -> p b (k d)", b=2))

                    @block.sync
                    def _(sp):
                        for k, (table, lo, hi) in enumerate(((c.rel_src_table, 0, 2 * D), (c.rel_dst_table, 2 * D, 3 * D))):
                            sp.dma_start(table.rearrange("(w n) d -> n w d", n=P), proj[:, :, lo:hi]).then_inc(tables_out, 16)
                        sp.wait_ge(tables_out, 32)
            attention(nc, c, H8, lambda: pass_a_relational(nc, c, c.rel_src_table, z_parts, parts, y_w[:], rel_count))
        with ExitStack() as fin:
            def sbf(name, shape, dt=F32):
                return fin.enter_context(nc.sbuf_tensor(unique(c, name), shape, dt))
            c.h_t = sbf("pre_self_t", [D, N_PAD])
            src_terms = sbf("src_terms", [P, WINDOWS, 2 * D])
            dst_term = sbf("dst_term", [P, WINDOWS, D])
            resid = sbf("resid", [P, 1])
            small = [sbf(f"small{k}", [P, WINDOWS, H8]) for k in range(5)]
            deg = sbf("deg", [P, WINDOWS, 2])
            rel_terms = sbf("rel_terms", [P, WINDOWS, 2 * D])
            relation_sums(nc, c, rel_count, z_rows, rel_terms)
            with semaphore(nc, c, "terms_in") as terms_in, semaphore(nc, c, "vec_done") as vec_done, nc.Block() as block:
                @block.sync
                def _(sp):
                    sp.dma_start(src_terms[:], c.rel_src_table.rearrange("(w n) d -> n w d", n=P)).then_inc(terms_in, 16)
                    sp.dma_start(dst_term[:], c.rel_dst_table.rearrange("(w n) d -> n w d", n=P)).then_inc(terms_in, 16)
                    sp.dma_start(resid[:], a["L0_gnn_residual_weight"].partition_broadcast(P)).then_inc(terms_in, 16)
                    sp.wait_ge(terms_in, 48)

                @block.vector
                def _(dve):
                    chain = Chain(dve, vec_done)
                    chain(nc.vector.tensor_reduce(c.mean[:], rel_count[:], AX.X, ALU.add))
                    chain(nc.vector.tensor_single_scalar(deg[:, :, 1], c.mean[:], 0.0, ALU.is_gt))
                    chain(nc.vector.tensor_single_scalar(c.mean[:], c.mean[:], 1.0, ALU.max))
                    chain(nc.vector.reciprocal(deg[:, :, 0], c.mean[:]))
                    chain(nc.vector.tensor_tensor(rel_terms[:, :, 0:2 * D], rel_terms[:, :, 0:2 * D],
                                                  deg[:, :, 0:1].to_broadcast([P, WINDOWS, 2 * D]), ALU.mult))
                    dve.wait_ge(terms_in, 48)
                    chain(nc.vector.tensor_tensor(dst_term[:], dst_term[:], src_terms[:, :, 0:D], ALU.add))
                    chain(nc.vector.tensor_tensor(dst_term[:], dst_term[:], rel_terms[:, :, 0:D], ALU.add))
                    chain(nc.vector.scalar_tensor_tensor(dst_term[:], dst_term[:], SLOPE, dst_term[:], ALU.mult, ALU.max))
                    chain(nc.vector.tensor_tensor(src_terms[:, :, D:2 * D], src_terms[:, :, D:2 * D],
                                                  rel_terms[:, :, D:2 * D], ALU.add))
            transpose_windows(nc, c, dst_term, c.h_t)
            with semaphore(nc, c, "self_scored") as self_scored, semaphore(nc, c, "args_ready") as args_ready, \
                    semaphore(nc, c, "exps_ready") as exps_ready, semaphore(nc, c, "vec_done") as vec_done, nc.Block() as block:
                m_e, self_e, top, f, g = small
                scores = c.banks[0][:, 0:WINDOWS * H8].rearrange("p (w h) -> p w h", h=H8)

                @block.tensor
                def _(pe):
                    for w in range(WINDOWS):
                        last = nc.tensor.matmul(c.banks[0][:, w * H8:(w + 1) * H8], c.h_t[:, w * P:(w + 1) * P], y_w[:],
                                                start=True, stop=True)
                    last.then_inc(self_scored, 1)

                @block.scalar
                def _(act):
                    act.wait_ge(args_ready, 1)
                    nc.scalar.activation(f[:], f[:], ACT.Exp)
                    nc.scalar.activation(g[:], g[:], ACT.Exp).then_inc(exps_ready, 1)

                @block.vector
                def _(dve):
                    chain = Chain(dve, vec_done)
                    chain(nc.vector.tensor_scalar(m_e[:], deg[:, :, 1:2].to_broadcast([P, WINDOWS, H8]), 1.0, BIG,
                                                  ALU.subtract, ALU.mult))
                    chain(nc.vector.tensor_tensor(m_e[:], m_e[:], c.acc[:, :, D + H8:D + 2 * H8], ALU.add))
                    dve.wait_ge(self_scored, 1)
                    chain(nc.vector.tensor_copy(self_e[:], scores))
                    chain(nc.vector.tensor_tensor(top[:], m_e[:], self_e[:], ALU.max))
                    chain(nc.vector.tensor_tensor(f[:], m_e[:], top[:], ALU.subtract))
                    nc.vector.tensor_tensor(g[:], self_e[:], top[:], ALU.subtract).then_inc(args_ready, 1)
                    dve.wait_ge(exps_ready, 1)
                    chain(nc.vector.tensor_tensor(top[:], c.acc[:, :, D:D + H8], f[:], ALU.mult))
                    chain(nc.vector.tensor_tensor(top[:], top[:], g[:], ALU.add))
                    chain(nc.vector.reciprocal(top[:], top[:]))
                    chain(nc.vector.tensor_tensor(f[:], f[:], top[:], ALU.mult))
                    chain(nc.vector.tensor_tensor(g[:], g[:], top[:], ALU.mult))
                    for v, by in ((c.acc[:, :, 0:D], f), (src_terms[:, :, D:2 * D], g)):
                        v4 = v.rearrange("p w (h k) -> p w h k", h=H8)
                        for w in range(WINDOWS):
                            last = nc.vector.tensor_tensor(v4[:, w], v4[:, w],
                                                           by[:, w, :].unsqueeze(2).to_broadcast([P, H8, D // H8]), ALU.mult)
                        chain(last)
                    out = c.wide_a
                    chain(nc.vector.tensor_tensor(out[:], c.acc[:, :, 0:D], src_terms[:, :, D:2 * D], ALU.add))
                    chain(nc.vector.scalar_tensor_tensor(out[:], c.h[:], resid[:], out[:], ALU.mult, ALU.add))
                    chain(nc.vector.scalar_tensor_tensor(out[:], out[:], SLOPE, out[:], ALU.mult, ALU.max))
                    chain(nc.vector.tensor_tensor(out[:], out[:], c.h[:], ALU.subtract))
                    chain(nc.vector.tensor_tensor(out[:], out[:], deg[:, :, 1:2].to_broadcast(wide), ALU.mult))
                    chain(nc.vector.tensor_tensor(out[:], out[:], c.h[:], ALU.add))
                    chain(nc.vector.tensor_tensor(c.x[:], c.x[:], out[:], ALU.add))



def gat_node_phase(nc, c, weights, transpose_weights, att_src, att_dst, rows, a_dst, parts):
    with ExitStack() as st:
        w_in = st.enter_context(nc.sbuf_tensor(unique(c, "w_in"), [D, D], F32))
        w_use = st.enter_context(nc.sbuf_tensor(unique(c, "w_use"), [D, D], F32))
        att = st.enter_context(nc.sbuf_tensor(unique(c, "att"), [P, 2, D], F32))
        normalise(nc, c)
        with semaphore(nc, c, "weights_in") as weights_in, semaphore(nc, c, "w_turned") as w_turned, \
                semaphore(nc, c, "w_done") as w_done, nc.Block() as block:
            @block.sync
            def _(sp):
                sp.dma_start(w_in[:], weights).then_inc(weights_in, 16)
                sp.dma_start(att[:, 0, :], att_src.partition_broadcast(P)).then_inc(weights_in, 16)
                sp.dma_start(att[:, 1, :], att_dst.partition_broadcast(P)).then_inc(weights_in, 16)
                sp.wait_ge(weights_in, 48)

            @block.tensor
            def _(pe):
                pe.wait_ge(weights_in, 48)
                nc.tensor.transpose(c.banks[0][:, 0:D], w_in[:], c.ident[:]).then_inc(w_turned, 1)

            @block.vector
            def _(dve):
                dve.wait_ge(w_turned, 1)
                nc.vector.tensor_copy(w_use[:], c.banks[0][:, 0:D] if transpose_weights else w_in[:])
        transpose_windows(nc, c, c.h, c.h_t)
        project(nc, c, w_use[:], D, rows)
        with semaphore(nc, c, "vec_done") as vec_done, semaphore(nc, c, "rows_ready") as rows_ready, \
                semaphore(nc, c, "table_out") as table_out, nc.Block() as block:
            @block.vector
            def _(dve):
                chain = Chain(dve, vec_done)
                for k, to in ((0, rows[:, :, D:D + H4]), (1, a_dst[:])):
                    chain(nc.vector.tensor_tensor(c.wide_a[:], rows[:, :, 0:D],
                                                  att[:, k:k + 1, :].to_broadcast([P, WINDOWS, D]), ALU.mult))
                    chain(nc.vector.tensor_reduce(to, c.wide_a[:].rearrange("p w (h k) -> p w h k", h=H4), AX.X, ALU.add))
                    if k == 0:
                        dve.sem_inc(rows_ready, 1)
                split_three(nc, chain, a_dst[:], [parts[:, :, k * H4:(k + 1) * H4] for k in range(3)], c.wide_a[:, :, 0:H4])

            @block.sync
            def _(sp):
                sp.wait_ge(rows_ready, 1)
                sp.dma_start(c.gat_table.rearrange("(w n) d -> n w d", n=P), rows[:]).then_inc(table_out, 16)
                sp.wait_ge(table_out, 16)


def gat_logits(nc, c, weighted):
    with semaphore(nc, c, "vec_done") as vec_done, nc.Block() as block:
        @block.vector
        def _(dve):
            chain = Chain(dve, vec_done)
            lg = c.logits[:, 0:H4, :]
            chain(nc.vector.scalar_tensor_tensor(lg, lg, SLOPE, lg, ALU.mult, ALU.max))
            if weighted:
                chain(nc.vector.tensor_tensor(lg, lg, c.weight[:].unsqueeze(1).to_broadcast([P, H4, STEPS]), ALU.mult))


def scale_heads(nc, chain, v, by, heads):
    v4 = v.rearrange("p w (h k) -> p w h k", h=heads)
    for w in range(WINDOWS):
        last = nc.vector.tensor_tensor(v4[:, w], v4[:, w],
                                       by[:, w, :].unsqueeze(2).to_broadcast([P, heads, D // heads]), ALU.mult)
    chain(last)


def layer1(nc, c, a):
    wide = [P, WINDOWS, D]
    with ExitStack() as st:
        def sb(name, shape, dt=F32):
            return st.enter_context(nc.sbuf_tensor(unique(c, name), shape, dt))
        rows = sb("gat_rows", [P, WINDOWS, GAT_ROW])
        a_dst = sb("a_dst", [P, WINDOWS, H4])
        parts = sb("dst_parts", [P, WINDOWS, 3 * H4], BF16)
        small = [sb(f"small{k}", [P, WINDOWS, H4]) for k in range(5)]
        vecs = sb("vecs", [P, 3, D])
        stat = sb("stat", [P, 2, D])
        c.h_t = sb("h_t", [D, N_PAD])
        c.acc = sb("acc", [P, WINDOWS, D + 2 * H4])
        gat_node_phase(nc, c, a["L1_gnn_W"], False, a["L1_gnn_att_src"].rearrange("h k -> (h k)"),
                       a["L1_gnn_att_dst"].rearrange("h k -> (h k)"), rows, a_dst, parts)
        attention(nc, c, H4, lambda: pass_a_gat(nc, c, c.gat_table, parts, weighted=False))
        with semaphore(nc, c, "vecs_in") as vecs_in, semaphore(nc, c, "args_ready") as args_ready, \
                semaphore(nc, c, "exps_ready") as exps_ready, semaphore(nc, c, "vec_done") as vec_done, \
                semaphore(nc, c, "sums_wanted") as sums_wanted, semaphore(nc, c, "sums_ready") as sums_ready, \
                semaphore(nc, c, "var_ready") as var_ready, semaphore(nc, c, "dev_ready") as dev_ready, nc.Block() as block:
            m_e, self_e, top, f, g = small
            out = c.wide_a

            @block.sync
            def _(sp):
                for k, v in enumerate((a["L1_gnn_bias"], a["L1_gnn_gamma"], a["L1_gnn_beta"])):
                    sp.dma_start(vecs[:, k, :], v.partition_broadcast(P)).then_inc(vecs_in, 16)
                sp.wait_ge(vecs_in, 48)

            @block.tensor
            def _(pe):
                for k, source in enumerate((out, c.h)):
                    pe.wait_ge(sums_wanted, k + 1)
                    for w in range(WINDOWS):
                        rows_in = P if w < WINDOWS - 1 else LAST_NODES
                        last = nc.tensor.matmul(c.banks[k][:, 0:D], c.ones[0:rows_in, :], source[0:rows_in, w, :],
                                                start=w == 0, stop=w == WINDOWS - 1)
                    last.then_inc(sums_ready, 1)

            @block.scalar
            def _(act):
                act.wait_ge(args_ready, 1)
                nc.scalar.activation(f[:], f[:], ACT.Exp)
                nc.scalar.activation(g[:], g[:], ACT.Exp).then_inc(exps_ready, 1)
                act.wait_ge(var_ready, 1)
                nc.scalar.activation(stat[:, 1, :], stat[:, 1, :], ACT.Sqrt).then_inc(dev_ready, 1)
                act.wait_ge(args_ready, 2)
                nc.scalar.activation(c.h[:], c.h[:], ACT.Exp).then_inc(exps_ready, 1)

            @block.vector
            def _(dve):
                chain = Chain(dve, vec_done)
                chain(nc.vector.tensor_tensor(self_e[:], a_dst[:], rows[:, :, D:D + H4], ALU.add))
                chain(nc.vector.scalar_tensor_tensor(self_e[:], self_e[:], SLOPE, self_e[:], ALU.mult, ALU.max))
                chain(nc.vector.tensor_scalar(m_e[:], c.acc[:, :, D:D + H4], 0.5, -BIG, ALU.is_lt, ALU.mult))
                chain(nc.vector.tensor_tensor(m_e[:], m_e[:], c.acc[:, :, D + H4:D + 2 * H4], ALU.add))
                chain(nc.vector.tensor_tensor(top[:], m_e[:], self_e[:], ALU.max))
                chain(nc.vector.tensor_tensor(f[:], m_e[:], top[:], ALU.subtract))
                nc.vector.tensor_tensor(g[:], self_e[:], top[:], ALU.subtract).then_inc(args_ready, 1)
                dve.wait_ge(exps_ready, 1)
                chain(nc.vector.tensor_tensor(top[:], c.acc[:, :, D:D + H4], f[:], ALU.mult))
                chain(nc.vector.tensor_tensor(top[:], top[:], g[:], ALU.add))
                chain(nc.vector.tensor_single_scalar(top[:], top[:], 1e-16, ALU.add))
                chain(nc.vector.reciprocal(top[:], top[:]))
                chain(nc.vector.tensor_tensor(f[:], f[:], top[:], ALU.mult))
                chain(nc.vector.tensor_tensor(g[:], g[:], top[:], ALU.mult))
                scale_heads(nc, chain, c.acc[:, :, 0:D], f, H4)
                scale_heads(nc, chain, rows[:, :, 0:D], g, H4)
                chain(nc.vector.tensor_tensor(out[:], c.acc[:, :, 0:D], rows[:, :, 0:D], ALU.add))
                dve.wait_ge(vecs_in, 48)
                nc.vector.tensor_tensor(out[:], out[:], vecs[:, 0:1, :].to_broadcast(wide), ALU.add).then_inc(sums_wanted, 1)
                dve.wait_ge(sums_ready, 1)
                chain(nc.vector.tensor_single_scalar(stat[:, 0, :], c.banks[0][:, 0:D], 1.0 / N_NODES, ALU.mult))
                chain(nc.vector.tensor_tensor(out[:], out[:], stat[:, 0:1, :].to_broadcast(wide), ALU.subtract))
                nc.vector.tensor_tensor(c.h[:], out[:], out[:], ALU.mult).then_inc(sums_wanted, 1)
                dve.wait_ge(sums_ready, 2)
                nc.vector.tensor_scalar(stat[:, 1, :], c.banks[1][:, 0:D], 1.0 / N_NODES, 1e-5, ALU.mult,
                                        ALU.add).then_inc(var_ready, 1)
                dve.wait_ge(dev_ready, 1)
                chain(nc.vector.reciprocal(stat[:, 1, :], stat[:, 1, :]))
                chain(nc.vector.tensor_tensor(stat[:, 1, :], stat[:, 1, :], vecs[:, 1, :], ALU.mult))
                chain(nc.vector.tensor_tensor(out[:], out[:], stat[:, 1:2, :].to_broadcast(wide), ALU.mult))
                chain(nc.vector.tensor_tensor(out[:], out[:], vecs[:, 2:3, :].to_broadcast(wide), ALU.add))
                nc.vector.tensor_single_scalar(c.h[:], out[:], 0.0, ALU.min).then_inc(args_ready, 1)
                chain(nc.vector.scalar_tensor_tensor(out[:], out[:], 0.0, c.x[:], ALU.max, ALU.add))
                dve.wait_ge(exps_ready, 2)
                chain(nc.vector.scalar_tensor_tensor(c.x[:], c.h[:], -1.0, out[:], ALU.add, ALU.add))


def layer2(nc, c, a):
    with ExitStack() as st:
        def sb(name, shape, dt=F32):
            return st.enter_context(nc.sbuf_tensor(unique(c, name), shape, dt))
        rows = sb("gat_rows", [P, WINDOWS, GAT_ROW])
        a_dst = sb("a_dst", [P, WINDOWS, H4])
        parts = sb("dst_parts", [P, WINDOWS, 3 * H4], BF16)
        f = sb("f", [P, WINDOWS, H4])
        c.h_t = sb("h_t", [D, N_PAD])
        c.acc = sb("acc", [P, WINDOWS, D + 2 * H4])
        gat_node_phase(nc, c, a["L2_gnn_W"], True, a["L2_gnn_a_src"].rearrange("o h k -> (o h k)"),
                       a["L2_gnn_a_dst"].rearrange("o h k -> (o h k)"), rows, a_dst, parts)
        attention(nc, c, H4, lambda: pass_a_gat(nc, c, c.gat_table, parts, weighted=True))
        with semaphore(nc, c, "args_ready") as args_ready, semaphore(nc, c, "exps_ready") as exps_ready, \
                semaphore(nc, c, "vec_done") as vec_done, nc.Block() as block:
            @block.scalar
            def _(act):
                act.wait_ge(args_ready, 1)
                nc.scalar.activation(f[:], f[:], ACT.Exp).then_inc(exps_ready, 1)

            @block.vector
            def _(dve):
                chain = Chain(dve, vec_done)
                m_e, total = c.acc[:, :, D + H4:D + 2 * H4], c.acc[:, :, D:D + H4]
                nc.vector.tensor_single_scalar(f[:], m_e, 0.0, ALU.min).then_inc(args_ready, 1)
                dve.wait_ge(exps_ready, 1)
                chain(nc.vector.tensor_tensor(total, total, f[:], ALU.mult))
                chain(nc.vector.tensor_single_scalar(total, total, 1e-8, ALU.add))
                chain(nc.vector.reciprocal(total, total))
                chain(nc.vector.tensor_tensor(f[:], f[:], total, ALU.mult))
                scale_heads(nc, chain, c.acc[:, :, 0:D], f, H4)
                chain(nc.vector.tensor_tensor(c.x[:], c.x[:], c.acc[:, :, 0:D], ALU.add))



def typed_weights(nc, chain, comp, basis, to):
    for ty in range(TYPES):
        for b in range(BASES):
            s = comp[:, ty * BASES + b:ty * BASES + b + 1]
            if b == 0:
                last = nc.vector.tensor_scalar(to[:, ty, :], basis[:, b, :], s, None, ALU.mult)
            else:
                last = nc.vector.scalar_tensor_tensor(to[:, ty, :], basis[:, b, :], s, to[:, ty, :], ALU.mult, ALU.add)
            chain(last)


def mask_by_type(nc, c, dve, typed, typed_ready, group_used):
    for g, (n0, n) in enumerate(GROUPS):
        if g >= 2:
            dve.wait_ge(group_used, g - 1)
        for ty in range(TYPES):
            last = nc.vector.scalar_tensor_tensor(typed[:, g % 2, ty, 0:n], c.node_type[:, n0:n0 + n], float(ty),
                                                  c.h_t[:, n0:n0 + n], ALU.is_equal, ALU.mult)
        last.then_inc(typed_ready, 1)


def typed_projections(nc, c, w_k, w_v, w_q, k_t, v_t):
    with nc.sbuf_tensor(unique(c, "typed"), [D, 2, TYPES, NODE_GROUP], F32) as typed, semaphore(nc, c, "typed_ready") as typed_ready, \
            semaphore(nc, c, "group_used") as group_used, semaphore(nc, c, "job_ready") as job_ready, \
            semaphore(nc, c, "job_taken") as job_taken, nc.Block() as block:
        jobs = []
        for g, (n0, n) in enumerate(GROUPS):
            jobs += [(g, w_k, k_t[:, n0:n0 + n], 0, n), (g, w_v, v_t[:, n0:n0 + n], 0, n)]
            jobs += [(g, w_q, c.h[:, (n0 + at) // P, :], at, 0) for at in range(0, n, P)]

        @block.vector
        def _(dve):
            mask_by_type(nc, c, dve, typed, typed_ready, group_used)

        @block.tensor
        def _(pe):
            for n, (g, w, to, at, cols) in enumerate(jobs):
                pe.wait_ge(typed_ready, g + 1)
                if n >= 8:
                    pe.wait_ge(job_taken, n - 7)
                for ty in range(TYPES):
                    first, final = ty == 0, ty == TYPES - 1
                    if cols:
                        last = nc.tensor.matmul(c.banks[n % 8][:, 0:cols], w[:, ty, :], typed[:, g % 2, ty, 0:cols],
                                                start=first, stop=final)
                    else:
                        last = nc.tensor.matmul(c.banks[n % 8][:, 0:D], typed[:, g % 2, ty, at:at + P], w[:, ty, :],
                                                start=first, stop=final)
                last.then_inc(job_ready, 1)
                if n + 1 == len(jobs) or jobs[n + 1][0] != g:
                    pe.wait_ge(job_ready, n + 1)
                    pe.sem_inc(group_used, 1)

        @block.scalar
        def _(act):
            for n, (g, w, to, at, cols) in enumerate(jobs):
                act.wait_ge(job_ready, n + 1)
                nc.scalar.copy(to, c.banks[n % 8][:, 0:cols or D]).then_inc(job_taken, 1)


def layer3(nc, c, a):
    with ExitStack() as st:
        def sb(name, shape, dt=F32):
            return st.enter_context(nc.sbuf_tensor(unique(c, name), shape, dt))
        w_a = sb("w_a", [D, TYPES, D])
        loop_w = sb("loop_w", [D, D])
        bias = sb("bias", [P, D])
        c.node_type = sb("node_type", [P, N_PAD])
        c.h_t = sb("h_t", [D, N_PAD])
        normalise(nc, c)
        with ExitStack() as inner:
            def sbi(name, shape, dt=F32):
                return inner.enter_context(nc.sbuf_tensor(unique(c, name), shape, dt))
            parts = [sbi(f"dst_part{k}", [P, WINDOWS, D], BF16) for k in range(3)]
            with ExitStack() as pre:
                def sbp(name, shape, dt=F32):
                    return pre.enter_context(nc.sbuf_tensor(unique(c, name), shape, dt))
                w_k, w_v, w_q = (sbp(f"w_{n}", [D, TYPES, D]) for n in "kvq")
                blocks = [sbp(f"blocks_{n}", [D, TYPES, D]) for n in ("att", "msg")]
                k_t, v_t = sbp("k_t", [D, N_PAD]), sbp("v_t", [D, N_PAD])
                transpose_windows(nc, c, c.h, c.h_t)
                with ExitStack() as load:
                    def sbl(name, shape, dt=F32):
                        return load.enter_context(nc.sbuf_tensor(unique(c, name), shape, dt))
                    type_i = sbl("type_i", [P, N_PAD], I32)
                    comp = sbl("comp", [P, 4, TYPES * BASES])
                    basis = sbl("basis", [D, 4, BASES, D])
                    pri = sbl("pri", [P, TYPES, H8])
                    with semaphore(nc, c, "cleared") as cleared, semaphore(nc, c, "loaded") as loaded, \
                            semaphore(nc, c, "vec_done") as vec_done, nc.Block() as block:
                        names = [("k", w_k), ("v", w_v), ("q", w_q), ("a", w_a)]
                        comps = dict(k=a["L3_gnn_w_comp_k"], v=a["L3_gnn_w_comp_v"], q=a["L3_gnn_w_comp_q"], a=a["L3_gnn_w_comp_a"])
                        bases = dict(k=a["L3_gnn_w_basis_k"], v=a["L3_gnn_w_basis_v"], q=a["L3_gnn_w_basis_q"], a=a["L3_gnn_w_basis_a"])
                        N_LOADS = 1 + 8 + 16 + 1 + 2

                        @block.sync
                        def _(sp):
                            sp.wait_ge(cleared, 3)
                            sp.dma_start(type_i[:, 0:N_NODES], a["node_type_8"].partition_broadcast(P)).then_inc(loaded, 16)
                            for k, (n, _w) in enumerate(names):
                                sp.dma_start(comp[:, k, :], comps[n].rearrange("t b -> (t b)").partition_broadcast(P)).then_inc(loaded, 16)
                                sp.dma_start(basis[:, k], bases[n].rearrange("b (i o) -> i b o", o=D)).then_inc(loaded, 16)
                            hd = D // H8
                            for to, source in zip(blocks, (a["L3_gnn_relation_att"], a["L3_gnn_relation_msg"])):
                                for h in range(H8):
                                    sp.dma_start(to[h * hd:(h + 1) * hd, :, h * hd:(h + 1) * hd],
                                                 source[:, h].rearrange("t i j -> i t j")).then_inc(loaded, 16)
                            sp.dma_start(pri[:].rearrange("p t h -> p (t h)"),
                                         a["L3_gnn_relation_pri"].rearrange("t h -> (t h)").partition_broadcast(P)).then_inc(loaded, 16)
                            sp.dma_start(loop_w[:], a["L3_gnn_loop_weight"]).then_inc(loaded, 16)
                            sp.dma_start(bias[:], a["L3_gnn_bias"].partition_broadcast(P)).then_inc(loaded, 16)
                            sp.wait_ge(loaded, 16 * N_LOADS)

                        @block.vector
                        def _(dve):
                            nc.vector.memset(type_i[:], 0).then_inc(cleared, 1)
                            for t in blocks:
                                nc.vector.memset(t[:], 0.0).then_inc(cleared, 1)
                            dve.wait_ge(loaded, 16 * N_LOADS)
                            chain = Chain(dve, vec_done)
                            chain(nc.vector.tensor_copy(c.node_type[:], type_i[:]))
                            for k, (n, w) in enumerate(names):
                                typed_weights(nc, chain, comp[:, k], basis[:, k], w)
                            chain(nc.vector.tensor_single_scalar(pri[:], pri[:], (D // H8) ** -0.5, ALU.mult))
                            for ty in range(TYPES):
                                b4 = blocks[0][:, ty, :].rearrange("p (h k) -> p h k", h=H8)
                                chain(nc.vector.tensor_tensor(b4, b4, pri[:, ty, :].unsqueeze(2).to_broadcast([P, H8, D // H8]),
                                                              ALU.mult))
                typed_projections(nc, c, w_k, w_v, w_q, k_t, v_t)
                with semaphore(nc, c, "vec_done") as vec_done, nc.Block() as block:
                    @block.vector
                    def _(dve):
                        split_three(nc, Chain(dve, vec_done), c.h[:], [p[:] for p in parts], c.wide_a[:])
                with ExitStack() as tab:
                    ring = tab.enter_context(nc.sbuf_tensor(unique(c, "ring"), [P, 2, TYPES, 2, D], F32))
                    with semaphore(nc, c, "half_ready") as half_ready, semaphore(nc, c, "half_taken") as half_taken, \
                            semaphore(nc, c, "half_taken_dve") as half_taken_dve, \
                            semaphore(nc, c, "rows_out0") as rows_out0, semaphore(nc, c, "rows_out1") as rows_out1, nc.Block() as block:
                        rows_out = [rows_out0, rows_out1]
                        quads = [(k, g) for k in range(2) for g in range(2)]

                        @block.tensor
                        def _(pe):
                            for w in range(WINDOWS):
                                for q, (k, g) in enumerate(quads):
                                    if w >= 2:
                                        pe.wait_ge(half_taken if k == 0 else half_taken_dve, 2 * (w - 2) + g + 1)
                                    nc.tensor.matmul(c.banks[(w % 2) * 4 + q][:, :], (k_t, v_t)[k][:, w * P:(w + 1) * P],
                                                     blocks[k][:, 4 * g:4 * g + 4, :].rearrange("p t d -> p (t d)"),
                                                     start=True, stop=True).then_inc(half_ready, 1)

                        @block.scalar
                        def _(act):
                            for w in range(WINDOWS):
                                if w >= 2:
                                    act.wait_ge(rows_out[w % 2], 16 * (w // 2))
                                for g in range(2):
                                    act.wait_ge(half_ready, 4 * w + g + 1)
                                    nc.scalar.copy(ring[:, w % 2, 4 * g:4 * g + 4, 0, :],
                                                   c.banks[(w % 2) * 4 + g][:, :].rearrange("p (t d) -> p t d", t=4)
                                                   ).then_inc(half_taken, 1)

                        @block.vector
                        def _(dve):
                            for w in range(WINDOWS):
                                if w >= 2:
                                    dve.wait_ge(rows_out[w % 2], 16 * (w // 2))
                                for g in range(2):
                                    dve.wait_ge(half_ready, 4 * w + 2 + g + 1)
                                    nc.vector.tensor_copy(ring[:, w % 2, 4 * g:4 * g + 4, 1, :],
                                                          c.banks[(w % 2) * 4 + 2 + g][:, :].rearrange("p (t d) -> p t d", t=4)
                                                          ).then_inc(half_taken_dve, 1)

                        @block.sync
                        def _(sp):
                            for w in range(WINDOWS):
                                sp.wait_ge(half_taken, 2 * w + 2)
                                sp.wait_ge(half_taken_dve, 2 * w + 2)
                                sp.dma_start(c.typed_table[w * P * TYPES:(w + 1) * P * TYPES, :].rearrange("(n t) d -> n (t d)", t=TYPES),
                                             ring[:, w % 2].rearrange("p t k d -> p (t k d)")).then_inc(rows_out[w % 2], 16)
                            sp.wait_ge(rows_out[0], 16 * ((WINDOWS + 1) // 2))
                            sp.wait_ge(rows_out[1], 16 * (WINDOWS // 2))
            c.acc = sbi("acc", [P, WINDOWS, D + 2 * H8])
            attention(nc, c, H8, lambda: pass_a_hgt(nc, c, c.typed_table, parts))
            with ExitStack() as fin:
                hgt_output(nc, c, fin, w_a, loop_w, bias)

def hgt_output(nc, c, fin, w_a, loop_w, bias):
    rden = fin.enter_context(nc.sbuf_tensor(unique(c, "rden"), [P, WINDOWS, H8], F32))
    loop_term = fin.enter_context(nc.sbuf_tensor(unique(c, "loop_term"), [P, WINDOWS, D], F32))
    typed = fin.enter_context(nc.sbuf_tensor(unique(c, "typed"), [D, 2, TYPES, NODE_GROUP], F32))
    project(nc, c, loop_w[:], D, loop_term)
    with semaphore(nc, c, "vec_done") as vec_done, nc.Block() as block:
        @block.vector
        def _(dve):
            chain = Chain(dve, vec_done)
            chain(nc.vector.tensor_single_scalar(rden[:], c.acc[:, :, D:D + H8], 1e-30, ALU.max))
            chain(nc.vector.reciprocal(rden[:], rden[:]))
            scale_heads(nc, chain, c.acc[:, :, 0:D], rden, H8)
            chain(nc.vector.tensor_copy(c.h[:], c.acc[:, :, 0:D]))
    transpose_windows(nc, c, c.h, c.h_t)
    with semaphore(nc, c, "typed_ready") as typed_ready, semaphore(nc, c, "group_used") as group_used, \
            semaphore(nc, c, "window_ready") as window_ready, semaphore(nc, c, "window_taken") as window_taken, nc.Block() as block:
        @block.vector
        def _(dve):
            mask_by_type(nc, c, dve, typed, typed_ready, group_used)

        @block.tensor
        def _(pe):
            w = 0
            for g, (n0, n) in enumerate(GROUPS):
                pe.wait_ge(typed_ready, g + 1)
                for at in range(0, n, P):
                    if w >= 4:
                        pe.wait_ge(window_taken, w - 3)
                    for ty in range(TYPES):
                        last = nc.tensor.matmul(c.banks[w % 4][:, 0:D], typed[:, g % 2, ty, at:at + P], w_a[:, ty, :],
                                                start=ty == 0, stop=ty == TYPES - 1)
                    last.then_inc(window_ready, 1)
                    w += 1
                pe.wait_ge(window_ready, w)
                pe.sem_inc(group_used, 1)

        @block.scalar
        def _(act):
            for w in range(WINDOWS):
                act.wait_ge(window_ready, w + 1)
                nc.scalar.copy(c.wide_a[:, w, :], c.banks[w % 4][:, 0:D]).then_inc(window_taken, 1)
    with semaphore(nc, c, "vec_done") as vec_done, nc.Block() as block:
        @block.vector
        def _(dve):
            chain = Chain(dve, vec_done)
            o = c.wide_a
            chain(nc.vector.tensor_tensor(o[:], o[:], loop_term[:], ALU.add))
            chain(nc.vector.tensor_tensor(o[:], o[:], bias[:].unsqueeze(1).to_broadcast([P, WINDOWS, D]), ALU.add))
            chain(nc.vector.scalar_tensor_tensor(c.x[:], o[:], 0.0, c.x[:], ALU.max, ALU.add))


def store_output(nc, c, out):
    with semaphore(nc, c, "out_stored") as out_stored, nc.Block() as block:
        @block.sync
        def _(sp):
            whole = (WINDOWS - 1) * P
            sp.dma_start(out[0:whole, :].rearrange("(w n) d -> n w d", n=P), c.x[:, 0:WINDOWS - 1, :]).then_inc(out_stored, 16)
            sp.dma_start(out[whole:N_NODES, :], c.x[0:LAST_NODES, WINDOWS - 1, :]).then_inc(out_stored, 16)
            sp.wait_ge(out_stored, 32)


def build_program(nc, a, out, layers=4):
    c = State()
    with ExitStack() as st:
        def sb(name, shape, dt=F32):
            return st.enter_context(nc.sbuf_tensor(unique(c, name), shape, dt))

        c.psum = st.enter_context(nc.psum_tensor("psum", [P, 8, 512], F32))
        c.banks = [c.psum[:, k, :] for k in range(8)]
        c.x = sb("x_nodes", [P, WINDOWS, D])
        c.h = sb("h_nodes", [P, WINDOWS, D])
        c.wide_a = sb("wide_a", [P, WINDOWS, D])
        c.ident = sb("ident", [P, P])
        c.ones = sb("ones", [P, P])
        c.iota = sb("iota", [P, 512])
        c.ident_b = sb("ident_b", [P, P], BF16)
        c.mean, c.rstd = sb("mean", [P, WINDOWS]), sb("rstd", [P, WINDOWS])
        c.window_i = sb("window_i", [1, STEPS], I32)
        c.dst_local = sb("dst_local", [P, STEPS])
        c.outside = sb("outside", [P, STEPS])
        c.is_end = sb("is_end", [P, STEPS])
        c.weight = sb("weight", [P, STEPS])
        c.idx_src = sb("idx_src", [P, STEPS + RING * GROUP], I32)
        c.idx_typed = sb("idx_typed", [P, STEPS + RING * GROUP], I32)
        c.relation = sb("relation", [P, STEPS])
        c.border = sb("border", [CH, NCH, P + 1])
        c.not_first = sb("not_first", [CH, NCH, P])
        c.not_last = sb("not_last", [CH, NCH, P])
        c.new_dst = sb("new_dst", [H8, STEPS + 1])
        c.stop_forward = sb("stop_forward", [H8, STEPS])
        c.stop_backward = sb("stop_backward", [H8, STEPS])
        load_constants(nc, c, a)
        build_steps(nc, c, a)
        c.stash = nc.dram_tensor("stash", [P, STEPS * D], F32, kind="Internal").ap()
        c.rel_src_table = nc.dram_tensor("rel_src_table", [N_PAD, 2 * D], F32, kind="Internal").ap()
        c.rel_dst_table = nc.dram_tensor("rel_dst_table", [N_PAD, D], F32, kind="Internal").ap()
        c.gat_table = nc.dram_tensor("gat_table", [N_PAD, GAT_ROW], F32, kind="Internal").ap()
        c.typed_table = nc.dram_tensor("typed_table", [N_PAD * TYPES, 2 * D], F32, kind="Internal").ap()
        for n, layer in enumerate((layer0, layer1, layer2, layer3)[0:layers]):
            c.layer = f"layer{n}"
            layer(nc, c, a)
            clear_semaphores(nc, c)
        store_output(nc, c, out)


_INS = ['x', 'src', 'dst', 'edge_type_200', 'edge_type_8', 'edge_weight', 'node_type_8', 'L0_gnn_z', 'L0_gnn_Wc_w',
        'L0_gnn_P_w', 'L0_gnn_y_w', 'L0_gnn_residual_weight', 'L1_gnn_W', 'L1_gnn_att_src', 'L1_gnn_att_dst',
        'L1_gnn_bias', 'L1_gnn_gamma', 'L1_gnn_beta', 'L2_gnn_W', 'L2_gnn_a_src', 'L2_gnn_a_dst', 'L3_gnn_w_comp_k',
        'L3_gnn_w_basis_k', 'L3_gnn_w_comp_q', 'L3_gnn_w_basis_q', 'L3_gnn_w_comp_v', 'L3_gnn_w_basis_v',
        'L3_gnn_w_comp_a', 'L3_gnn_w_basis_a', 'L3_gnn_relation_pri', 'L3_gnn_relation_att', 'L3_gnn_relation_msg',
        'L3_gnn_loop_weight', 'L3_gnn_bias']


def kernel(**inputs):
    import concourse.bacc as bacc
    from concourse.bass_utils import run_bass_kernel_spmd

    nc = bacc.Bacc("TRN2", target_bir_lowering=False, num_devices=1)
    arrays = {f"in_{n}": np.ascontiguousarray(inputs[n]) for n in _INS}
    a = {n: nc.dram_tensor(f"in_{n}", arrays[f"in_{n}"].shape, mybir.dt.from_np(arrays[f"in_{n}"].dtype),
                                             kind="ExternalInput").ap() for n in _INS}
    out = nc.dram_tensor("out", (N_NODES, D), F32, kind="ExternalOutput").ap()
    build_program(nc, a, out)
    r = run_bass_kernel_spmd(nc, [arrays], core_ids=[0])
    return r.results[0]["out"]
```

```python
import numpy as np
import concourse.bass as bass
import concourse.mybir as mybir
from contextlib import ExitStack, contextmanager

F32 = mybir.dt.float32
BF16 = mybir.dt.bfloat16
I32 = mybir.dt.int32
ALU = mybir.AluOpType
ACT = mybir.ActivationFunctionType
AX = mybir.AxisListType

P = 128
N_NODES = 3125
N_EDGES = 50000
D = 128
WINDOWS = -(-N_NODES // P)
LAST_NODES = N_NODES - (WINDOWS - 1) * P
N_PAD = WINDOWS * P
EDGE_TILES = -(-N_EDGES // P)
GROUP = 4
RING = 4
USED_STEPS = EDGE_TILES + WINDOWS - 1
TRIPS = -(-USED_STEPS // (GROUP * RING))
STEPS = TRIPS * GROUP * RING
CH = 104
NCH = STEPS // CH
SUMS_BY_VECTOR = 12
SPLIT_WINDOWS = 3
assert NCH * CH == STEPS and GROUP == 4
IC = 4
IP = 98
FULL_TILES = N_EDGES // P
TAIL = N_EDGES - FULL_TILES * P
LAST_ROWS = FULL_TILES - (IC - 1) * IP
SENTINEL = 4000
BIG = 1e30
RELS = 200
HALF_RELS = RELS // 2
TYPES = 8
BASES = 4
SLOPE = 0.2
GAT_ROW = D + 4
H8, H4 = 8, 4


class State:

    def __init__(self):
        self.serial = 0
        self.semaphores = []
        self.layer = ""


def unique(c, name):
    c.serial += 1
    return f"{name}_{c.serial}"


@contextmanager
def semaphore(nc, c, name):
    handle = nc.alloc_semaphore(unique(c, name))
    c.semaphores.append(handle)
    yield handle


def clear_semaphores(nc, c):
    nc.all_engine_barrier()
    nc.clear_and_free_semaphores(c.semaphores)
    nc.all_engine_barrier()
    c.semaphores = []


class Chain:

    def __init__(self, engine, sem):
        self.engine, self.sem, self.n = engine, sem, 0

    def __call__(self, instruction):
        self.n += 1
        instruction.then_inc(self.sem, 1)
        self.engine.wait_ge(self.sem, self.n)


def done(q):
    return q + 1 + RING


def before(q, ring=RING):
    return q + 1 + RING - ring


def in_bank(bank, n, width):
    return bank[:, n * width:(n + 1) * width]



def load_constants(nc, c, a):
    with semaphore(nc, c, "const_done") as const_done, semaphore(nc, c, "vec_done") as vec_done, nc.sbuf_tensor(unique(c, "iota_i"), [P, 512], I32) as iota_i, \
            nc.sbuf_tensor(unique(c, "down_i"), [P, 2], I32) as down_i, nc.Block() as block:

        @block.gpsimd
        def _(pool):
            nc.gpsimd.memset(c.ident[:], 0.0).then_inc(const_done, 1)
            pool.wait_ge(const_done, 1)
            nc.gpsimd.affine_select(out=c.ident[:], in_=c.ident[:], compare_op=ALU.not_equal, fill=1.0, base=0,
                                    pattern=[[-1, P]], channel_multiplier=1).then_inc(const_done, 1)
            nc.gpsimd.iota(iota_i[:], pattern=[[1, 512]], base=0, channel_multiplier=0).then_inc(const_done, 1)
            nc.gpsimd.iota(down_i[:], pattern=[[HALF_RELS, 2]], base=0, channel_multiplier=1).then_inc(const_done, 1)

        @block.vector
        def _(dve):
            chain = Chain(dve, vec_done)
            chain(nc.vector.memset(c.x[:], 0.0))
            chain(nc.vector.memset(c.ones[:], 1.0))
            dve.wait_ge(const_done, 4)
            chain(nc.vector.tensor_copy(c.down[:], down_i[:]))
            chain(nc.vector.tensor_copy(c.iota[:], iota_i[:]))

        @block.sync
        def _(sp):
            sp.wait_ge(vec_done, 1)
            whole = (WINDOWS - 1) * P
            sp.dma_start(c.x[:, 0:WINDOWS - 1, :], a["x"][0:whole, :].rearrange("(w n) d -> n w d", n=P)).then_inc(c.x_loaded, 16)
            sp.dma_start(c.x[0:LAST_NODES, WINDOWS - 1, :], a["x"][whole:N_NODES, :]).then_inc(c.x_loaded, 16)


def build_steps(nc, c, a):
    with ExitStack() as st:
        def sb(name, shape, dt=F32):
            return st.enter_context(nc.sbuf_tensor(unique(c, name), shape, dt))

        nat_i = sb("nat_i", [IP, 5, IC, P], I32)
        nat = sb("nat", [IP, 6, IC, P])
        tile_i = sb("tile_i", [IP, IC], I32)
        tile_no = sb("tile_no", [IP, IC])
        tile_row = sb("tile_row", [IP, IC, P])
        win_i = sb("win_i", [IP, 2, IC], I32)
        key = sb("key", [IP, 2, IC])
        after = sb("after", [IP, STEPS])
        pick = sb("pick", [IP, IC, STEPS])
        ends = sb("ends", [IP, 2, IC, H8])
        tmp = sb("tmp", [P, STEPS])
        window = sb("window", [P, STEPS])
        dst_t = sb("dst_t", [CH, NCH, P])
        fl = sb("fl", [H8, 2, STEPS])
        single = sb("single", [H8, STEPS])
        loaded = st.enter_context(semaphore(nc, c, "edges_loaded"))
        cleared = st.enter_context(semaphore(nc, c, "nat_cleared"))
        tiles_numbered = st.enter_context(semaphore(nc, c, "tiles_numbered"))
        vec_done = st.enter_context(semaphore(nc, c, "vec_done"))
        picked = st.enter_context(semaphore(nc, c, "picked"))
        by_step = st.enter_context(semaphore(nc, c, "by_step"))
        taken = st.enter_context(semaphore(nc, c, "by_step_taken"))
        by_chunk = st.enter_context(semaphore(nc, c, "by_chunk"))
        c.stats_ready = st.enter_context(semaphore(nc, c, "stats_ready"))
        c.root_ready = st.enter_context(semaphore(nc, c, "root_ready"))
        block = st.enter_context(nc.Block())
        sources = [(a["dst"], 0), (a["dst"], 1), (a["src"], 0), (a["edge_type_200"], 0), (a["edge_type_8"], 0)]

        @block.sync
        def _(sp):
            sp.wait_ge(cleared, 6)
            n = 0
            for k in range(6):
                source, off = (a["edge_weight"], 0) if k == 5 else sources[k]
                to = nat[:, 5] if k == 5 else nat_i[:, k]
                rows = (IC - 1) * IP
                sp.dma_start(to[:, 0:IC - 1, :],
                             source[off:off + rows * P].rearrange("(c p e) -> p c e", p=IP, e=P)).then_inc(loaded, 16)
                sp.dma_start(to[0:LAST_ROWS, IC - 1, :],
                             source[off + rows * P:off + FULL_TILES * P].rearrange("(p e) -> p e", e=P)).then_inc(loaded, 16)
                sp.dma_start(to[LAST_ROWS:LAST_ROWS + 1, IC - 1, 0:TAIL - off],
                             source[off + FULL_TILES * P:N_EDGES].rearrange("(p e) -> p e", p=1)).then_inc(loaded, 16)
                n += 3
            sp.wait_ge(loaded, 16 * n)

        @block.scalar
        def _(act):
            act.wait_ge(c.stats_ready, 1)
            nc.scalar.activation(c.rstd[:], c.rstd[:], ACT.Sqrt).then_inc(c.root_ready, 1)

        @block.gpsimd
        def _(pool):
            nc.gpsimd.iota(tile_i[:], pattern=[[IP, IC]], base=0, channel_multiplier=1).then_inc(tiles_numbered, 1)

        @block.vector
        def _(dve):
            for k in range(5):
                nc.vector.memset(nat_i[:, k], SENTINEL if k < 2 else 0).then_inc(cleared, 1)
            nc.vector.memset(nat[:, 5], 0.0).then_inc(cleared, 1)
            chain = Chain(dve, vec_done)
            dve.wait_ge(tiles_numbered, 1)
            chain(nc.vector.tensor_copy(tile_no[:], tile_i[:]))
            chain(nc.vector.tensor_copy(tile_row[:], tile_no[:].unsqueeze(2).to_broadcast([IP, IC, P])))
            dve.wait_ge(c.x_loaded, 32)
            layernorm(nc, c, chain)
            dve.wait_ge(loaded, 16 * 18)
            chain(nc.vector.tensor_copy(nat[:, 0:5], nat_i[:]))
            nc.vector.tensor_single_scalar(win_i[:, 0], nat_i[:, 0, :, 0], 7, ALU.arith_shift_right)
            chain(nc.vector.tensor_single_scalar(win_i[:, 1], nat_i[:, 1, :, P - 1], 7, ALU.arith_shift_right))
            chain(nc.vector.tensor_copy(key[:], win_i[:]))
            chain(nc.vector.tensor_tensor(key[:, 0], key[:, 0], tile_no[:], ALU.add))
            chain(nc.vector.scalar_tensor_tensor(key[:, 1], key[:, 1], 1.0, tile_no[:], ALU.add, ALU.add))
            chain(nc.vector.memset(key[0:1, 0, 0:1], 0.0))
            for k in range(IC):
                chain(nc.vector.tensor_scalar(after[:], c.iota[0:IP, 0:STEPS], key[:, 1, k:k + 1], None, ALU.is_ge))
                chain(nc.vector.scalar_tensor_tensor(pick[:, k, :], c.iota[0:IP, 0:STEPS], key[:, 0, k:k + 1], after[:],
                                                     ALU.is_ge, ALU.subtract))
            chain(nc.vector.tensor_copy(ends[:, 0], nat[:, 0, :, 0:1].to_broadcast([IP, IC, H8])))
            chain(nc.vector.tensor_copy(ends[:, 1], nat[:, 0, :, P - 1:P].to_broadcast([IP, IC, H8])))
            nc.vector.tensor_tensor(nat[:, 1], nat[:, 0], nat[:, 1], ALU.not_equal).then_inc(picked, 1)
            dve.wait_ge(by_step, 7)
            chain(nc.vector.tensor_tensor(window[:], c.iota[:, 0:STEPS], c.banks[6][:, 0:STEPS], ALU.subtract))
            chain(nc.vector.tensor_scalar(window[:], window[:], float(WINDOWS - 1), 0.0, ALU.min, ALU.max))
            chain(nc.vector.tensor_copy(c.window_i[:], window[0:1, :]))
            chain(nc.vector.scalar_tensor_tensor(c.dst_local, window[:], -float(P), c.banks[0][:, 0:STEPS],
                                                 ALU.mult, ALU.add))
            chain(nc.vector.memset(c.dst_local[:, USED_STEPS:STEPS], -1.0))
            chain(nc.vector.tensor_single_scalar(tmp[:], c.dst_local, 0.0, ALU.is_ge))
            chain(nc.vector.scalar_tensor_tensor(tmp[:], c.dst_local, float(P), tmp[:], ALU.is_lt, ALU.mult))
            chain(nc.vector.tensor_scalar(c.outside[:], tmp[:], 1.0, BIG, ALU.subtract, ALU.mult))
            chain(nc.vector.tensor_copy(c.is_end[:], c.banks[1][:, 0:STEPS]))
            chain(nc.vector.tensor_copy(tmp[:], c.banks[2][:, 0:STEPS]))
            chain(nc.vector.tensor_copy(c.idx_src[:, 0:STEPS], tmp[:]))
            chain(nc.vector.scalar_tensor_tensor(tmp[:], tmp[:], float(TYPES), c.banks[4][:, 0:STEPS],
                                                 ALU.mult, ALU.add))
            chain(nc.vector.tensor_copy(c.idx_typed[:, 0:STEPS], tmp[:]))
            chain(nc.vector.tensor_copy(c.relation[:, 0:STEPS], c.banks[3][:, 0:STEPS]))
            chain(nc.vector.tensor_copy(c.weight[:], c.banks[5][:, 0:STEPS]))
            for t in (c.idx_src, c.idx_typed, c.dst_pad, c.relation):
                chain(nc.vector.memset(t[:, STEPS:], 0))
            dve.sem_inc(taken, 1)
            dve.wait_ge(by_chunk, 2)
            for k in range(NCH):
                chain(nc.vector.tensor_copy(dst_t[:, k], c.banks[k // 4][0:CH, (k % 4) * P:(k % 4 + 1) * P]))
            chain(nc.vector.memset(c.border[:], -BIG))
            chain(nc.vector.tensor_tensor(c.border[:, :, 1:P], dst_t[:, :, 1:P], dst_t[:, :, 0:P - 1], ALU.not_equal))
            chain(nc.vector.tensor_single_scalar(c.border[:, :, 1:P], c.border[:, :, 1:P], -BIG, ALU.mult))
            for k in range(NCH):
                chain(nc.vector.tensor_scalar(c.not_first[:, k], dst_t[:, k], dst_t[:, k, 0:1], -BIG,
                                              ALU.not_equal, ALU.mult))
                chain(nc.vector.tensor_scalar(c.not_last[:, k], dst_t[:, k], dst_t[:, k, P - 1:P], -BIG,
                                              ALU.not_equal, ALU.mult))
            for k in range(2):
                chain(nc.vector.tensor_copy(fl[:, k], c.banks[2 + k][0:H8, 0:STEPS]))
            chain(nc.vector.memset(c.new_dst[:], -BIG))
            chain(nc.vector.tensor_tensor(c.new_dst[:, 1:STEPS], fl[:, 0, 1:STEPS], fl[:, 1, 0:STEPS - 1], ALU.not_equal))
            chain(nc.vector.tensor_single_scalar(c.new_dst[:, 1:STEPS], c.new_dst[:, 1:STEPS], -BIG, ALU.mult))
            chain(nc.vector.tensor_tensor(single[:], fl[:, 0], fl[:, 1], ALU.not_equal))
            chain(nc.vector.scalar_tensor_tensor(c.stop_forward[:], single[:], -BIG, c.new_dst[:, 0:STEPS], ALU.mult, ALU.add))
            chain(nc.vector.scalar_tensor_tensor(c.stop_backward[:], single[:], -BIG, c.new_dst[:, 1:STEPS + 1], ALU.mult, ALU.add))

        @block.tensor
        def _(pe):
            pe.wait_ge(picked, 1)
            for k in range(7):
                for i in range(IC):
                    lhs = tile_row[:, i, :] if k == 6 else nat[:, k, i, :]
                    last = nc.tensor.matmul(c.banks[k][:, 0:STEPS], lhs, pick[:, i, :], start=i == 0, stop=i == IC - 1)
                last.then_inc(by_step, 1)
            pe.wait_ge(taken, 1)
            for k in range(NCH):
                for i in range(IC):
                    last = nc.tensor.matmul(c.banks[k // 4][0:CH, (k % 4) * P:(k % 4 + 1) * P],
                                            pick[:, i, k * CH:(k + 1) * CH], nat[:, 0, i, :],
                                            start=i == 0, stop=i == IC - 1)
            last.then_inc(by_chunk, 1)
            for k in range(2):
                for i in range(IC):
                    last = nc.tensor.matmul(c.banks[2 + k][0:H8, 0:STEPS], ends[:, k, i, :], pick[:, i, :],
                                            start=i == 0, stop=i == IC - 1)
            last.then_inc(by_chunk, 1)


def store_edge_rows(nc, c):
    row_parts, row_pad, rows_out = c.row_parts, c.row_pad, c.edge_rows_out
    with semaphore(nc, c, "turned") as turned, semaphore(nc, c, "copied") as copied, nc.Block() as block:

        @block.tensor
        def _(pe):
            for b, source in enumerate((c.dst_local, c.relation)):
                for k in range(NCH):
                    last = nc.tensor.transpose(c.banks[b][0:CH, k * P:(k + 1) * P], source[:, k * CH:(k + 1) * CH], c.ident[:])
                last.then_inc(turned, 1)

        @block.vector
        def _(dve):
            nc.vector.memset(row_pad[:], -1.0).then_inc(copied, 1)
            for b in range(2):
                dve.wait_ge(turned, b + 1)
                nc.vector.tensor_copy(row_parts[:, b].rearrange("s k e -> s (k e)"), c.banks[b][0:CH, :]).then_inc(copied, 1)

        @block.sync
        def _(sp):
            sp.wait_ge(copied, 3)
            for b, rows in enumerate((c.dst_rows, c.relation_rows)):
                sp.dma_start(rows[0:STEPS * P].rearrange("(k s e) -> s k e", k=NCH, e=P), row_parts[:, b]).then_inc(rows_out, 16)
                sp.dma_start(rows[STEPS * P:(STEPS + 2 * GROUP) * P].rearrange("(s e) -> s e", e=P), row_pad[:]).then_inc(rows_out, 16)



def layernorm(nc, c, chain):
    wide = [P, WINDOWS, D]
    chain(nc.vector.tensor_reduce(c.mean[:], c.x[:], AX.X, ALU.add))
    chain(nc.vector.tensor_single_scalar(c.mean[:], c.mean[:], 1.0 / D, ALU.mult))
    chain(nc.vector.tensor_tensor(c.h[:], c.x[:], c.mean[:].unsqueeze(2).to_broadcast(wide), ALU.subtract))
    chain(nc.vector.tensor_tensor(c.wide_a[:], c.h[:], c.h[:], ALU.mult))
    chain(nc.vector.tensor_reduce(c.rstd[:], c.wide_a[:], AX.X, ALU.add))
    nc.vector.tensor_scalar(c.rstd[:], c.rstd[:], 1.0 / D, 1e-5, ALU.mult, ALU.add).then_inc(c.stats_ready, 1)
    chain.engine.wait_ge(c.root_ready, 1)
    chain(nc.vector.reciprocal(c.rstd[:], c.rstd[:]))
    chain(nc.vector.tensor_tensor(c.h[:], c.h[:], c.rstd[:].unsqueeze(2).to_broadcast(wide), ALU.mult))
    chain(nc.vector.tensor_single_scalar(c.h[:], c.h[:], 0.0, ALU.max))


def normalise(nc, c):
    with semaphore(nc, c, "stats_ready") as c.stats_ready, semaphore(nc, c, "root_ready") as c.root_ready, \
            semaphore(nc, c, "vec_done") as vec_done, nc.Block() as block:

        @block.vector
        def _(dve):
            layernorm(nc, c, Chain(dve, vec_done))

        @block.scalar
        def _(act):
            act.wait_ge(c.stats_ready, 1)
            nc.scalar.activation(c.rstd[:], c.rstd[:], ACT.Sqrt).then_inc(c.root_ready, 1)


def transpose_windows(nc, c, source, to):
    groups = -(-WINDOWS // 4)
    with semaphore(nc, c, "group_ready") as group_ready, semaphore(nc, c, "group_taken") as group_taken, nc.Block() as block:

        @block.tensor
        def _(pe):
            for g in range(groups):
                if g >= 4:
                    pe.wait_ge(group_taken, g - 3)
                for w in range(4 * g, min(4 * g + 4, WINDOWS)):
                    last = nc.tensor.transpose(c.banks[g % 4][:, (w % 4) * P:(w % 4 + 1) * P], source[:, w, :], c.ident[:])
                last.then_inc(group_ready, 1)

        @block.scalar
        def _(act):
            for g in range(groups):
                n = (min(4 * g + 4, WINDOWS) - 4 * g) * P
                act.wait_ge(group_ready, g + 1)
                nc.scalar.copy(to[:, 4 * g * P:4 * g * P + n], c.banks[g % 4][:, 0:n]).then_inc(group_taken, 1)


def project(nc, c, weights, width, to):
    with semaphore(nc, c, "window_ready") as window_ready, semaphore(nc, c, "window_taken") as window_taken, nc.Block() as block:

        @block.tensor
        def _(pe):
            for w in range(WINDOWS):
                if w >= 4:
                    pe.wait_ge(window_taken, w - 3)
                nc.tensor.matmul(c.banks[w % 4][:, 0:width], c.h_t[:, w * P:(w + 1) * P], weights,
                                 start=True, stop=True).then_inc(window_ready, 1)

        @block.scalar
        def _(act):
            for w in range(WINDOWS):
                act.wait_ge(window_ready, w + 1)
                nc.scalar.copy(to[:, w, 0:width], c.banks[w % 4][:, 0:width]).then_inc(window_taken, 1)


def split_three(nc, chain, value, parts, rest):
    chain(nc.vector.tensor_copy(parts[0], value))
    chain(nc.vector.tensor_tensor(rest, value, parts[0], ALU.subtract))
    chain(nc.vector.tensor_copy(parts[1], rest))
    chain(nc.vector.tensor_tensor(rest, rest, parts[1], ALU.subtract))
    chain(nc.vector.tensor_copy(parts[2], rest))



def edge_softmax(nc, c, heads):
    hd = heads
    with ExitStack() as st:
        seg_max = st.enter_context(nc.sbuf_tensor(unique(c, "seg_max"), [CH, NCH, hd, P], F32))
        run = st.enter_context(nc.sbuf_tensor(unique(c, "run"), [CH, hd, P], F32))
        edge_vals = st.enter_context(nc.sbuf_tensor(unique(c, "edge_vals"), [CH, 2, NCH, hd], F32))
        chains = st.enter_context(nc.sbuf_tensor(unique(c, "chains"), [H8, 2, STEPS], F32))
        carry = st.enter_context(nc.sbuf_tensor(unique(c, "carry"), [H8, 2, STEPS], F32))
        carry_t = st.enter_context(nc.sbuf_tensor(unique(c, "carry_t"), [CH, NCH, 2, hd], F32))
        masked = st.enter_context(semaphore(nc, c, "logits_masked"))
        vec_done = st.enter_context(semaphore(nc, c, "vec_done"))
        turned = st.enter_context(semaphore(nc, c, "logits_turned"))
        scanned = st.enter_context(semaphore(nc, c, "chunk_scanned"))
        edges_out = st.enter_context(semaphore(nc, c, "edge_vals_ready"))
        edges_turned = st.enter_context(semaphore(nc, c, "edge_vals_turned"))
        carries = st.enter_context(semaphore(nc, c, "carries_ready"))
        carries_turned = st.enter_context(semaphore(nc, c, "carries_turned"))
        maxima = st.enter_context(semaphore(nc, c, "maxima_ready"))
        back = st.enter_context(semaphore(nc, c, "maxima_back"))
        args = st.enter_context(semaphore(nc, c, "exp_args_ready"))
        block = st.enter_context(nc.Block())

        def turned_logits(k, h):
            n = (k % 2) * 2 * 4 + h
            return c.banks[n // 4][0:CH, (n % 4) * P:(n % 4 + 1) * P]

        @block.tensor
        def _(pe):
            pe.wait_ge(masked, 1)
            for k in range(NCH):
                if k >= 2:
                    pe.wait_ge(scanned, k - 1)
                for h in range(hd):
                    last = nc.tensor.transpose(turned_logits(k, h), c.logits[:, h, k * CH:(k + 1) * CH], c.ident[:])
                last.then_inc(turned, 1)
            pe.wait_ge(edges_out, 1)
            for b in range(2):
                for k in range(NCH):
                    last = nc.tensor.transpose(c.banks[4 + b][0:hd, k * CH:(k + 1) * CH], edge_vals[:, b, k, :],
                                               c.ident[0:CH, 0:CH])
            last.then_inc(edges_turned, 1)
            pe.wait_ge(carries, 1)
            for k in range(NCH):
                for b in range(2):
                    n = (k * 2 + b) * hd
                    last = nc.tensor.transpose(c.banks[6][0:CH, n:n + hd], carry[0:hd, b, k * CH:(k + 1) * CH],
                                               c.ident[0:hd, 0:hd])
            last.then_inc(carries_turned, 1)
            pe.wait_ge(maxima, 1)
            for h in range(hd):
                for k in range(NCH):
                    last = nc.tensor.transpose(c.banks[h][:, k * CH:(k + 1) * CH], seg_max[:, k, h, :],
                                               c.ident[0:CH, 0:CH])
                last.then_inc(back, 1)

        @block.vector
        def _(dve):
            chain = Chain(dve, vec_done)
            nc.vector.tensor_tensor(c.logits[:, 0:hd, :], c.logits[:, 0:hd, :],
                                    c.outside[:].unsqueeze(1).to_broadcast([P, hd, STEPS]), ALU.add).then_inc(masked, 1)
            for k in range(NCH):
                dve.wait_ge(turned, k + 1)
                for h in range(hd):
                    last = nc.vector.tensor_tensor_scan(run[:, h, :], c.border[:, k, 0:P], turned_logits(k, h),
                                                        -BIG, ALU.add, ALU.max)
                chain(last)
                for h in range(hd):
                    last = nc.vector.tensor_tensor_scan(seg_max[:, k, h, ::-1], c.border[:, k, 1:P + 1][:, ::-1],
                                                        run[:, h, ::-1], -BIG, ALU.add, ALU.max)
                last.then_inc(scanned, 1)
                dve.wait_ge(scanned, k + 1)
            chain(nc.vector.tensor_copy(edge_vals[:, 0], seg_max[:, :, :, 0]))
            nc.vector.tensor_copy(edge_vals[:, 1], seg_max[:, :, :, P - 1]).then_inc(edges_out, 1)
            dve.wait_ge(edges_turned, 1)
            chain(nc.vector.tensor_tensor_scan(chains[0:hd, 0], c.stop_forward[0:hd, :], c.banks[5][0:hd, 0:STEPS],
                                               -BIG, ALU.add, ALU.max))
            chain(nc.vector.tensor_tensor_scan(chains[0:hd, 1, ::-1], c.stop_backward[0:hd, ::-1],
                                               c.banks[4][0:hd, 0:STEPS][:, ::-1], -BIG, ALU.add, ALU.max))
            chain(nc.vector.memset(carry[:], -BIG))
            chain(nc.vector.tensor_tensor(carry[0:hd, 0, 1:STEPS], chains[0:hd, 0, 0:STEPS - 1],
                                          c.new_dst[0:hd, 1:STEPS], ALU.add))
            nc.vector.tensor_tensor(carry[0:hd, 1, 0:STEPS - 1], chains[0:hd, 1, 1:STEPS],
                                    c.new_dst[0:hd, 1:STEPS], ALU.add).then_inc(carries, 1)
            dve.wait_ge(carries_turned, 1)
            chain(nc.vector.tensor_copy(carry_t[:].rearrange("p k b h -> p (k b h)"),
                                        c.banks[6][0:CH, 0:NCH * 2 * hd]))
            for b, off in ((0, c.not_first), (1, c.not_last)):
                for k in range(NCH):
                    for h in range(hd):
                        last = nc.vector.scalar_tensor_tensor(seg_max[:, k, h, :], off[:, k, :], carry_t[:, k, b, h:h + 1],
                                                              seg_max[:, k, h, :], ALU.add, ALU.max)
                chain(last)
            dve.sem_inc(maxima, 1)
            for h in range(hd):
                dve.wait_ge(back, h + 1)
                m = c.banks[h][:, 0:STEPS]
                nc.vector.tensor_tensor(c.shares[:, :, hd + h], m, c.is_end[:], ALU.mult)
                nc.vector.tensor_tensor(c.logits[:, h, :], c.logits[:, h, :], m, ALU.subtract).then_inc(args, 1)

        @block.scalar
        def _(act):
            for h in range(hd):
                act.wait_ge(args, h + 1)
                nc.scalar.activation(c.shares[:, :, h], c.logits[:, h, :], ACT.Exp)



def onehots_for_group(nc, c, onehot, g, q):
    return nc.vector.tensor_tensor(onehot[:, g], c.iota[:, 0:P].unsqueeze(1).to_broadcast([P, GROUP, P]),
                                   c.dst_pad[:, bass.ds(q * GROUP, GROUP)].unsqueeze(2).to_broadcast([P, GROUP, P]),
                                   ALU.is_equal)


def load_windows(nc, c, engine, q):
    _, windows = nc.values_load_multi_w_load_instructions(
        c.window_i[0:1, bass.ds(q * GROUP, GROUP)], engines=[engine.engine], min_val=0, max_val=WINDOWS - 1,
        skip_runtime_bounds_check_because="build_steps clamps every window to 0..WINDOWS - 1")
    return windows


def pass_b(nc, c, heads):
    width = D + 2 * heads
    with ExitStack() as st:
        def sb(name, shape, dt=F32):
            return st.enter_context(nc.sbuf_tensor(unique(c, name), shape, dt))

        values = sb("values", [P, RING, GROUP, D])
        weighted = c.wide_a[:].rearrange("p w d -> p (w d)")[:, 0:RING * GROUP * width].rearrange(
            "p (g u d) -> p g u d", g=RING, u=GROUP)
        rest = sb("rest", [P, RING, GROUP, width])
        parts = [sb(f"part{k}", [P, RING, GROUP, width], BF16) for k in range(3)]
        onehot = sb("onehot", [P, RING, GROUP, P], BF16)
        zeros = sb("zeros", [P, P], BF16)
        wide_zeros = zeros[:].unsqueeze(1).to_broadcast([P, 4, P])
        values_in = [st.enter_context(semaphore(nc, c, f"values_in{g}")) for g in range(RING)]
        weighted_ready = st.enter_context(semaphore(nc, c, "weighted_ready"))
        shares_ready = st.enter_context(semaphore(nc, c, "shares_ready"))
        part0_ready = st.enter_context(semaphore(nc, c, "part0_ready"))
        rest_ready = st.enter_context(semaphore(nc, c, "rest_ready"))
        part1_ready = st.enter_context(semaphore(nc, c, "part1_ready"))
        part2_ready = st.enter_context(semaphore(nc, c, "part2_ready"))
        onehot_ready = st.enter_context(semaphore(nc, c, "onehot_ready"))
        summed = st.enter_context(semaphore(nc, c, "summed"))
        zeros_ready = st.enter_context(semaphore(nc, c, "zeros_ready"))
        issue = st.enter_context(semaphore(nc, c, "issue"))
        block = st.enter_context(nc.Block())
        value_sums = c.psum[:, 0:7, :].rearrange("p b d -> p (b d)").rearrange("p (w d) -> p w d", d=D)
        share_sums = c.psum[:, 7, :].rearrange("p (w h) -> p w h", h=2 * heads)

        @block.sync
        def _(sp):
            with sp.Fori(0, TRIPS) as t:
                for g in range(RING):
                    q = t * RING + g
                    sp.wait_ge(weighted_ready, q + 1)
                    sp.dma_start(values[:, g].rearrange("p u d -> p (u d)"),
                                 c.stash[:, bass.ds(q * (GROUP * D), GROUP * D)]).then_inc(values_in[g], 16)

        @block.gpsimd
        def _(pool):
            pool.sem_inc(part2_ready, RING)
            with pool.Fori(0, TRIPS) as t:
                for g in range(RING):
                    q = t * RING + g
                    pool.wait_ge(part1_ready, done(q))
                    pool.sem_inc(issue, 1)
                    nc.gpsimd.tensor_tensor(parts[2][:, g], rest[:, g], parts[1][:, g], ALU.subtract).then_inc(part2_ready, 1)

        @block.vector
        def _(dve):
            nc.vector.memset(zeros[:], 0.0).then_inc(zeros_ready, 1)
            dve.sem_inc(weighted_ready, RING)
            dve.sem_inc(rest_ready, RING)
            dve.sem_inc(onehot_ready, RING)

            def weigh(t, g):
                q = t * RING + g
                dve.wait_ge(rest_ready, q + 1)
                dve.wait_ge(values_in[g], t * 16 + 16)
                nc.vector.tensor_tensor(
                    weighted[:, g, :, 0:D].rearrange("p u (h k) -> p u h k", h=heads),
                    values[:, g].rearrange("p u (h k) -> p u h k", h=heads),
                    c.shares[:, bass.ds(q * GROUP, GROUP), 0:heads].unsqueeze(3).to_broadcast([P, GROUP, heads, D // heads]),
                    ALU.mult).then_inc(weighted_ready, 1)

            with dve.Fori(0, TRIPS) as t:
                weigh(t, 0)
                for g in range(RING):
                    q = t * RING + g
                    if g + 1 < RING:
                        weigh(t, g + 1)
                    dve.wait_ge(summed, q + 1)
                    onehots_for_group(nc, c, onehot, g, q).then_inc(onehot_ready, 1)
                    dve.wait_ge(part0_ready, done(q))
                    dve.wait_ge(part2_ready, q + 1)
                    nc.vector.tensor_tensor(rest[:, g], weighted[:, g], parts[0][:, g], ALU.subtract).then_inc(rest_ready, 1)
            dve.wait_ge(summed, STEPS // GROUP + RING + 1)
            for w in range(0, SUMS_BY_VECTOR, 4):
                nc.vector.tensor_copy(c.acc[:, w:w + 4, 0:D], value_sums[:, w:w + 4, :])

        @block.scalar
        def _(act):
            act.sem_inc(part0_ready, RING)
            act.sem_inc(part1_ready, RING)
            act.sem_inc(shares_ready, RING)

            def first_part(t, g):
                q = t * RING + g
                act.wait_ge(rest_ready, q + 1)
                act.sem_inc(issue, 1)
                nc.scalar.copy(weighted[:, g, :, D:width], c.shares[:, bass.ds(q * GROUP, GROUP), :]).then_inc(shares_ready, 1)
                act.wait_ge(weighted_ready, done(q))
                act.wait_ge(shares_ready, done(q))
                act.wait_ge(summed, q + 1)
                nc.scalar.copy(parts[0][:, g], weighted[:, g]).then_inc(part0_ready, 1)

            with act.Fori(0, TRIPS) as t:
                first_part(t, 0)
                for g in range(RING):
                    q = t * RING + g
                    if g + 1 < RING:
                        first_part(t, g + 1)
                    act.wait_ge(rest_ready, done(q))
                    nc.scalar.copy(parts[1][:, g], rest[:, g]).then_inc(part1_ready, 1)
            act.wait_ge(summed, STEPS // GROUP + RING + 1)
            for w in range(SUMS_BY_VECTOR, WINDOWS, 4):
                n = min(4, WINDOWS - w)
                nc.scalar.copy(c.acc[:, w:w + n, 0:D], value_sums[:, w:w + n, :])
            nc.scalar.copy(c.acc[:, :, D:width], share_sums[:, 0:WINDOWS, :])

        @block.tensor
        def _(pe):
            pe.wait_ge(zeros_ready, 1)
            for k in range(8):
                last = nc.tensor.matmul(c.banks[k][:, :], zeros[:], wide_zeros, start=True, stop=False)
            pe.sem_inc(summed, RING)
            with pe.Fori(0, TRIPS) as t:
                for g in range(RING):
                    q = t * RING + g
                    js = load_windows(nc, c, pe, q)
                    pe.wait_ge(onehot_ready, done(q))
                    pe.wait_ge(part2_ready, done(q))
                    for u in range(GROUP):
                        for k in range(3):
                            nc.tensor.matmul(value_sums[:, js[u], :], onehot[:, g, u, :], parts[k][:, g, u, 0:D],
                                             start=False, stop=False)
                        for k in range(3):
                            last = nc.tensor.matmul(share_sums[:, js[u], :], onehot[:, g, u, :],
                                                    parts[k][:, g, u, D:width], start=False, stop=False)
                    last.then_inc(summed, 1)
            for k in range(8):
                last = nc.tensor.matmul(c.banks[k][:, :], zeros[:], wide_zeros, start=False, stop=True)
            last.then_inc(summed, 1)


def attention(nc, c, heads, pass_a):
    with nc.sbuf_tensor(unique(c, c.layer + "_logits"), [P, heads, STEPS], F32) as c.logits:
        pass_a()
        with nc.sbuf_tensor(unique(c, c.layer + "_shares"), [P, STEPS, 2 * heads], F32) as c.shares:
            edge_softmax(nc, c, heads)
            pass_b(nc, c, heads)



def gather_group(nc, rows, g, table, idx, sem):
    for u in range(GROUP):
        nc.gpsimd.indirect_dma_start(out=rows[:, g, u, :], out_offset=None, in_=table[:, :],
                                     in_offset=bass.IndirectOffsetOnAxis(ap=idx[:, g * GROUP + u:g * GROUP + u + 1], axis=0)
                                     ).then_inc(sem, 16)


def load_row(c, sp, to, rows, q):
    return sp.dma_start(to, rows[bass.ds(q * (GROUP * P), GROUP * P)].partition_broadcast(to.shape[0]))


def compare_row(nc, c, to, row, half=0):
    return nc.vector.tensor_scalar(to, row, c.down[0:to.shape[0], half:half + 1], None, ALU.is_equal)


def pass_a_gat(nc, c, table, parts, weighted):
    with ExitStack() as st:
        def sb(name, shape, dt=F32):
            return st.enter_context(nc.sbuf_tensor(unique(c, name), shape, dt))

        rows = sb("rows", [P, RING, GROUP, GAT_ROW])
        dst_term = sb("dst_term", [P, RING, GROUP, H4])
        idx = sb("idx", [P, RING * GROUP], I32)
        dst_row = sb("dst_row", [P, RING, GROUP * P], BF16)
        onehot_t = sb("onehot_t", [P, RING, GROUP * P], BF16)
        row_in = [st.enter_context(semaphore(nc, c, f"row_in{g}")) for g in range(RING)]
        gathered = [st.enter_context(semaphore(nc, c, f"gathered{g}")) for g in range(RING)]
        stored = [st.enter_context(semaphore(nc, c, f"stored{g}")) for g in range(RING)]
        idx_ready = st.enter_context(semaphore(nc, c, "idx_ready"))
        issue = st.enter_context(semaphore(nc, c, "issue"))
        onehot_ready = st.enter_context(semaphore(nc, c, "onehot_t_ready"))
        fetched = st.enter_context(semaphore(nc, c, "dst_term_ready"))
        dst_summed = st.enter_context(semaphore(nc, c, "dst_parts_summed"))
        logits_out = st.enter_context(semaphore(nc, c, "logits_written"))
        block = st.enter_context(nc.Block())

        @block.gpsimd
        def _(pool):
            with pool.Fori(0, TRIPS) as t:
                for g in range(RING):
                    q = t * RING + g
                    pool.wait_ge(idx_ready, q + 1)
                    pool.wait_ge(logits_out, before(q))
                    pool.wait_ge(stored[g], t * 16 + 16)
                    pool.sem_inc(issue, 1)
                    gather_group(nc, rows, g, table, idx, gathered[g])

        @block.sync
        def _(sp):
            for g in range(RING):
                sp.sem_inc(stored[g], 16)
            with sp.Fori(0, TRIPS) as t:
                for g in range(RING):
                    q = t * RING + g
                    sp.wait_ge(onehot_ready, before(q))
                    load_row(c, sp, dst_row[:, g], c.dst_rows, q).then_inc(row_in[g], 16)
                for g in range(RING):
                    q = t * RING + g
                    sp.wait_ge(gathered[g], t * (16 * GROUP) + 16 * GROUP)
                    sp.sem_inc(issue, 1)
                    sp.dma_start(c.stash[:, bass.ds(q * (GROUP * D), GROUP * D)].rearrange("p (u d) -> p u d", d=D),
                                 rows[:, g, :, 0:D]).then_inc(stored[g], 16)
            for g in range(RING):
                sp.wait_ge(stored[g], 16 * (TRIPS + 1))

        @block.vector
        def _(dve):
            for sem in (logits_out, onehot_ready, dst_summed):
                dve.sem_inc(sem, RING)
            nc.vector.tensor_copy(idx[:], c.idx_src[:, 0:RING * GROUP]).then_inc(idx_ready, RING)
            with dve.Fori(0, TRIPS) as t:
                for g in range(RING):
                    q = t * RING + g
                    dve.wait_ge(row_in[g], t * 16 + 16)
                    dve.wait_ge(fetched, before(q))
                    compare_row(nc, c, onehot_t[:, g], dst_row[:, g]).then_inc(onehot_ready, 1)
                for g in range(RING):
                    q = t * RING + g
                    dve.wait_ge(gathered[g], t * (16 * GROUP) + 16 * GROUP)
                    nc.vector.tensor_scalar(idx[:, g * GROUP:(g + 1) * GROUP], c.idx_src[:, bass.ds((q + RING) * GROUP, GROUP)],
                                            0, None, ALU.add).then_inc(idx_ready, 1)
                    dve.wait_ge(fetched, done(q))
                    nc.vector.tensor_reduce(dst_term[:, g], c.banks[g][:, 0:GROUP * 3 * H4].rearrange("p (u k h) -> p u h k", k=3, h=H4),
                                            AX.X, ALU.add).then_inc(dst_summed, 1)
                    dve.wait_ge(dst_summed, done(q))
                    nc.vector.tensor_tensor(c.logits[:, :, bass.ds(q * GROUP, GROUP)],
                                            rows[:, g, :, D:D + H4].rearrange("p u h -> p h u"),
                                            dst_term[:, g].rearrange("p u h -> p h u"), ALU.add).then_inc(logits_out, 1)

        @block.tensor
        def _(pe):
            pe.sem_inc(fetched, RING)
            with pe.Fori(0, TRIPS) as t:
                for g in range(RING):
                    q = t * RING + g
                    js = load_windows(nc, c, pe, q)
                    pe.wait_ge(onehot_ready, done(q))
                    pe.wait_ge(dst_summed, before(q))
                    for u in range(GROUP):
                        last = nc.tensor.matmul(in_bank(c.banks[g], u, 3 * H4), in_bank(onehot_t[:, g], u, P),
                                                parts[:, js[u], :], start=True, stop=True)
                    last.then_inc(fetched, 1)
    gat_logits(nc, c, weighted)


def pass_a_hgt(nc, c, table, parts):
    with ExitStack() as st:
        def sb(name, shape, dt=F32):
            return st.enter_context(nc.sbuf_tensor(unique(c, name), shape, dt))

        rows = sb("rows", [P, RING, GROUP, 2 * D])
        idx = sb("idx", [P, RING * GROUP], I32)
        dst_row = sb("dst_row", [P, RING, GROUP * P], BF16)
        onehot_t = sb("onehot_t", [P, RING, GROUP * P], BF16)
        product = sb("product", [P, 2, GROUP, D])
        scores = sb("scores", [P, 2, GROUP, H8])
        row_in = [st.enter_context(semaphore(nc, c, f"row_in{g}")) for g in range(RING)]
        gathered = [st.enter_context(semaphore(nc, c, f"gathered{g}")) for g in range(RING)]
        stored = [st.enter_context(semaphore(nc, c, f"stored{g}")) for g in range(RING)]
        idx_ready = st.enter_context(semaphore(nc, c, "idx_ready"))
        issue = st.enter_context(semaphore(nc, c, "issue"))
        onehot_ready = st.enter_context(semaphore(nc, c, "onehot_t_ready"))
        fetched = st.enter_context(semaphore(nc, c, "queries_ready"))
        product_ready = st.enter_context(semaphore(nc, c, "product_ready"))
        scores_ready = st.enter_context(semaphore(nc, c, "scores_ready"))
        scores_out = st.enter_context(semaphore(nc, c, "scores_out"))
        block = st.enter_context(nc.Block())

        @block.gpsimd
        def _(pool):
            with pool.Fori(0, TRIPS) as t:
                for g in range(RING):
                    q = t * RING + g
                    pool.wait_ge(idx_ready, q + 1)
                    pool.wait_ge(product_ready, before(q))
                    pool.wait_ge(stored[g], t * 16 + 16)
                    pool.sem_inc(issue, 1)
                    gather_group(nc, rows, g, table, idx, gathered[g])

        @block.sync
        def _(sp):
            for g in range(RING):
                sp.sem_inc(stored[g], 16)
            with sp.Fori(0, TRIPS) as t:
                for g in range(RING):
                    q = t * RING + g
                    sp.wait_ge(onehot_ready, before(q))
                    load_row(c, sp, dst_row[:, g], c.dst_rows, q).then_inc(row_in[g], 16)
                for g in range(RING):
                    q = t * RING + g
                    sp.wait_ge(gathered[g], t * (16 * GROUP) + 16 * GROUP)
                    sp.sem_inc(issue, 1)
                    sp.dma_start(c.stash[:, bass.ds(q * (GROUP * D), GROUP * D)].rearrange("p (u d) -> p u d", d=D),
                                 rows[:, g, :, D:2 * D]).then_inc(stored[g], 16)
            for g in range(RING):
                sp.wait_ge(stored[g], 16 * (TRIPS + 1))

        @block.vector
        def _(dve):
            for sem in (product_ready, scores_ready, scores_out, onehot_ready):
                dve.sem_inc(sem, RING)
            nc.vector.tensor_copy(idx[:], c.idx_typed[:, 0:RING * GROUP]).then_inc(idx_ready, RING)
            with dve.Fori(0, TRIPS) as t:
                for g in range(RING):
                    q = t * RING + g
                    dve.wait_ge(row_in[g], t * 16 + 16)
                    dve.wait_ge(fetched, before(q))
                    compare_row(nc, c, onehot_t[:, g], dst_row[:, g]).then_inc(onehot_ready, 1)
                for g in range(RING):
                    q = t * RING + g
                    dve.wait_ge(gathered[g], t * (16 * GROUP) + 16 * GROUP)
                    nc.vector.tensor_scalar(idx[:, g * GROUP:(g + 1) * GROUP], c.idx_typed[:, bass.ds((q + RING) * GROUP, GROUP)],
                                            0, None, ALU.add).then_inc(idx_ready, 1)
                    dve.wait_ge(fetched, done(q))
                    dve.wait_ge(scores_ready, before(q, 2))
                    nc.vector.tensor_tensor(product[:, g % 2], rows[:, g, :, 0:D],
                                            c.banks[g][:, :].rearrange("p (u d) -> p u d", d=D),
                                            ALU.mult).then_inc(product_ready, 1)
                    dve.wait_ge(product_ready, done(q))
                    dve.wait_ge(scores_out, before(q, 2))
                    nc.vector.tensor_reduce(scores[:, g % 2].rearrange("p u h -> p (u h)"),
                                            product[:, g % 2].rearrange("p u (h k) -> p (u h) k", h=H8),
                                            AX.X, ALU.add).then_inc(scores_ready, 1)
                    dve.wait_ge(scores_ready, done(q))
                    nc.vector.tensor_scalar(c.logits[:, :, bass.ds(q * GROUP, GROUP)], scores[:, g % 2].rearrange("p u h -> p h u"),
                                            0.0, None, ALU.add).then_inc(scores_out, 1)

        @block.tensor
        def _(pe):
            pe.sem_inc(fetched, RING)
            with pe.Fori(0, TRIPS) as t:
                for g in range(RING):
                    q = t * RING + g
                    js = load_windows(nc, c, pe, q)
                    pe.wait_ge(onehot_ready, done(q))
                    pe.wait_ge(product_ready, before(q))
                    for u in range(GROUP):
                        for k in range(3):
                            last = nc.tensor.matmul(in_bank(c.banks[g], u, D), in_bank(onehot_t[:, g], u, P),
                                                    parts[k][:, js[u], :], start=k == 0, stop=k == 2)
                    last.then_inc(fetched, 1)


def pass_a_relational(nc, c, table, z_parts, dst_parts, y_w, rel_count):
    with ExitStack() as st:
        def sb(name, shape, dt=F32):
            return st.enter_context(nc.sbuf_tensor(unique(c, name), shape, dt))

        rows = sb("rows", [P, RING, GROUP, 2 * D])
        values = sb("values", [P, RING, GROUP, D])
        idx = sb("idx", [P, RING * GROUP], I32)
        edge_row = sb("edge_row", [P, RING, 2, GROUP * P], BF16)
        onehot = sb("onehot", [P, RING, GROUP, P], BF16)
        onehot_t = sb("onehot_t", [P, RING, GROUP * P], BF16)
        rel_hot = sb("rel_hot", [P, RING, GROUP, RELS], BF16)
        rel_hot_t = sb("rel_hot_t", [HALF_RELS, RING, 2, GROUP * P], BF16)
        sloped = sb("sloped", [P, 2, GROUP * P])
        leaky = sb("leaky", [P, 2, GROUP * P])
        row_in = [st.enter_context(semaphore(nc, c, f"row_in{g}")) for g in range(RING)]
        gathered = [st.enter_context(semaphore(nc, c, f"gathered{g}")) for g in range(RING)]
        stored = [st.enter_context(semaphore(nc, c, f"stored{g}")) for g in range(RING)]
        idx_ready = st.enter_context(semaphore(nc, c, "idx_ready"))
        issue = st.enter_context(semaphore(nc, c, "issue"))
        added = st.enter_context(semaphore(nc, c, "counts_added"))
        cleared = st.enter_context(semaphore(nc, c, "counts_cleared"))
        hots_ready = st.enter_context(semaphore(nc, c, "hots_ready"))
        pre_ready = st.enter_context(semaphore(nc, c, "pre_ready"))
        sloped_ready = st.enter_context(semaphore(nc, c, "sloped_ready"))
        leaky_ready = st.enter_context(semaphore(nc, c, "leaky_ready"))
        rel_values = st.enter_context(semaphore(nc, c, "rel_values"))
        values_ready = st.enter_context(semaphore(nc, c, "values_ready"))
        counted = st.enter_context(semaphore(nc, c, "rel_counted"))
        scored = st.enter_context(semaphore(nc, c, "scored"))
        logits_out = st.enter_context(semaphore(nc, c, "logits_written"))
        block = st.enter_context(nc.Block())
        pre_banks, value_banks, count_banks, logit_banks = (c.banks[k:k + 2] for k in (0, 2, 4, 6))

        @block.gpsimd
        def _(pool):
            with pool.Fori(0, TRIPS) as t:
                for g in range(RING):
                    q = t * RING + g
                    pool.wait_ge(idx_ready, q + 1)
                    pool.wait_ge(values_ready, before(q))
                    pool.wait_ge(pre_ready, before(q))
                    pool.sem_inc(issue, 1)
                    gather_group(nc, rows, g, table, idx, gathered[g])

        @block.sync
        def _(sp):
            for g in range(RING):
                sp.sem_inc(stored[g], 16)

            def load(q, g):
                sp.wait_ge(hots_ready, before(q))
                for b, source in enumerate((c.dst_rows, c.relation_rows)):
                    load_row(c, sp, edge_row[:, g, b], source, q).then_inc(row_in[g], 16)

            sp.wait_ge(c.edge_rows_out, 64)
            load(0, 0)
            load(1, 1)
            with sp.Fori(0, TRIPS) as t:
                for g in range(RING):
                    q = t * RING + g
                    load(q + 2, (g + 2) % RING)
                    sp.wait_ge(values_ready, done(q))
                    sp.sem_inc(issue, 1)
                    sp.dma_start(c.stash.rearrange("p (s d) -> p s d", d=D)[:, bass.ds(q * GROUP, GROUP), :],
                                 values[:, g]).then_inc(stored[g], 16)
            for g in range(2):
                sp.wait_ge(row_in[g], 32 * (TRIPS + 1))
            for g in range(RING):
                sp.wait_ge(stored[g], 16 * (TRIPS + 1))

        @block.vector
        def _(dve):
            nc.vector.memset(rel_count[:], 0.0).then_inc(cleared, 1)
            for sem in (values_ready, hots_ready, leaky_ready):
                dve.sem_inc(sem, RING)
            dve.sem_inc(added, 2 * GROUP)
            dve.wait_ge(cleared, 1)
            nc.vector.tensor_copy(idx[:], c.idx_src[:, 0:RING * GROUP]).then_inc(idx_ready, RING)

            def relation_hots(q, g):
                dve.wait_ge(counted, before(q))
                nc.vector.tensor_tensor(rel_hot[:, g], c.iota[:, 0:RELS].unsqueeze(1).to_broadcast([P, GROUP, RELS]),
                                        c.relation[:, bass.ds(q * GROUP, GROUP)].unsqueeze(2).to_broadcast([P, GROUP, RELS]),
                                        ALU.is_equal)

            def transposed_relation_hots(q, g, loads):
                dve.wait_ge(rel_values, before(q))
                dve.wait_ge(row_in[g], loads)
                for half in range(2):
                    compare_row(nc, c, rel_hot_t[:, g, half], edge_row[0:HALF_RELS, g, 1], half)

            def transposed_hots(g):
                compare_row(nc, c, onehot_t[:, g], edge_row[:, g, 0]).then_inc(hots_ready, 1)

            def add_counts(q, u, j):
                dve.wait_ge(added, q * GROUP + u + 2 * GROUP)
                nc.vector.tensor_tensor(rel_count[:, j, :], rel_count[:, j, :],
                                        in_bank(count_banks[u // 2], u % 2, RELS), ALU.add).then_inc(added, 1)

            relation_hots(0, 0)
            onehots_for_group(nc, c, onehot, 0, 0)
            transposed_relation_hots(0, 0, 32)
            transposed_hots(0)
            with dve.Fori(0, TRIPS) as t:
                for g in range(RING):
                    q = t * RING + g
                    g_next, loads = (g + 1) % RING, t * 32 + (32 if g + 1 < RING else 64)
                    js = load_windows(nc, c, dve, q)
                    dve.wait_ge(counted, done(q))
                    add_counts(q, 0, js[0])
                    relation_hots(q + 1, g_next)
                    add_counts(q, 1, js[1])
                    onehots_for_group(nc, c, onehot, g_next, q + 1)
                    add_counts(q, 2, js[2])
                    transposed_relation_hots(q + 1, g_next, loads)
                    add_counts(q, 3, js[3])
                    transposed_hots(g_next)
                    dve.wait_ge(gathered[g], t * (16 * GROUP) + 16 * GROUP)
                    nc.vector.tensor_scalar(idx[:, g * GROUP:(g + 1) * GROUP], c.idx_src[:, bass.ds((q + RING) * GROUP, GROUP)],
                                            0, None, ALU.add).then_inc(idx_ready, 1)
                    dve.wait_ge(sloped_ready, done(q))
                    dve.wait_ge(scored, before(q, 2))
                    nc.vector.tensor_tensor(leaky[:, g % 2], sloped[:, g % 2], pre_banks[g % 2], ALU.max).then_inc(leaky_ready, 1)
                    dve.wait_ge(rel_values, done(q))
                    dve.wait_ge(stored[g], t * 16 + 16)
                    nc.vector.tensor_tensor(values[:, g], rows[:, g, :, D:2 * D],
                                            value_banks[g % 2].rearrange("p (u d) -> p u d", d=D),
                                            ALU.add).then_inc(values_ready, 1)

        @block.tensor
        def _(pe):
            for sem in (pre_ready, rel_values, counted, scored):
                pe.sem_inc(sem, RING)

            def score(t, g):
                q = t * RING + g
                pe.wait_ge(leaky_ready, done(q))
                pe.wait_ge(logits_out, before(q, 2))
                for u in range(GROUP):
                    last = nc.tensor.matmul(in_bank(logit_banks[g % 2], u, H8), in_bank(leaky[:, g % 2], u, P), y_w,
                                            start=True, stop=True)
                last.then_inc(scored, 1)

            with pe.Fori(0, TRIPS) as t:
                for g in range(RING):
                    q = t * RING + g
                    js = load_windows(nc, c, pe, q)
                    pe.wait_ge(hots_ready, done(q))
                    pe.wait_ge(added, q * GROUP + 2 * GROUP)
                    for u in range(GROUP):
                        last = nc.tensor.matmul(in_bank(count_banks[u // 2], u % 2, RELS), onehot[:, g, u, :],
                                                rel_hot[:, g, u, :], start=True, stop=True)
                    last.then_inc(counted, 1)
                    pe.wait_ge(leaky_ready, before(q, 2))
                    pe.wait_ge(gathered[g], t * (16 * GROUP) + 16 * GROUP)
                    for u in range(GROUP):
                        pre = in_bank(pre_banks[g % 2], u, P)
                        nc.tensor.matmul(pre, rows[:, g, u, 0:D], c.ident[:], start=True, stop=False)
                        for b in range(2):
                            for k in range(3):
                                nc.tensor.matmul(pre, z_parts[k][:, b, 0:D], in_bank(rel_hot_t[:, g, b], u, P), start=False, stop=False)
                        for k in range(3):
                            last = nc.tensor.matmul(pre, dst_parts[k][:, js[u], :], in_bank(onehot_t[:, g], u, P),
                                                    start=False, stop=k == 2)
                    last.then_inc(pre_ready, 1)
                    pe.wait_ge(values_ready, before(q, 2))
                    for u in range(GROUP):
                        for b in range(2):
                            for k in range(3):
                                last = nc.tensor.matmul(in_bank(value_banks[g % 2], u, D), in_bank(rel_hot_t[:, g, b], u, P),
                                                        z_parts[k][:, b, D:2 * D], start=b + k == 0, stop=b + k == 3)
                    last.then_inc(rel_values, 1)
                    if g:
                        score(t, g - 1)
                score(t, RING - 1)

        @block.scalar
        def _(act):
            act.sem_inc(logits_out, RING)
            act.sem_inc(sloped_ready, RING)

            def take_logits(t, g):
                q = t * RING + g
                act.wait_ge(scored, done(q))
                act.sem_inc(issue, 1)
                nc.scalar.copy(c.logits[:, :, bass.ds(q * GROUP, GROUP)],
                               logit_banks[g % 2][:, 0:GROUP * H8].rearrange("p (u h) -> p h u", h=H8)).then_inc(logits_out, 1)

            with act.Fori(0, TRIPS) as t:
                for g in range(RING):
                    q = t * RING + g
                    act.wait_ge(pre_ready, done(q))
                    act.wait_ge(leaky_ready, before(q, 2))
                    nc.scalar.activation(sloped[:, g % 2], pre_banks[g % 2], ACT.Copy, scale=SLOPE).then_inc(sloped_ready, 1)
                    if g:
                        take_logits(t, g - 1)
                take_logits(t, RING - 1)



def self_terms(nc, c, a, rel_count, z_rows, deg, dst_term, terms, resid):
    with nc.sbuf_tensor(unique(c, "count_t"), [HALF_RELS, 2, 2, P], F32) as count_t, \
            semaphore(nc, c, "counts_turned") as turned, semaphore(nc, c, "counts_copied") as copied, \
            semaphore(nc, c, "window_ready") as window_ready, semaphore(nc, c, "window_taken") as window_taken, \
            semaphore(nc, c, "terms_in") as terms_in, semaphore(nc, c, "vec_done") as vec_done, nc.Block() as block:

        def turned_bank(w):
            return c.banks[w % 2][0:HALF_RELS, 0:2 * P]

        @block.tensor
        def _(pe):
            def turn(w):
                if w >= 2:
                    pe.wait_ge(copied, w - 1)
                for b in range(2):
                    last = nc.tensor.transpose(turned_bank(w)[:, b * P:(b + 1) * P],
                                               rel_count[:, w, b * HALF_RELS:(b + 1) * HALF_RELS], c.ident[:])
                last.then_inc(turned, 1)

            turn(0)
            for w in range(WINDOWS):
                if w + 1 < WINDOWS:
                    turn(w + 1)
                pe.wait_ge(copied, w + 1)
                if w >= 4:
                    pe.wait_ge(window_taken, w - 3)
                for b in range(2):
                    last = nc.tensor.matmul(c.banks[4 + w % 4][:, 0:2 * D], count_t[:, w % 2, b, :], z_rows[:, b, :],
                                            start=b == 0, stop=b == 1)
                last.then_inc(window_ready, 1)

        @block.scalar
        def _(act):
            for w in range(WINDOWS):
                act.wait_ge(turned, w + 1)
                if w >= 2:
                    act.wait_ge(window_ready, w - 1)
                nc.scalar.copy(count_t[:, w % 2].rearrange("p b n -> p (b n)"), turned_bank(w)).then_inc(copied, 1)

        @block.sync
        def _(sp):
            sp.dma_start(terms[:], c.rel_src_table.rearrange("(w n) d -> n w d", n=P)).then_inc(terms_in, 16)
            sp.dma_start(dst_term[:], c.rel_dst_table.rearrange("(w n) d -> n w d", n=P)).then_inc(terms_in, 16)
            sp.dma_start(resid[:], a["L0_gnn_residual_weight"].partition_broadcast(P)).then_inc(terms_in, 16)
            sp.wait_ge(terms_in, 48)

        @block.vector
        def _(dve):
            chain = Chain(dve, vec_done)
            chain(nc.vector.tensor_reduce(c.mean[:], rel_count[:], AX.X, ALU.add))
            chain(nc.vector.tensor_single_scalar(deg[:, :, 1], c.mean[:], 0.0, ALU.is_gt))
            chain(nc.vector.tensor_single_scalar(c.mean[:], c.mean[:], 1.0, ALU.max))
            chain(nc.vector.reciprocal(deg[:, :, 0], c.mean[:]))
            dve.wait_ge(terms_in, 48)
            chain(nc.vector.tensor_tensor(terms[:, :, 0:D], terms[:, :, 0:D], dst_term[:], ALU.add))
            for w in range(WINDOWS):
                dve.wait_ge(window_ready, w + 1)
                nc.vector.scalar_tensor_tensor(terms[:, w, :], c.banks[4 + w % 4][:, 0:2 * D], deg[:, w, 0:1],
                                               terms[:, w, :], ALU.mult, ALU.add).then_inc(window_taken, 1)
            dve.wait_ge(window_taken, WINDOWS)
            nc.vector.scalar_tensor_tensor(dst_term[:], terms[:, :, 0:D], SLOPE, terms[:, :, 0:D], ALU.mult, ALU.max)


def layer0(nc, c, a):
    wide = [P, WINDOWS, D]
    with ExitStack() as st:
        def sb(name, shape, dt=F32):
            return st.enter_context(nc.sbuf_tensor(unique(c, name), shape, dt))

        rel_count = sb("rel_count", [P, WINDOWS, RELS])
        z_rows = sb("z_rows", [HALF_RELS, 2, 2 * D])
        y_w = sb("y_w", [D, H8])
        c.acc = sb("acc", [P, WINDOWS, D + 2 * H8])
        with ExitStack() as inner:
            def sbi(name, shape, dt=F32):
                return inner.enter_context(nc.sbuf_tensor(unique(c, name), shape, dt))
            parts = [sbi(f"dst_part{k}", [P, WINDOWS, D], BF16) for k in range(3)]
            z_parts = [sbi(f"z_part{k}", [HALF_RELS, 2, 2 * D], BF16) for k in range(3)]
            with ExitStack() as pre:
                def sbp(name, shape, dt=F32):
                    return pre.enter_context(nc.sbuf_tensor(unique(c, name), shape, dt))
                c.h_t = sbp("h_t", [D, N_PAD])
                w_node = sbp("w_node", [D, 3, D])
                w_rel = sbp("w_rel", [D, 2, D])
                z = sbp("z", [RELS // 2, 2, D])
                z_t = sbp("z_t", [D, RELS])
                proj = sbp("proj", [P, WINDOWS, 3 * D])
                with semaphore(nc, c, "weights_in") as weights_in, nc.Block() as block:
                    @block.sync
                    def _(sp):
                        for to, source in ((w_node[:, 0], a["L0_gnn_P_w"][D:2 * D, :]), (w_node[:, 1], a["L0_gnn_Wc_w"][0:D, :]),
                                           (w_node[:, 2], a["L0_gnn_P_w"][0:D, :]), (w_rel[:, 0], a["L0_gnn_P_w"][2 * D:3 * D, :]),
                                           (w_rel[:, 1], a["L0_gnn_Wc_w"][D:2 * D, :]), (y_w[:], a["L0_gnn_y_w"]),
                                           (z[:], a["L0_gnn_z"].rearrange("(b r) d -> r b d", b=2))):
                            sp.dma_start(to, source).then_inc(weights_in, 16)
                        sp.wait_ge(weights_in, 16 * 7)
                transpose_windows(nc, c, c.h, c.h_t)
                project(nc, c, w_node[:].rearrange("p k d -> p (k d)"), 3 * D, proj)
                with semaphore(nc, c, "z_turned") as z_turned, semaphore(nc, c, "z_t_ready") as z_t_ready, \
                        semaphore(nc, c, "z_projected") as z_projected, semaphore(nc, c, "z_rows_ready") as z_rows_ready, \
                        semaphore(nc, c, "vec_done") as vec_done, semaphore(nc, c, "tables_out") as tables_out, nc.Block() as block:
                    @block.tensor
                    def _(pe):
                        for b in range(2):
                            last = nc.tensor.transpose(c.banks[0][:, b * 100:(b + 1) * 100], z[:, b, :], c.ident[0:100, 0:100])
                        last.then_inc(z_turned, 1)
                        pe.wait_ge(z_t_ready, 1)
                        for b in range(2):
                            last = nc.tensor.matmul(c.banks[1 + b][0:100, 0:2 * D], z_t[:, b * 100:(b + 1) * 100],
                                                    w_rel[:].rearrange("p k d -> p (k d)"), start=True, stop=True)
                        last.then_inc(z_projected, 1)

                    @block.scalar
                    def _(act):
                        act.wait_ge(z_turned, 1)
                        nc.scalar.copy(z_t[:], c.banks[0][:, 0:RELS]).then_inc(z_t_ready, 1)
                        act.wait_ge(z_projected, 1)
                        for b in range(2):
                            nc.scalar.copy(z_rows[:, b, 0:2 * D], c.banks[1 + b][0:100, 0:2 * D]).then_inc(z_rows_ready, 1)

                    @block.vector
                    def _(dve):
                        chain = Chain(dve, vec_done)
                        split_three(nc, chain, proj[:, :, 2 * D:3 * D], [p[:] for p in parts], c.wide_a[:])
                        dve.wait_ge(z_rows_ready, 2)
                        split_three(nc, chain, z_rows[:], [p[:] for p in z_parts],
                                    c.wide_a[0:HALF_RELS, 0:4, :].rearrange("p (b k) d -> p b (k d)", b=2))

                    @block.sync
                    def _(sp):
                        for k, (table, lo, hi) in enumerate(((c.rel_src_table, 0, 2 * D), (c.rel_dst_table, 2 * D, 3 * D))):
                            sp.dma_start(table.rearrange("(w n) d -> n w d", n=P), proj[:, :, lo:hi]).then_inc(tables_out, 16)
                        sp.wait_ge(tables_out, 32)
            attention(nc, c, H8, lambda: pass_a_relational(nc, c, c.rel_src_table, z_parts, parts, y_w[:], rel_count))
        with ExitStack() as fin:
            def sbf(name, shape, dt=F32):
                return fin.enter_context(nc.sbuf_tensor(unique(c, name), shape, dt))
            c.h_t = sbf("pre_self_t", [D, N_PAD])
            src_terms = sbf("src_terms", [P, WINDOWS, 2 * D])
            dst_term = sbf("dst_term", [P, WINDOWS, D])
            resid = sbf("resid", [P, 1])
            small = [sbf(f"small{k}", [P, WINDOWS, H8]) for k in range(5)]
            deg = sbf("deg", [P, WINDOWS, 2])
            self_terms(nc, c, a, rel_count, z_rows, deg, dst_term, src_terms, resid)
            transpose_windows(nc, c, dst_term, c.h_t)
            with semaphore(nc, c, "self_scored") as self_scored, semaphore(nc, c, "args_ready") as args_ready, \
                    semaphore(nc, c, "exps_ready") as exps_ready, semaphore(nc, c, "vec_done") as vec_done, \
                    semaphore(nc, c, "h_added") as h_added, nc.Block() as block:
                m_e, self_e, top, f, g = small
                scores = c.banks[0][:, 0:WINDOWS * H8].rearrange("p (w h) -> p w h", h=H8)

                @block.gpsimd
                def _(pool):
                    nc.gpsimd.tensor_tensor(c.x[:], c.x[:], c.h[:], ALU.add).then_inc(h_added, 1)

                @block.tensor
                def _(pe):
                    for w in range(WINDOWS):
                        last = nc.tensor.matmul(c.banks[0][:, w * H8:(w + 1) * H8], c.h_t[:, w * P:(w + 1) * P], y_w[:],
                                                start=True, stop=True)
                    last.then_inc(self_scored, 1)

                @block.scalar
                def _(act):
                    act.wait_ge(args_ready, 1)
                    nc.scalar.activation(f[:], f[:], ACT.Exp)
                    nc.scalar.activation(g[:], g[:], ACT.Exp).then_inc(exps_ready, 1)

                @block.vector
                def _(dve):
                    chain = Chain(dve, vec_done)
                    chain(nc.vector.tensor_scalar(m_e[:], deg[:, :, 1:2].to_broadcast([P, WINDOWS, H8]), 1.0, BIG,
                                                  ALU.subtract, ALU.mult))
                    chain(nc.vector.tensor_tensor(m_e[:], m_e[:], c.acc[:, :, D + H8:D + 2 * H8], ALU.add))
                    dve.wait_ge(self_scored, 1)
                    chain(nc.vector.tensor_copy(self_e[:], scores))
                    chain(nc.vector.tensor_tensor(top[:], m_e[:], self_e[:], ALU.max))
                    chain(nc.vector.tensor_tensor(f[:], m_e[:], top[:], ALU.subtract))
                    nc.vector.tensor_tensor(g[:], self_e[:], top[:], ALU.subtract).then_inc(args_ready, 1)
                    dve.wait_ge(exps_ready, 1)
                    chain(nc.vector.tensor_tensor(top[:], c.acc[:, :, D:D + H8], f[:], ALU.mult))
                    chain(nc.vector.tensor_tensor(top[:], top[:], g[:], ALU.add))
                    chain(nc.vector.reciprocal(top[:], top[:]))
                    chain(nc.vector.tensor_tensor(f[:], f[:], top[:], ALU.mult))
                    chain(nc.vector.tensor_tensor(g[:], g[:], top[:], ALU.mult))
                    for v, by in ((c.acc[:, :, 0:D], f), (src_terms[:, :, D:2 * D], g)):
                        v4 = v.rearrange("p w (h k) -> p w h k", h=H8)
                        for w in range(WINDOWS):
                            last = nc.vector.tensor_tensor(v4[:, w], v4[:, w],
                                                           by[:, w, :].unsqueeze(2).to_broadcast([P, H8, D // H8]), ALU.mult)
                        chain(last)
                    out = c.wide_a
                    chain(nc.vector.tensor_tensor(out[:], c.acc[:, :, 0:D], src_terms[:, :, D:2 * D], ALU.add))
                    chain(nc.vector.scalar_tensor_tensor(out[:], c.h[:], resid[:], out[:], ALU.mult, ALU.add))
                    chain(nc.vector.scalar_tensor_tensor(out[:], out[:], SLOPE, out[:], ALU.mult, ALU.max))
                    chain(nc.vector.tensor_tensor(out[:], out[:], c.h[:], ALU.subtract))
                    chain(nc.vector.tensor_tensor(out[:], out[:], deg[:, :, 1:2].to_broadcast(wide), ALU.mult))
                    dve.wait_ge(h_added, 1)
                    chain(nc.vector.tensor_tensor(c.x[:], c.x[:], out[:], ALU.add))



def gat_node_phase(nc, c, weights, transpose_weights, att_src, att_dst, rows, a_dst, parts):
    with ExitStack() as st:
        w_in = st.enter_context(nc.sbuf_tensor(unique(c, "w_in"), [D, D], F32))
        w_use = st.enter_context(nc.sbuf_tensor(unique(c, "w_use"), [D, D + 2 * H4], F32))
        product = st.enter_context(nc.sbuf_tensor(unique(c, "product"), [D, 2, D], F32))
        att = st.enter_context(nc.sbuf_tensor(unique(c, "att"), [P, 2, D], F32))
        normalise(nc, c)
        with semaphore(nc, c, "weights_in") as weights_in, semaphore(nc, c, "w_turned") as w_turned, \
                semaphore(nc, c, "vec_done") as vec_done, nc.Block() as block:
            @block.sync
            def _(sp):
                sp.dma_start(w_in[:], weights).then_inc(weights_in, 16)
                sp.dma_start(att[:, 0, :], att_src.partition_broadcast(P)).then_inc(weights_in, 16)
                sp.dma_start(att[:, 1, :], att_dst.partition_broadcast(P)).then_inc(weights_in, 16)
                sp.wait_ge(weights_in, 48)

            @block.tensor
            def _(pe):
                pe.wait_ge(weights_in, 48)
                nc.tensor.transpose(c.banks[0][:, 0:D], w_in[:], c.ident[:]).then_inc(w_turned, 1)

            @block.vector
            def _(dve):
                chain = Chain(dve, vec_done)
                dve.wait_ge(w_turned, 1)
                chain(nc.vector.tensor_copy(w_use[:, 0:D], c.banks[0][:, 0:D] if transpose_weights else w_in[:]))
                chain(nc.vector.tensor_tensor(product[:], w_use[:, 0:D].unsqueeze(1).to_broadcast([D, 2, D]), att[:], ALU.mult))
                nc.vector.tensor_reduce(w_use[:, D:D + 2 * H4], product[:].rearrange("p a (h k) -> p (a h) k", h=H4), AX.X, ALU.add)
        transpose_windows(nc, c, c.h, c.h_t)
        project(nc, c, w_use[:], D + 2 * H4, rows)
        with semaphore(nc, c, "vec_done") as vec_done, semaphore(nc, c, "table_out") as table_out, nc.Block() as block:
            @block.vector
            def _(dve):
                split_three(nc, Chain(dve, vec_done), a_dst, [parts[:, :, k * H4:(k + 1) * H4] for k in range(3)],
                            c.wide_a[:, :, 0:H4])

            @block.sync
            def _(sp):
                sp.dma_start(c.gat_table.rearrange("(w n) d -> n w d", n=P), rows[:, :, 0:GAT_ROW]).then_inc(table_out, 16)
                sp.wait_ge(table_out, 16)


def gat_logits(nc, c, weighted):
    with semaphore(nc, c, "vec_done") as vec_done, nc.Block() as block:
        @block.vector
        def _(dve):
            chain = Chain(dve, vec_done)
            lg = c.logits[:, 0:H4, :]
            chain(nc.vector.scalar_tensor_tensor(lg, lg, SLOPE, lg, ALU.mult, ALU.max))
            if weighted:
                chain(nc.vector.tensor_tensor(lg, lg, c.weight[:].unsqueeze(1).to_broadcast([P, H4, STEPS]), ALU.mult))


def scale_heads(nc, chain, v, by, heads):
    v4 = v.rearrange("p w (h k) -> p w h k", h=heads)
    for w in range(WINDOWS):
        last = nc.vector.tensor_tensor(v4[:, w], v4[:, w],
                                       by[:, w, :].unsqueeze(2).to_broadcast([P, heads, D // heads]), ALU.mult)
    chain(last)


def layer1(nc, c, a):
    wide = [P, WINDOWS, D]
    with ExitStack() as st:
        def sb(name, shape, dt=F32):
            return st.enter_context(nc.sbuf_tensor(unique(c, name), shape, dt))
        rows = sb("gat_rows", [P, WINDOWS, GAT_ROW + H4])
        a_dst = rows[:, :, GAT_ROW:GAT_ROW + H4]
        parts = sb("dst_parts", [P, WINDOWS, 3 * H4], BF16)
        small = [sb(f"small{k}", [P, WINDOWS, H4]) for k in range(5)]
        vecs = sb("vecs", [P, 3, D])
        stat = sb("stat", [P, 2, D])
        c.h_t = sb("h_t", [D, N_PAD])
        c.acc = sb("acc", [P, WINDOWS, D + 2 * H4])
        gat_node_phase(nc, c, a["L1_gnn_W"], False, a["L1_gnn_att_src"].rearrange("h k -> (h k)"),
                       a["L1_gnn_att_dst"].rearrange("h k -> (h k)"), rows, a_dst, parts)
        attention(nc, c, H4, lambda: pass_a_gat(nc, c, c.gat_table, parts, weighted=False))
        with semaphore(nc, c, "vecs_in") as vecs_in, semaphore(nc, c, "args_ready") as args_ready, \
                semaphore(nc, c, "exps_ready") as exps_ready, semaphore(nc, c, "vec_done") as vec_done, \
                semaphore(nc, c, "sums_wanted") as sums_wanted, semaphore(nc, c, "sums_ready") as sums_ready, \
                semaphore(nc, c, "var_ready") as var_ready, semaphore(nc, c, "dev_ready") as dev_ready, nc.Block() as block:
            m_e, self_e, top, f, g = small
            out = c.wide_a

            @block.sync
            def _(sp):
                for k, v in enumerate((a["L1_gnn_bias"], a["L1_gnn_gamma"], a["L1_gnn_beta"])):
                    sp.dma_start(vecs[:, k, :], v.partition_broadcast(P)).then_inc(vecs_in, 16)
                sp.wait_ge(vecs_in, 48)

            @block.tensor
            def _(pe):
                for k, source in enumerate((out, c.h)):
                    pe.wait_ge(sums_wanted, k + 1)
                    for w in range(WINDOWS):
                        rows_in = P if w < WINDOWS - 1 else LAST_NODES
                        last = nc.tensor.matmul(c.banks[k][:, 0:D], c.ones[0:rows_in, :], source[0:rows_in, w, :],
                                                start=w == 0, stop=w == WINDOWS - 1)
                    last.then_inc(sums_ready, 1)

            @block.scalar
            def _(act):
                act.wait_ge(args_ready, 1)
                nc.scalar.activation(f[:], f[:], ACT.Exp)
                nc.scalar.activation(g[:], g[:], ACT.Exp).then_inc(exps_ready, 1)
                act.wait_ge(var_ready, 1)
                nc.scalar.activation(stat[:, 1, :], stat[:, 1, :], ACT.Sqrt).then_inc(dev_ready, 1)
                act.wait_ge(args_ready, 2)
                nc.scalar.activation(c.h[:], c.h[:], ACT.Exp).then_inc(exps_ready, 1)

            @block.vector
            def _(dve):
                chain = Chain(dve, vec_done)
                chain(nc.vector.tensor_tensor(self_e[:], a_dst, rows[:, :, D:D + H4], ALU.add))
                chain(nc.vector.scalar_tensor_tensor(self_e[:], self_e[:], SLOPE, self_e[:], ALU.mult, ALU.max))
                chain(nc.vector.tensor_scalar(m_e[:], c.acc[:, :, D:D + H4], 0.5, -BIG, ALU.is_lt, ALU.mult))
                chain(nc.vector.tensor_tensor(m_e[:], m_e[:], c.acc[:, :, D + H4:D + 2 * H4], ALU.add))
                chain(nc.vector.tensor_tensor(top[:], m_e[:], self_e[:], ALU.max))
                chain(nc.vector.tensor_tensor(f[:], m_e[:], top[:], ALU.subtract))
                nc.vector.tensor_tensor(g[:], self_e[:], top[:], ALU.subtract).then_inc(args_ready, 1)
                dve.wait_ge(exps_ready, 1)
                chain(nc.vector.tensor_tensor(top[:], c.acc[:, :, D:D + H4], f[:], ALU.mult))
                chain(nc.vector.tensor_tensor(top[:], top[:], g[:], ALU.add))
                chain(nc.vector.tensor_single_scalar(top[:], top[:], 1e-16, ALU.add))
                chain(nc.vector.reciprocal(top[:], top[:]))
                chain(nc.vector.tensor_tensor(f[:], f[:], top[:], ALU.mult))
                chain(nc.vector.tensor_tensor(g[:], g[:], top[:], ALU.mult))
                scale_heads(nc, chain, c.acc[:, :, 0:D], f, H4)
                scale_heads(nc, chain, rows[:, :, 0:D], g, H4)
                chain(nc.vector.tensor_tensor(out[:], c.acc[:, :, 0:D], rows[:, :, 0:D], ALU.add))
                dve.wait_ge(vecs_in, 48)
                nc.vector.tensor_tensor(out[:], out[:], vecs[:, 0:1, :].to_broadcast(wide), ALU.add).then_inc(sums_wanted, 1)
                dve.wait_ge(sums_ready, 1)
                chain(nc.vector.tensor_single_scalar(stat[:, 0, :], c.banks[0][:, 0:D], 1.0 / N_NODES, ALU.mult))
                chain(nc.vector.tensor_tensor(out[:], out[:], stat[:, 0:1, :].to_broadcast(wide), ALU.subtract))
                nc.vector.tensor_tensor(c.h[:], out[:], out[:], ALU.mult).then_inc(sums_wanted, 1)
                dve.wait_ge(sums_ready, 2)
                nc.vector.tensor_scalar(stat[:, 1, :], c.banks[1][:, 0:D], 1.0 / N_NODES, 1e-5, ALU.mult,
                                        ALU.add).then_inc(var_ready, 1)
                dve.wait_ge(dev_ready, 1)
                chain(nc.vector.reciprocal(stat[:, 1, :], stat[:, 1, :]))
                chain(nc.vector.tensor_tensor(stat[:, 1, :], stat[:, 1, :], vecs[:, 1, :], ALU.mult))
                chain(nc.vector.tensor_tensor(out[:], out[:], stat[:, 1:2, :].to_broadcast(wide), ALU.mult))
                chain(nc.vector.tensor_tensor(out[:], out[:], vecs[:, 2:3, :].to_broadcast(wide), ALU.add))
                nc.vector.tensor_single_scalar(c.h[:], out[:], 0.0, ALU.min).then_inc(args_ready, 1)
                chain(nc.vector.scalar_tensor_tensor(out[:], out[:], 0.0, c.x[:], ALU.max, ALU.add))
                dve.wait_ge(exps_ready, 2)
                chain(nc.vector.scalar_tensor_tensor(c.x[:], c.h[:], -1.0, out[:], ALU.add, ALU.add))


def layer2(nc, c, a):
    with ExitStack() as st:
        def sb(name, shape, dt=F32):
            return st.enter_context(nc.sbuf_tensor(unique(c, name), shape, dt))
        rows = sb("gat_rows", [P, WINDOWS, GAT_ROW + H4])
        a_dst = rows[:, :, GAT_ROW:GAT_ROW + H4]
        parts = sb("dst_parts", [P, WINDOWS, 3 * H4], BF16)
        f = sb("f", [P, WINDOWS, H4])
        c.h_t = sb("h_t", [D, N_PAD])
        c.acc = sb("acc", [P, WINDOWS, D + 2 * H4])
        gat_node_phase(nc, c, a["L2_gnn_W"], True, a["L2_gnn_a_src"].rearrange("o h k -> (o h k)"),
                       a["L2_gnn_a_dst"].rearrange("o h k -> (o h k)"), rows, a_dst, parts)
        attention(nc, c, H4, lambda: pass_a_gat(nc, c, c.gat_table, parts, weighted=True))
        with semaphore(nc, c, "args_ready") as args_ready, semaphore(nc, c, "exps_ready") as exps_ready, \
                semaphore(nc, c, "vec_done") as vec_done, nc.Block() as block:
            @block.scalar
            def _(act):
                act.wait_ge(args_ready, 1)
                nc.scalar.activation(f[:], f[:], ACT.Exp).then_inc(exps_ready, 1)

            @block.vector
            def _(dve):
                chain = Chain(dve, vec_done)
                m_e, total = c.acc[:, :, D + H4:D + 2 * H4], c.acc[:, :, D:D + H4]
                nc.vector.tensor_single_scalar(f[:], m_e, 0.0, ALU.min).then_inc(args_ready, 1)
                dve.wait_ge(exps_ready, 1)
                chain(nc.vector.tensor_tensor(total, total, f[:], ALU.mult))
                chain(nc.vector.tensor_single_scalar(total, total, 1e-8, ALU.add))
                chain(nc.vector.reciprocal(total, total))
                chain(nc.vector.tensor_tensor(f[:], f[:], total, ALU.mult))
                scale_heads(nc, chain, c.acc[:, :, 0:D], f, H4)
                chain(nc.vector.tensor_tensor(c.x[:], c.x[:], c.acc[:, :, 0:D], ALU.add))



def node_coefficients(nc, c, chain, comp, mask, product, to):
    shape = [P, WINDOWS, 4, BASES]
    for ty in range(TYPES):
        chain(nc.vector.tensor_single_scalar(mask[:], c.node_type[:], float(ty), ALU.is_equal))
        term = to if ty == 0 else product
        chain(nc.vector.tensor_tensor(term[:], mask[:].unsqueeze(2).unsqueeze(3).to_broadcast(shape),
                                      comp[:, :, ty, :].unsqueeze(1).to_broadcast(shape), ALU.mult))
        if ty:
            chain(nc.vector.tensor_tensor(to[:], to[:], product[:], ALU.add))


def typed_projections(nc, c, basis, coef, jobs):
    many = len(jobs)
    with semaphore(nc, c, "bases_projected") as projected, semaphore(nc, c, "base_added") as base_added, nc.Block() as block:

        def after_base(w, b, m):
            return (w * BASES + b) * many + m + 1

        @block.tensor
        def _(pe):
            for w in range(WINDOWS):
                for m, (k, _to) in enumerate(jobs):
                    n = w * many + m
                    if n >= 8:
                        pe.wait_ge(base_added, after_base((n - 8) // many, BASES - 1, (n - 8) % many))
                    nc.tensor.matmul(c.banks[n % 8], c.h_t[:, w * P:(w + 1) * P], basis[:, k].rearrange("i b o -> i (b o)"),
                                     start=True, stop=True).then_inc(projected, 1)

        @block.vector
        def _(dve):
            for w in range(WINDOWS):
                for b in range(BASES):
                    for m, (k, to) in enumerate(jobs):
                        n = w * many + m
                        term, by = in_bank(c.banks[n % 8], b, D), coef[:, w, k, b:b + 1]
                        if b == 0:
                            dve.wait_ge(projected, n + 1)
                            last = nc.vector.tensor_scalar(to[:, w, :], term, by, None, ALU.mult)
                        else:
                            dve.wait_ge(base_added, after_base(w, b - 1, m))
                            last = nc.vector.scalar_tensor_tensor(to[:, w, :], term, by, to[:, w, :], ALU.mult, ALU.add)
                        last.then_inc(base_added, 1)


def layer3(nc, c, a):
    with ExitStack() as st:
        def sb(name, shape, dt=F32):
            return st.enter_context(nc.sbuf_tensor(unique(c, name), shape, dt))
        basis = sb("basis", [D, 4, BASES, D])
        coef = sb("coef", [P, WINDOWS, 4, BASES])
        loop_w = sb("loop_w", [D, D])
        bias = sb("bias", [P, D])
        c.node_type = sb("node_type", [P, WINDOWS])
        c.h_t = sb("h_t", [D, N_PAD])
        normalise(nc, c)
        with ExitStack() as inner:
            def sbi(name, shape, dt=F32):
                return inner.enter_context(nc.sbuf_tensor(unique(c, name), shape, dt))
            parts = [sbi(f"dst_part{k}", [P, WINDOWS, D], BF16) for k in range(3)]
            with ExitStack() as pre:
                def sbp(name, shape, dt=F32):
                    return pre.enter_context(nc.sbuf_tensor(unique(c, name), shape, dt))
                blocks = [sbp(f"blocks_{n}", [D, TYPES, D]) for n in ("att", "msg")]
                keys, values = sbp("keys", [P, WINDOWS, D]), sbp("values", [P, WINDOWS, D])
                k_t, v_t = sbp("k_t", [D, N_PAD]), sbp("v_t", [D, N_PAD])
                transpose_windows(nc, c, c.h, c.h_t)
                with ExitStack() as load:
                    def sbl(name, shape, dt=F32):
                        return load.enter_context(nc.sbuf_tensor(unique(c, name), shape, dt))
                    type_i = sbl("type_i", [WINDOWS, P], I32)
                    type_row = sbl("type_row", [WINDOWS, P])
                    comp = sbl("comp", [P, 4, TYPES, BASES])
                    mask = sbl("mask", [P, WINDOWS])
                    product = sbl("product", [P, WINDOWS, 4, BASES])
                    pri = sbl("pri", [P, TYPES, H8])
                    with semaphore(nc, c, "cleared") as cleared, semaphore(nc, c, "loaded") as loaded, \
                            semaphore(nc, c, "types_ready") as types_ready, semaphore(nc, c, "types_turned") as types_turned, \
                            semaphore(nc, c, "vec_done") as vec_done, nc.Block() as block:
                        comps = [a["L3_gnn_w_comp_k"], a["L3_gnn_w_comp_v"], a["L3_gnn_w_comp_q"], a["L3_gnn_w_comp_a"]]
                        bases = [a["L3_gnn_w_basis_k"], a["L3_gnn_w_basis_v"], a["L3_gnn_w_basis_q"], a["L3_gnn_w_basis_a"]]
                        N_LOADS = 2 + 8 + 16 + 1 + 2

                        @block.sync
                        def _(sp):
                            sp.wait_ge(cleared, 3)
                            whole = (WINDOWS - 1) * P
                            sp.dma_start(type_i[0:WINDOWS - 1, :],
                                         a["node_type_8"][0:whole].rearrange("(w n) -> w n", n=P)).then_inc(loaded, 16)
                            sp.dma_start(type_i[WINDOWS - 1:WINDOWS, 0:LAST_NODES],
                                         a["node_type_8"][whole:N_NODES].rearrange("(w n) -> w n", w=1)).then_inc(loaded, 16)
                            for k in range(4):
                                sp.dma_start(comp[:, k].rearrange("p t b -> p (t b)"),
                                             comps[k].rearrange("t b -> (t b)").partition_broadcast(P)).then_inc(loaded, 16)
                                sp.dma_start(basis[:, k], bases[k].rearrange("b (i o) -> i b o", o=D)).then_inc(loaded, 16)
                            hd = D // H8
                            for to, source in zip(blocks, (a["L3_gnn_relation_att"], a["L3_gnn_relation_msg"])):
                                for h in range(H8):
                                    sp.dma_start(to[h * hd:(h + 1) * hd, :, h * hd:(h + 1) * hd],
                                                 source[:, h].rearrange("t i j -> i t j")).then_inc(loaded, 16)
                            sp.dma_start(pri[:].rearrange("p t h -> p (t h)"),
                                         a["L3_gnn_relation_pri"].rearrange("t h -> (t h)").partition_broadcast(P)).then_inc(loaded, 16)
                            sp.dma_start(loop_w[:], a["L3_gnn_loop_weight"]).then_inc(loaded, 16)
                            sp.dma_start(bias[:], a["L3_gnn_bias"].partition_broadcast(P)).then_inc(loaded, 16)
                            sp.wait_ge(loaded, 16 * N_LOADS)

                        @block.tensor
                        def _(pe):
                            pe.wait_ge(types_ready, 1)
                            nc.tensor.transpose(c.banks[0][:, 0:WINDOWS], type_row[:], c.ident[0:WINDOWS, 0:WINDOWS]).then_inc(types_turned, 1)

                        @block.vector
                        def _(dve):
                            nc.vector.memset(type_i[:], 0).then_inc(cleared, 1)
                            for t in blocks:
                                nc.vector.memset(t[:], 0.0).then_inc(cleared, 1)
                            dve.wait_ge(loaded, 16 * N_LOADS)
                            chain = Chain(dve, vec_done)
                            nc.vector.tensor_copy(type_row[:], type_i[:]).then_inc(types_ready, 1)
                            dve.wait_ge(types_turned, 1)
                            chain(nc.vector.tensor_copy(c.node_type[:], c.banks[0][:, 0:WINDOWS]))
                            node_coefficients(nc, c, chain, comp, mask, product, coef)
                            chain(nc.vector.tensor_single_scalar(pri[:], pri[:], (D // H8) ** -0.5, ALU.mult))
                            for ty in range(TYPES):
                                b4 = blocks[0][:, ty, :].rearrange("p (h k) -> p h k", h=H8)
                                chain(nc.vector.tensor_tensor(b4, b4, pri[:, ty, :].unsqueeze(2).to_broadcast([P, H8, D // H8]),
                                                              ALU.mult))
                typed_projections(nc, c, basis, coef, [(0, keys), (1, values), (2, c.h)])
                transpose_windows(nc, c, keys, k_t)
                transpose_windows(nc, c, values, v_t)
                with ExitStack() as tab:
                    ring = tab.enter_context(nc.sbuf_tensor(unique(c, "ring"), [P, 2, TYPES, 2, D], F32))
                    with semaphore(nc, c, "half_ready") as half_ready, semaphore(nc, c, "half_taken") as half_taken, \
                            semaphore(nc, c, "half_taken_dve") as half_taken_dve, \
                            semaphore(nc, c, "rows_out0") as rows_out0, semaphore(nc, c, "rows_out1") as rows_out1, \
                            semaphore(nc, c, "vec_done") as vec_done, nc.Block() as block:
                        rows_out = [rows_out0, rows_out1]
                        quads = [(k, g) for k in range(2) for g in range(2)]

                        @block.tensor
                        def _(pe):
                            for w in range(WINDOWS):
                                for q, (k, g) in enumerate(quads):
                                    if w >= 2:
                                        pe.wait_ge(half_taken if k == 0 else half_taken_dve, 2 * (w - 2) + g + 1)
                                    nc.tensor.matmul(c.banks[(w % 2) * 4 + q][:, :], (k_t, v_t)[k][:, w * P:(w + 1) * P],
                                                     blocks[k][:, 4 * g:4 * g + 4, :].rearrange("p t d -> p (t d)"),
                                                     start=True, stop=True).then_inc(half_ready, 1)

                        @block.scalar
                        def _(act):
                            for w in range(WINDOWS):
                                if w >= 2:
                                    act.wait_ge(rows_out[w % 2], 16 * (w // 2))
                                for g in range(2):
                                    act.wait_ge(half_ready, 4 * w + g + 1)
                                    nc.scalar.copy(ring[:, w % 2, 4 * g:4 * g + 4, 0, :],
                                                   c.banks[(w % 2) * 4 + g][:, :].rearrange("p (t d) -> p t d", t=4)
                                                   ).then_inc(half_taken, 1)

                        @block.vector
                        def _(dve):
                            chain = Chain(dve, vec_done)
                            for w in range(WINDOWS):
                                if w >= 2:
                                    dve.wait_ge(rows_out[w % 2], 16 * (w // 2))
                                for g in range(2):
                                    dve.wait_ge(half_ready, 4 * w + 2 + g + 1)
                                    nc.vector.tensor_copy(ring[:, w % 2, 4 * g:4 * g + 4, 1, :],
                                                          c.banks[(w % 2) * 4 + 2 + g][:, :].rearrange("p (t d) -> p t d", t=4)
                                                          ).then_inc(half_taken_dve, 1)
                                if w % SPLIT_WINDOWS == 0:
                                    these = slice(w, min(w + SPLIT_WINDOWS, WINDOWS))
                                    split_three(nc, chain, c.h[:, these, :], [p[:, these, :] for p in parts], c.wide_a[:, these, :])

                        @block.sync
                        def _(sp):
                            for w in range(WINDOWS):
                                sp.wait_ge(half_taken, 2 * w + 2)
                                sp.wait_ge(half_taken_dve, 2 * w + 2)
                                sp.dma_start(c.typed_table[w * P * TYPES:(w + 1) * P * TYPES, :].rearrange("(n t) d -> n (t d)", t=TYPES),
                                             ring[:, w % 2].rearrange("p t k d -> p (t k d)")).then_inc(rows_out[w % 2], 16)
                            sp.wait_ge(rows_out[0], 16 * ((WINDOWS + 1) // 2))
                            sp.wait_ge(rows_out[1], 16 * (WINDOWS // 2))
            c.acc = sbi("acc", [P, WINDOWS, D + 2 * H8])
            attention(nc, c, H8, lambda: pass_a_hgt(nc, c, c.typed_table, parts))
            with ExitStack() as fin:
                hgt_output(nc, c, fin, basis, coef, loop_w, bias)

def hgt_output(nc, c, fin, basis, coef, loop_w, bias):
    rden = fin.enter_context(nc.sbuf_tensor(unique(c, "rden"), [P, WINDOWS, H8], F32))
    loop_term = fin.enter_context(nc.sbuf_tensor(unique(c, "loop_term"), [P, WINDOWS, D], F32))
    project(nc, c, loop_w[:], D, loop_term)
    with semaphore(nc, c, "vec_done") as vec_done, nc.Block() as block:
        @block.vector
        def _(dve):
            chain = Chain(dve, vec_done)
            chain(nc.vector.tensor_single_scalar(rden[:], c.acc[:, :, D:D + H8], 1e-30, ALU.max))
            chain(nc.vector.reciprocal(rden[:], rden[:]))
            scale_heads(nc, chain, c.acc[:, :, 0:D], rden, H8)
            chain(nc.vector.tensor_copy(c.h[:], c.acc[:, :, 0:D]))
    transpose_windows(nc, c, c.h, c.h_t)
    typed_projections(nc, c, basis, coef, [(3, c.wide_a)])
    with semaphore(nc, c, "vec_done") as vec_done, nc.Block() as block:
        @block.vector
        def _(dve):
            chain = Chain(dve, vec_done)
            o = c.wide_a
            chain(nc.vector.tensor_tensor(o[:], o[:], loop_term[:], ALU.add))
            chain(nc.vector.tensor_tensor(o[:], o[:], bias[:].unsqueeze(1).to_broadcast([P, WINDOWS, D]), ALU.add))
            chain(nc.vector.scalar_tensor_tensor(c.x[:], o[:], 0.0, c.x[:], ALU.max, ALU.add))


def store_output(nc, c, out):
    with semaphore(nc, c, "out_stored") as out_stored, nc.Block() as block:
        @block.sync
        def _(sp):
            whole = (WINDOWS - 1) * P
            sp.dma_start(out[0:whole, :].rearrange("(w n) d -> n w d", n=P), c.x[:, 0:WINDOWS - 1, :]).then_inc(out_stored, 16)
            sp.dma_start(out[whole:N_NODES, :], c.x[0:LAST_NODES, WINDOWS - 1, :]).then_inc(out_stored, 16)
            sp.wait_ge(out_stored, 32)


def build_program(nc, a, out, layers=4):
    c = State()
    with ExitStack() as st:
        def sb(name, shape, dt=F32):
            return st.enter_context(nc.sbuf_tensor(unique(c, name), shape, dt))

        c.psum = st.enter_context(nc.psum_tensor("psum", [P, 8, 512], F32))
        c.banks = [c.psum[:, k, :] for k in range(8)]
        c.x = sb("x_nodes", [P, WINDOWS, D])
        c.h = sb("h_nodes", [P, WINDOWS, D])
        c.wide_a = sb("wide_a", [P, WINDOWS, D])
        c.ident = sb("ident", [P, P])
        c.ones = sb("ones", [P, P])
        c.iota = sb("iota", [P, 512])
        c.down = sb("down", [P, 2])
        c.mean, c.rstd = sb("mean", [P, WINDOWS]), sb("rstd", [P, WINDOWS])
        c.window_i = sb("window_i", [1, STEPS], I32)
        c.dst_pad = sb("dst_local", [P, STEPS + GROUP])
        c.dst_local = c.dst_pad[:, 0:STEPS]
        c.outside = sb("outside", [P, STEPS])
        c.is_end = sb("is_end", [P, STEPS])
        c.weight = sb("weight", [P, STEPS])
        c.idx_src = sb("idx_src", [P, STEPS + RING * GROUP], I32)
        c.idx_typed = sb("idx_typed", [P, STEPS + RING * GROUP], I32)
        c.relation = sb("relation", [P, STEPS + GROUP])
        c.border = sb("border", [CH, NCH, P + 1])
        c.not_first = sb("not_first", [CH, NCH, P])
        c.not_last = sb("not_last", [CH, NCH, P])
        c.new_dst = sb("new_dst", [H8, STEPS + 1])
        c.stop_forward = sb("stop_forward", [H8, STEPS])
        c.stop_backward = sb("stop_backward", [H8, STEPS])
        c.row_parts = sb("row_parts", [CH, 2, NCH, P], BF16)
        c.row_pad = sb("row_pad", [2 * GROUP, P], BF16)
        c.x_loaded = nc.alloc_semaphore("x_loaded")
        c.edge_rows_out = nc.alloc_semaphore("edge_rows_out")
        c.dst_rows = nc.dram_tensor("dst_rows", [(STEPS + 2 * GROUP) * P], BF16, kind="Internal").ap()
        c.relation_rows = nc.dram_tensor("relation_rows", [(STEPS + 2 * GROUP) * P], BF16, kind="Internal").ap()
        load_constants(nc, c, a)
        build_steps(nc, c, a)
        store_edge_rows(nc, c)
        c.stash = nc.dram_tensor("stash", [P, STEPS * D], F32, kind="Internal").ap()
        c.rel_src_table = nc.dram_tensor("rel_src_table", [N_PAD, 2 * D], F32, kind="Internal").ap()
        c.rel_dst_table = nc.dram_tensor("rel_dst_table", [N_PAD, D], F32, kind="Internal").ap()
        c.gat_table = nc.dram_tensor("gat_table", [N_PAD, GAT_ROW], F32, kind="Internal").ap()
        c.typed_table = nc.dram_tensor("typed_table", [N_PAD * TYPES, 2 * D], F32, kind="Internal").ap()
        for n, layer in enumerate((layer0, layer1, layer2, layer3)[0:layers]):
            c.layer = f"layer{n}"
            layer(nc, c, a)
            clear_semaphores(nc, c)
        store_output(nc, c, out)


_INS = ['x', 'src', 'dst', 'edge_type_200', 'edge_type_8', 'edge_weight', 'node_type_8', 'L0_gnn_z', 'L0_gnn_Wc_w',
        'L0_gnn_P_w', 'L0_gnn_y_w', 'L0_gnn_residual_weight', 'L1_gnn_W', 'L1_gnn_att_src', 'L1_gnn_att_dst',
        'L1_gnn_bias', 'L1_gnn_gamma', 'L1_gnn_beta', 'L2_gnn_W', 'L2_gnn_a_src', 'L2_gnn_a_dst', 'L3_gnn_w_comp_k',
        'L3_gnn_w_basis_k', 'L3_gnn_w_comp_q', 'L3_gnn_w_basis_q', 'L3_gnn_w_comp_v', 'L3_gnn_w_basis_v',
        'L3_gnn_w_comp_a', 'L3_gnn_w_basis_a', 'L3_gnn_relation_pri', 'L3_gnn_relation_att', 'L3_gnn_relation_msg',
        'L3_gnn_loop_weight', 'L3_gnn_bias']


def kernel(**inputs):
    import concourse.bacc as bacc
    from concourse.bass_utils import run_bass_kernel_spmd

    nc = bacc.Bacc("TRN2", target_bir_lowering=False, num_devices=1)
    arrays = {f"in_{n}": np.ascontiguousarray(inputs[n]) for n in _INS}
    a = {n: nc.dram_tensor(f"in_{n}", arrays[f"in_{n}"].shape, mybir.dt.from_np(arrays[f"in_{n}"].dtype),
                                             kind="ExternalInput").ap() for n in _INS}
    out = nc.dram_tensor("out", (N_NODES, D), F32, kind="ExternalOutput").ap()
    build_program(nc, a, out)
    r = run_bass_kernel_spmd(nc, [arrays], core_ids=[0])
    return r.results[0]["out"]
```
